# Optimizing a Trainium2 kernel written in Bass

```python
import numpy as np
import jax
import jax.numpy as jnp

def _softmax(x, axis=-1):
    return jax.nn.softmax(x, axis=axis)

def _gelu(x):
    return jax.nn.gelu(x, approximate=True)

def _silu(x):
    return jax.nn.silu(x)

def _sigmoid(x):
    return jax.nn.sigmoid(x)

def _layernorm(x, axis=-1, eps=1e-05):
    m = jnp.mean(x, axis=axis, keepdims=True)
    v = jnp.var(x, axis=axis, keepdims=True)
    return (x - m) / jnp.sqrt(v + eps)

def _scatter_add(tgt, idx, src, axis=0):
    return tgt.at[idx].add(src)

def _segment_sum(src, seg, n):
    return jax.ops.segment_sum(src, seg, n)
kernel_name = 'mk_hybrid_d2_jaxref_r8_579c6a'

def setup_inputs(seed: int=0):
    np.random.seed(seed)
    _w = jnp.asarray

    def _L0_attn_a_setup():
        import jax, jax.numpy as jnp
        import numpy as np
        DT_RANK = 64
        D_STATE = 16
        key = jax.random.key(seed)
        ks = jax.random.split(key, 5)
        b, s, d = (2, 256, 128)
        u = jax.random.normal(ks[0], (b, s, d), dtype=jnp.float32)
        A_log = jnp.log(jnp.arange(1, D_STATE + 1, dtype=jnp.float32))
        x_proj_w = jax.random.normal(ks[1], (DT_RANK + 2 * D_STATE, d), dtype=jnp.float32) * (1.0 / np.sqrt(d))
        dt_proj_w = jax.random.normal(ks[2], (d, DT_RANK), dtype=jnp.float32) * (1.0 / np.sqrt(DT_RANK))
        dt_proj_b = jax.random.normal(ks[3], (d,), dtype=jnp.float32) * 0.01
        D = jnp.ones((d,), dtype=jnp.float32)
        return {'u': u, 'A_log': A_log, 'x_proj_w': x_proj_w, 'dt_proj_w': dt_proj_w, 'dt_proj_b': dt_proj_b, 'D': D}
    _L0_attn_a_in = _L0_attn_a_setup()

    def _L0_attn_b_setup():
        import jax, jax.numpy as jnp
        import numpy as np
        DIM = 128
        HEADS = 16
        DIM_HEAD = 64
        SCALE = 16.0
        EPS = 1e-05

        def layernorm(x, g):
            mean = jnp.mean(x, axis=-1, keepdims=True)
            var = jnp.var(x, axis=-1, keepdims=True)
            return (x - mean) * jax.lax.rsqrt(var + EPS) * g

        def l2norm(t):
            return t / jnp.maximum(jnp.linalg.norm(t, axis=-1, keepdims=True), 1e-12)
        key = jax.random.key(seed)
        ks = jax.random.split(key, 5)
        inner = HEADS * DIM_HEAD
        x = jax.random.normal(ks[0], (2, 256, DIM), dtype=jnp.float32)
        Wq = jax.random.normal(ks[1], (inner, DIM), dtype=jnp.float32) * 0.02
        Wkv = jax.random.normal(ks[2], (2 * DIM_HEAD, DIM), dtype=jnp.float32) * 0.02
        Wout = jax.random.normal(ks[3], (DIM, inner), dtype=jnp.float32) * 0.02
        g1 = jnp.ones((DIM,), dtype=jnp.float32)
        g2 = jnp.ones((DIM,), dtype=jnp.float32)
        return {'x': x, 'g1': g1, 'Wq': Wq, 'Wkv': Wkv, 'Wout': Wout, 'g2': g2}
    _L0_attn_b_in = _L0_attn_b_setup()

    def _L0_ffn_setup():
        import jax, jax.numpy as jnp
        import numpy as np
        INT4_QMAX = 7.0

        def simulate_quantize_int4(w):
            scale = jnp.max(jnp.abs(w)) / INT4_QMAX
            q = jnp.clip(jnp.round(w / scale), -8.0, 7.0)
            return q * scale
        key = jax.random.key(seed)
        k_x, k_w, k_bias, k_a, k_b = jax.random.split(key, 5)
        d_in, features, rank = (128, 128, 16)
        x = jax.random.normal(k_x, (4, 1024, d_in), dtype=jnp.float32)
        kernel = jax.random.normal(k_w, (d_in, features), dtype=jnp.float32)
        bias = jax.random.normal(k_bias, (features,), dtype=jnp.float32)
        a = jax.random.normal(k_a, (d_in, rank), dtype=jnp.float32) * (1.0 / np.sqrt(d_in))
        b = jax.random.normal(k_b, (rank, features), dtype=jnp.float32) * 0.01
        return {'x': x, 'kernel': kernel, 'bias': bias, 'a': a, 'b': b}
    _L0_ffn_in = _L0_ffn_setup()

    def _L1_attn_a_setup():
        import jax, jax.numpy as jnp
        import numpy as np
        B, S, D = (4, 256, 128)
        key = jax.random.key(seed)
        k1, k2, k3, k4 = jax.random.split(key, 4)
        x = jax.random.normal(k1, (B, S, D), dtype=jnp.float32)
        Qw = jax.random.normal(k2, (D, D), dtype=jnp.float32) / 40
        Kw = jax.random.normal(k3, (D, D), dtype=jnp.float32) / 40
        Vw = jax.random.normal(k4, (D, D), dtype=jnp.float32) / 40
        return {'x': x, 'Qw': Qw, 'Kw': Kw, 'Vw': Vw}
    _L1_attn_a_in = _L1_attn_a_setup()

    def _L1_attn_b_setup():
        import jax, jax.numpy as jnp
        import numpy as np
        D_MODEL = 128
        N_HEADS = 16
        D_HEAD = D_MODEL // N_HEADS

        def _rmsnorm(x, w):
            xf = x.astype(jnp.float32)
            rms = jnp.mean(xf * xf, axis=-1, keepdims=True)
            return (xf / jnp.sqrt(rms + 1e-06) * w.astype(jnp.float32)).astype(x.dtype)
        key = jax.random.key(seed)
        ks = jax.random.split(key, 7)
        x = jax.random.normal(ks[0], (1, 512, D_MODEL), dtype=jnp.float32)
        Wqkv = jax.random.normal(ks[1], (3 * D_MODEL, D_MODEL), dtype=jnp.float32) * (1.0 / np.sqrt(D_MODEL))
        bqkv = jax.random.normal(ks[2], (3 * D_MODEL,), dtype=jnp.float32) * 0.01
        Wo = jax.random.normal(ks[3], (D_MODEL, D_MODEL), dtype=jnp.float32) * (1.0 / np.sqrt(D_MODEL))
        bo = jax.random.normal(ks[4], (D_MODEL,), dtype=jnp.float32) * 0.01
        wq = jnp.ones((D_HEAD,), dtype=jnp.float32)
        wk = jnp.ones((D_HEAD,), dtype=jnp.float32)
        return {'x': x, 'Wqkv': Wqkv, 'bqkv': bqkv, 'Wo': Wo, 'bo': bo, 'wq': wq, 'wk': wk}
    _L1_attn_b_in = _L1_attn_b_setup()

    def _L1_ffn_setup():
        import jax, jax.numpy as jnp
        import numpy as np
        S_LEN, BATCH, HIDDEN = (256, 2, 128)
        N_HEADS, N_KV = (16, 8)
        N_EXP, TOP_K, CAP_F = (8, 2, 1.25)
        FFN = 512
        HEAD_DIM = HIDDEN // N_HEADS
        Q_PER_KV = N_HEADS // N_KV
        EPS = 1e-05
        NEG = -1000000000.0

        def _ln(x, w, b):
            mu = jnp.mean(x, -1, keepdims=True)
            var = jnp.var(x, -1, keepdims=True)
            return (x - mu) * jax.lax.rsqrt(var + EPS) * w + b

        def _forward(hidden_states, ln1_weight, ln1_bias, ln2_weight, ln2_bias, qkv_weight, proj_weight, router_weight, moe_w1, moe_w2):
            S, B, H = hidden_states.shape
            ln1 = _ln(hidden_states, ln1_weight, ln1_bias)
            qkv = (ln1 @ qkv_weight.T).reshape(S, B, N_KV, (Q_PER_KV + 2) * HEAD_DIM)
            q_dim = Q_PER_KV * HEAD_DIM
            q = qkv[..., :q_dim].reshape(S, B, N_HEADS, HEAD_DIM)
            k = jnp.repeat(qkv[..., q_dim:q_dim + HEAD_DIM], Q_PER_KV, axis=2)
            v = jnp.repeat(qkv[..., q_dim + HEAD_DIM:], Q_PER_KV, axis=2)
            scores = jnp.einsum('sbhd,tbhd->bhst', q, k) / jnp.sqrt(jnp.float32(HEAD_DIM))
            causal = jnp.tril(jnp.ones((S, S), bool))
            attn = jax.nn.softmax(jnp.where(causal[None, None], scores, NEG), axis=-1)
            attn_out = jnp.einsum('bhst,tbhd->sbhd', attn, v).reshape(S, B, H)
            hidden_after_attn = hidden_states + attn_out @ proj_weight.T
            x = _ln(hidden_after_attn, ln2_weight, ln2_bias).reshape(-1, H)
            N = S * B
            probs = jax.nn.softmax(x.astype(jnp.float32) @ router_weight, axis=-1)
            top_p, top_i = jax.lax.top_k(probs, TOP_K)
            top_p = top_p / jnp.sum(top_p, -1, keepdims=True)
            flat_exp = top_i.reshape(-1)
            order = jnp.argsort(flat_exp)
            sorted_exp = flat_exp[order]
            counts = jnp.bincount(sorted_exp, length=N_EXP)
            offsets = jnp.concatenate([jnp.zeros((1,), counts.dtype), jnp.cumsum(counts)])
            within = jnp.arange(N * TOP_K) - offsets[sorted_exp]
            cap = int(np.ceil(N * TOP_K / N_EXP * CAP_F))
            keep = within < cap
            slot = jnp.where(keep, sorted_exp * cap + within, N_EXP * cap)
            tok_id = order // TOP_K
            padded_tokens = jnp.zeros((N_EXP * cap + 1, H), x.dtype).at[slot].set(x[tok_id])[:-1]
            padded_probs = jnp.zeros((N_EXP * cap + 1,), jnp.float32).at[slot].set(top_p.reshape(-1)[order])[:-1]
            padded_ids = jnp.zeros((N_EXP * cap + 1,), jnp.int32).at[slot].set(tok_id.astype(jnp.int32))[:-1]
            exp_in = padded_tokens.reshape(N_EXP, cap, H)
            act = jax.nn.gelu(jnp.einsum('ech,ehf->ecf', exp_in, moe_w1), approximate=False)
            exp_out = jnp.einsum('ecf,efh->ech', act, moe_w2).reshape(N_EXP * cap, H)
            weighted = exp_out * padded_probs[:, None].astype(exp_out.dtype)
            moe = jnp.zeros((N, H), exp_out.dtype).at[padded_ids].add(weighted)
            return hidden_after_attn + moe.reshape(S, B, H)
        ks = jax.random.split(jax.random.key(seed), 6)
        qkv_out = N_KV * (Q_PER_KV + 2) * HEAD_DIM
        sc = 0.02
        return {'hidden_states': jax.random.normal(ks[0], (S_LEN, BATCH, HIDDEN), jnp.float32), 'ln1_weight': jnp.ones((HIDDEN,), jnp.float32), 'ln1_bias': jnp.zeros((HIDDEN,), jnp.float32), 'ln2_weight': jnp.ones((HIDDEN,), jnp.float32), 'ln2_bias': jnp.zeros((HIDDEN,), jnp.float32), 'qkv_weight': jax.random.normal(ks[1], (qkv_out, HIDDEN), jnp.float32) * sc, 'proj_weight': jax.random.normal(ks[2], (HIDDEN, HIDDEN), jnp.float32) * sc, 'router_weight': jax.random.normal(ks[3], (HIDDEN, N_EXP), jnp.float32) * sc, 'moe_w1': jax.random.normal(ks[4], (N_EXP, HIDDEN, FFN), jnp.float32) * sc, 'moe_w2': jax.random.normal(ks[5], (N_EXP, FFN, HIDDEN), jnp.float32) * sc}
    _L1_ffn_in = _L1_ffn_setup()
    _d = {'L0_attn_a_u': _L0_attn_a_in['u'], 'L0_attn_a_A_log': _L0_attn_a_in['A_log'], 'L0_attn_a_x_proj_w': _L0_attn_a_in['x_proj_w'], 'L0_attn_a_dt_proj_w': _L0_attn_a_in['dt_proj_w'], 'L0_attn_a_dt_proj_b': _L0_attn_a_in['dt_proj_b'], 'L0_attn_a_D': _L0_attn_a_in['D'], 'L0_attn_b_g1': _L0_attn_b_in['g1'], 'L0_attn_b_Wq': _L0_attn_b_in['Wq'], 'L0_attn_b_Wkv': _L0_attn_b_in['Wkv'], 'L0_attn_b_Wout': _L0_attn_b_in['Wout'], 'L0_attn_b_g2': _L0_attn_b_in['g2'], 'L0_ffn_kernel': _L0_ffn_in['kernel'], 'L0_ffn_bias': _L0_ffn_in['bias'], 'L0_ffn_a': _L0_ffn_in['a'], 'L0_ffn_b': _L0_ffn_in['b'], 'L1_attn_a_Qw': _L1_attn_a_in['Qw'], 'L1_attn_a_Kw': _L1_attn_a_in['Kw'], 'L1_attn_a_Vw': _L1_attn_a_in['Vw'], 'L1_attn_b_Wqkv': _L1_attn_b_in['Wqkv'], 'L1_attn_b_bqkv': _L1_attn_b_in['bqkv'], 'L1_attn_b_Wo': _L1_attn_b_in['Wo'], 'L1_attn_b_bo': _L1_attn_b_in['bo'], 'L1_attn_b_wq': _L1_attn_b_in['wq'], 'L1_attn_b_wk': _L1_attn_b_in['wk'], 'L1_ffn_ln1_weight': _L1_ffn_in['ln1_weight'], 'L1_ffn_ln1_bias': _L1_ffn_in['ln1_bias'], 'L1_ffn_ln2_weight': _L1_ffn_in['ln2_weight'], 'L1_ffn_ln2_bias': _L1_ffn_in['ln2_bias'], 'L1_ffn_qkv_weight': _L1_ffn_in['qkv_weight'], 'L1_ffn_proj_weight': _L1_ffn_in['proj_weight'], 'L1_ffn_router_weight': _L1_ffn_in['router_weight'], 'L1_ffn_moe_w1': _L1_ffn_in['moe_w1'], 'L1_ffn_moe_w2': _L1_ffn_in['moe_w2']}
    _x0 = _d['L0_attn_a_u']
    _d['L0_attn_a_u'] = jax.random.normal(jax.random.fold_in(jax.random.key(seed), 1), (4, 1024, 128), dtype=_x0.dtype)
    del _x0
    return _d

def reference(L0_attn_a_u, L0_attn_a_A_log, L0_attn_a_x_proj_w, L0_attn_a_dt_proj_w, L0_attn_a_dt_proj_b, L0_attn_a_D, L0_attn_b_g1, L0_attn_b_Wq, L0_attn_b_Wkv, L0_attn_b_Wout, L0_attn_b_g2, L0_ffn_kernel, L0_ffn_bias, L0_ffn_a, L0_ffn_b, L1_attn_a_Qw, L1_attn_a_Kw, L1_attn_a_Vw, L1_attn_b_Wqkv, L1_attn_b_bqkv, L1_attn_b_Wo, L1_attn_b_bo, L1_attn_b_wq, L1_attn_b_wk, L1_ffn_ln1_weight, L1_ffn_ln1_bias, L1_ffn_ln2_weight, L1_ffn_ln2_bias, L1_ffn_qkv_weight, L1_ffn_proj_weight, L1_ffn_router_weight, L1_ffn_moe_w1, L1_ffn_moe_w2):

    def _L0_attn_a_ref(u, A_log, x_proj_w, dt_proj_w, dt_proj_b, D):
        import jax, jax.numpy as jnp
        import numpy as np
        DT_RANK = 64
        D_STATE = 16
        batch, seq_len, d_model = u.shape
        xp = jnp.einsum('bsd,kd->bsk', u, x_proj_w)
        dt_raw = xp[..., :DT_RANK]
        B = xp[..., DT_RANK:DT_RANK + D_STATE]
        C = xp[..., DT_RANK + D_STATE:]
        delta = jax.nn.softplus(jnp.einsum('bsk,dk->bsd', dt_raw, dt_proj_w) + dt_proj_b)
        A = -jnp.exp(A_log)
        dA = jnp.exp(delta[..., None] * A)
        dB = delta[..., None] * B[:, :, None, :]

        def step(state, inputs):
            dA_t, dBu_t, C_t = inputs
            state = dA_t * state + dBu_t
            y_t = jnp.einsum('bdn,bn->bd', state, C_t)
            return (state, y_t)
        dBu = dB * u[..., None]
        xs = (jnp.swapaxes(dA, 0, 1), jnp.swapaxes(dBu, 0, 1), jnp.swapaxes(C, 0, 1))
        init = jnp.zeros((batch, d_model, D_STATE), dtype=u.dtype)
        _, ys = jax.lax.scan(step, init, xs)
        return jnp.swapaxes(ys, 0, 1) + u * D

    def _L0_attn_b_ref(x, g1, Wq, Wkv, Wout, g2):
        import jax, jax.numpy as jnp
        import numpy as np
        DIM = 128
        HEADS = 16
        DIM_HEAD = 64
        SCALE = 16.0
        EPS = 1e-05

        def layernorm(x, g):
            mean = jnp.mean(x, axis=-1, keepdims=True)
            var = jnp.var(x, axis=-1, keepdims=True)
            return (x - mean) * jax.lax.rsqrt(var + EPS) * g

        def l2norm(t):
            return t / jnp.maximum(jnp.linalg.norm(t, axis=-1, keepdims=True), 1e-12)
        b, n, _ = x.shape
        xn = layernorm(x, g1)
        q = xn @ Wq.T
        kv = xn @ Wkv.T
        k, v = (kv[..., :DIM_HEAD], kv[..., DIM_HEAD:])
        q = q.reshape(b, n, HEADS, DIM_HEAD).transpose(0, 2, 1, 3)
        q = q * SCALE
        q, k = (l2norm(q), l2norm(k))
        srt = np.sqrt(SCALE).astype(np.float32)
        q, k = (q * srt, k * srt)
        sim = jnp.einsum('bhid,bjd->bhij', q, k)
        max_neg = -jnp.finfo(sim.dtype).max
        causal_mask = jnp.triu(jnp.ones((n, n), dtype=bool), 1)
        sim = jnp.where(causal_mask, max_neg, sim)
        attn = jax.nn.softmax(sim.astype(jnp.float32), axis=-1).astype(sim.dtype)
        out = jnp.einsum('bhij,bjd->bhid', attn, v)
        out = out.transpose(0, 2, 1, 3).reshape(b, n, HEADS * DIM_HEAD)
        out = out @ Wout.T
        return layernorm(out, g2)

    def _L0_ffn_ref(x, kernel, bias, a, b):
        import jax, jax.numpy as jnp
        import numpy as np
        INT4_QMAX = 7.0

        def simulate_quantize_int4(w):
            scale = jnp.max(jnp.abs(w)) / INT4_QMAX
            q = jnp.clip(jnp.round(w / scale), -8.0, 7.0)
            return q * scale
        w = simulate_quantize_int4(kernel)
        y = jnp.einsum('bsd,df->bsf', x, w) + bias
        lora = jnp.einsum('bsr,rf->bsf', jnp.einsum('bsd,dr->bsr', x, a), b)
        return y + lora

    def _L1_attn_a_ref(x, Qw, Kw, Vw):
        import jax, jax.numpy as jnp
        import numpy as np
        B, S, D = (4, 256, 128)
        Q = x @ Qw
        K = x @ Kw
        V = x @ Vw
        d = x.shape[-1]
        S_len = x.shape[-2]
        mask = jnp.where(jnp.tril(jnp.ones((S_len, S_len), dtype=x.dtype)) == 0, -jnp.inf, 0.0).astype(x.dtype)
        scores = jnp.einsum('bqd,bkd->bqk', Q, K) / jnp.sqrt(jnp.asarray(d, x.dtype))
        scores = scores + mask
        attn = jax.nn.softmax(scores, axis=-1)
        return jnp.einsum('bqk,bkd->bqd', attn, V)

    def _L1_attn_b_ref(x, Wqkv, bqkv, Wo, bo, wq, wk):
        import jax, jax.numpy as jnp
        import numpy as np
        D_MODEL = 128
        N_HEADS = 16
        D_HEAD = D_MODEL // N_HEADS

        def _rmsnorm(x, w):
            xf = x.astype(jnp.float32)
            rms = jnp.mean(xf * xf, axis=-1, keepdims=True)
            return (xf / jnp.sqrt(rms + 1e-06) * w.astype(jnp.float32)).astype(x.dtype)
        b, s, d = x.shape
        qkv = x @ Wqkv.T + bqkv
        q, k, v = jnp.split(qkv, 3, axis=-1)
        q = q.reshape(b, s, N_HEADS, D_HEAD)
        k = k.reshape(b, s, N_HEADS, D_HEAD)
        v = v.reshape(b, s, N_HEADS, D_HEAD)
        q = _rmsnorm(q, wq)
        k = _rmsnorm(k, wk)
        qf = q.astype(jnp.float32)
        kf = k.astype(jnp.float32)
        vf = v.astype(jnp.float32)
        attn = jnp.einsum('bqhd,bkhd->bhqk', qf, kf)
        attn = jax.nn.softmax(attn, axis=-1)
        z = jnp.einsum('bhqk,bkhd->bqhd', attn, vf).astype(x.dtype)
        z = z.reshape(b, s, d)
        return z @ Wo.T + bo

    def _L1_ffn_ref(hidden_states, ln1_weight, ln1_bias, ln2_weight, ln2_bias, qkv_weight, proj_weight, router_weight, moe_w1, moe_w2):
        import jax, jax.numpy as jnp
        import numpy as np
        S_LEN, BATCH, HIDDEN = (256, 2, 128)
        N_HEADS, N_KV = (16, 8)
        N_EXP, TOP_K, CAP_F = (8, 2, 1.25)
        FFN = 512
        HEAD_DIM = HIDDEN // N_HEADS
        Q_PER_KV = N_HEADS // N_KV
        EPS = 1e-05
        NEG = -1000000000.0

        def _ln(x, w, b):
            mu = jnp.mean(x, -1, keepdims=True)
            var = jnp.var(x, -1, keepdims=True)
            return (x - mu) * jax.lax.rsqrt(var + EPS) * w + b

        def _forward(hidden_states, ln1_weight, ln1_bias, ln2_weight, ln2_bias, qkv_weight, proj_weight, router_weight, moe_w1, moe_w2):
            S, B, H = hidden_states.shape
            ln1 = _ln(hidden_states, ln1_weight, ln1_bias)
            qkv = (ln1 @ qkv_weight.T).reshape(S, B, N_KV, (Q_PER_KV + 2) * HEAD_DIM)
            q_dim = Q_PER_KV * HEAD_DIM
            q = qkv[..., :q_dim].reshape(S, B, N_HEADS, HEAD_DIM)
            k = jnp.repeat(qkv[..., q_dim:q_dim + HEAD_DIM], Q_PER_KV, axis=2)
            v = jnp.repeat(qkv[..., q_dim + HEAD_DIM:], Q_PER_KV, axis=2)
            scores = jnp.einsum('sbhd,tbhd->bhst', q, k) / jnp.sqrt(jnp.float32(HEAD_DIM))
            causal = jnp.tril(jnp.ones((S, S), bool))
            attn = jax.nn.softmax(jnp.where(causal[None, None], scores, NEG), axis=-1)
            attn_out = jnp.einsum('bhst,tbhd->sbhd', attn, v).reshape(S, B, H)
            hidden_after_attn = hidden_states + attn_out @ proj_weight.T
            x = _ln(hidden_after_attn, ln2_weight, ln2_bias).reshape(-1, H)
            N = S * B
            probs = jax.nn.softmax(x.astype(jnp.float32) @ router_weight, axis=-1)
            top_p, top_i = jax.lax.top_k(probs, TOP_K)
            top_p = top_p / jnp.sum(top_p, -1, keepdims=True)
            flat_exp = top_i.reshape(-1)
            order = jnp.argsort(flat_exp)
            sorted_exp = flat_exp[order]
            counts = jnp.bincount(sorted_exp, length=N_EXP)
            offsets = jnp.concatenate([jnp.zeros((1,), counts.dtype), jnp.cumsum(counts)])
            within = jnp.arange(N * TOP_K) - offsets[sorted_exp]
            cap = int(np.ceil(N * TOP_K / N_EXP * CAP_F))
            keep = within < cap
            slot = jnp.where(keep, sorted_exp * cap + within, N_EXP * cap)
            tok_id = order // TOP_K
            padded_tokens = jnp.zeros((N_EXP * cap + 1, H), x.dtype).at[slot].set(x[tok_id])[:-1]
            padded_probs = jnp.zeros((N_EXP * cap + 1,), jnp.float32).at[slot].set(top_p.reshape(-1)[order])[:-1]
            padded_ids = jnp.zeros((N_EXP * cap + 1,), jnp.int32).at[slot].set(tok_id.astype(jnp.int32))[:-1]
            exp_in = padded_tokens.reshape(N_EXP, cap, H)
            act = jax.nn.gelu(jnp.einsum('ech,ehf->ecf', exp_in, moe_w1), approximate=False)
            exp_out = jnp.einsum('ecf,efh->ech', act, moe_w2).reshape(N_EXP * cap, H)
            weighted = exp_out * padded_probs[:, None].astype(exp_out.dtype)
            moe = jnp.zeros((N, H), exp_out.dtype).at[padded_ids].add(weighted)
            return hidden_after_attn + moe.reshape(S, B, H)
        return _forward(hidden_states, ln1_weight, ln1_bias, ln2_weight, ln2_bias, qkv_weight, proj_weight, router_weight, moe_w1, moe_w2)
    x = L0_attn_a_u
    x = x + _L0_attn_a_ref(_layernorm(x, axis=-1), L0_attn_a_A_log, L0_attn_a_x_proj_w, L0_attn_a_dt_proj_w, L0_attn_a_dt_proj_b, L0_attn_a_D)
    x = x + _L0_ffn_ref(_layernorm(x, axis=-1), L0_ffn_kernel, L0_ffn_bias, L0_ffn_a, L0_ffn_b)
    x = x + _L0_attn_b_ref(_layernorm(x, axis=-1), L0_attn_b_g1, L0_attn_b_Wq, L0_attn_b_Wkv, L0_attn_b_Wout, L0_attn_b_g2)
    x = x + _L0_ffn_ref(_layernorm(x, axis=-1), L0_ffn_kernel, L0_ffn_bias, L0_ffn_a, L0_ffn_b)
    x = x + _L1_attn_a_ref(_layernorm(x, axis=-1), L1_attn_a_Qw, L1_attn_a_Kw, L1_attn_a_Vw)
    x = x + _L1_ffn_ref(_layernorm(x, axis=-1), L1_ffn_ln1_weight, L1_ffn_ln1_bias, L1_ffn_ln2_weight, L1_ffn_ln2_bias, L1_ffn_qkv_weight, L1_ffn_proj_weight, L1_ffn_router_weight, L1_ffn_moe_w1, L1_ffn_moe_w2)
    x = x + _L1_attn_b_ref(_layernorm(x, axis=-1), L1_attn_b_Wqkv, L1_attn_b_bqkv, L1_attn_b_Wo, L1_attn_b_bo, L1_attn_b_wq, L1_attn_b_wk)
    x = x + _L1_ffn_ref(_layernorm(x, axis=-1), L1_ffn_ln1_weight, L1_ffn_ln1_bias, L1_ffn_ln2_weight, L1_ffn_ln2_bias, L1_ffn_qkv_weight, L1_ffn_proj_weight, L1_ffn_router_weight, L1_ffn_moe_w1, L1_ffn_moe_w2)
    return x

_drawn_inputs = setup_inputs


def setup_inputs(seed=0):
    import zlib

    import numpy as np

    out = dict(_drawn_inputs(seed))
    spreads = {'L0_attn_a_D': (1.0, 0.2),
     'L0_attn_b_g1': (1.0, 0.547),
     'L0_attn_b_g2': (1.0, 0.6),
     'L1_attn_b_wq': (1.0, 0.6),
     'L1_attn_b_wk': (1.0, 0.6),
     'L1_ffn_ln1_weight': (1.0, 0.6),
     'L1_ffn_ln1_bias': (0.0, 0.8),
     'L1_ffn_ln2_weight': (1.0, 0.6),
     'L1_ffn_ln2_bias': (0.0, 0.8)}
    factors = {'L0_attn_a_dt_proj_b': 8.0,
     'L0_ffn_a': 8.0,
     'L0_ffn_b': 8.0,
     'L1_attn_a_Qw': 8.0,
     'L1_attn_a_Kw': 8.0,
     'L1_attn_a_Vw': 8.0,
     'L1_attn_b_Wqkv': 3.798,
     'L1_attn_b_bqkv': 8.0,
     'L1_attn_b_Wo': 3.66,
     'L1_attn_b_bo': 55.939,
     'L1_ffn_qkv_weight': 8.0,
     'L1_ffn_proj_weight': 8.0,
     'L1_ffn_router_weight': 8.0,
     'L1_ffn_moe_w1': 8.0,
     'L1_ffn_moe_w2': 8.0}
    for name, (base, spread) in spreads.items():
        noise = np.random.default_rng([zlib.crc32(name.encode()), seed]).standard_normal(out[name].shape)
        drawn = base * np.exp(spread * noise) if base else spread * noise
        out[name] = jnp.asarray(drawn.astype(out[name].dtype))
    for name, factor in factors.items():
        out[name] = (out[name] * factor).astype(out[name].dtype)
    return out
```

```python
from contextlib import ExitStack

import numpy as np

import concourse.bass as bass
from concourse import mybir

F32 = mybir.dt.float32
BF16 = mybir.dt.bfloat16
I32 = mybir.dt.int32
U32 = mybir.dt.uint32
ALU = mybir.AluOpType
ACT = mybir.ActivationFunctionType
AX = mybir.AxisListType
RMAX = bass.bass_isa.ReduceOp.max

P = 128
D = 128
BATCH, SEQ = 4, 1024
TOKENS = BATCH * SEQ
TILES = TOKENS // P
BTILES = SEQ // P
GT = 4
GROUPS = TILES // GT
EPS = 1e-5


class Chain:

    def __init__(self, eng, sem, base=0):
        self.eng, self.sem, self.base, self.n = eng, sem, base, 0

    def __call__(self, ins):
        ins.then_inc(self.sem, 1)
        self.n += 1
        self.eng.wait_ge(self.sem, self.base + self.n)


def steps(eng, n, unroll, peel, body):
    rounds = (n - peel) // unroll
    with eng.Fori(0, rounds) as i:
        for u in range(unroll):
            body(i * unroll + u, u, False)
    for g in range(rounds * unroll, n):
        body(g, g % unroll, g == n - 1)


def newton_rsqrt(eng, step, y, v, t):
    step(eng.tensor_scalar(y.bitcast(I32), v.bitcast(I32), -0.5, 1597463007.0, ALU.mult, ALU.add))
    for _ in range(4):
        step(eng.scalar_tensor_tensor(out=t, in0=y, scalar=-0.5, in1=y, op0=ALU.mult, op1=ALU.mult))
        step(eng.tensor_tensor(t, t, v, ALU.mult))
        step(eng.scalar_tensor_tensor(out=y, in0=t, scalar=1.5, in1=y, op0=ALU.add, op1=ALU.mult))


class Core:

    def __init__(self, nc, ctx):
        self.nc, self.ctx, self.sems = nc, ctx, []
        self.X = self.sb("X", [P, TILES, D])
        self.ident = self.sb("ident", [P, P])
        self.identb = self.sb("identb", [P, P], BF16)
        self.rstd = self.sb("rstd", [P, TILES])
        self.shift = self.sb("shift", [P, TILES])
        self.rstd2 = self.sb("rstd2", [P, TILES])
        self.shift2 = self.sb("shift2", [P, TILES])
        self.stats = self.sb("stats", [P, TILES, 6])
        self.tmp = self.sb("tmp", [P, 3, TILES])

    def sb(self, name, shape, dt=F32, ctx=None):
        return (ctx or self.ctx).enter_context(self.nc.sbuf_tensor(name, shape, dt))

    def ps(self, name, shape, dt=F32, ctx=None):
        return (ctx or self.ctx).enter_context(self.nc.psum_tensor(name, shape, dt))

    def sem(self, name):
        self.sems.append(self.nc.alloc_semaphore(name=name))
        return self.sems[-1]

    def end_stage(self):
        self.nc.clear_and_free_semaphores(self.sems)
        self.nc.all_engine_barrier()
        self.sems = []


def load_stream(core, x):
    nc = core.nc
    loaded, made = core.sem("x_loaded"), core.sem("ident_made")
    with nc.Block() as block:
        @block.sync
        def _(sp):
            sp.dma_start(core.X[:], x.rearrange("(t p) d -> p t d", p=P)).then_inc(loaded, 16)
            sp.wait_ge(loaded, 16)

        @block.gpsimd
        def _(pool):
            pool.memset(core.ident[:], 0.0).then_inc(made, 1)
            pool.wait_ge(made, 1)
            pool.affine_select(out=core.ident[:], in_=core.ident[:], compare_op=ALU.not_equal, fill=1.0, base=0,
                               pattern=[[-1, P]], channel_multiplier=1).then_inc(made, 1)
            pool.wait_ge(made, 2)
            pool.tensor_copy(core.identb[:], core.ident[:]).then_inc(made, 1)


def store_stream(core, out):
    stored = core.sem("out_stored")
    with core.nc.Block() as block:
        @block.sync
        def _(sp):
            sp.dma_start(out.rearrange("(t p) d -> p t d", p=P), core.X[:]).then_inc(stored, 16)
            sp.wait_ge(stored, 16)


def moments(dve, step, stats, n, mean, var, t, eps):
    me, m2e, mo, m2o = (stats[:, :, k] for k in (1, 2, 4, 5))
    step(dve.tensor_tensor(t, me, mo, ALU.subtract))
    dve.tensor_tensor(mean, me, mo, ALU.add)
    step(dve.tensor_tensor(var, m2e, m2o, ALU.add))
    step(dve.scalar_tensor_tensor(out=t, in0=t, scalar=n / 4.0, in1=t, op0=ALU.mult, op1=ALU.mult))
    step(dve.tensor_tensor(var, var, t, ALU.add))
    dve.tensor_scalar(mean, mean, 0.5, None, ALU.mult)
    step(dve.tensor_scalar(var, var, 1.0 / n, eps, ALU.mult, ALU.add))


def second_norm(dve, step, core, var, t):
    r2 = core.rstd2[:]
    step(dve.tensor_scalar(var, var, EPS, None, ALU.subtract))
    step(dve.tensor_tensor(var, var, core.rstd[:], ALU.mult))
    step(dve.tensor_tensor(var, var, core.rstd[:], ALU.mult))
    step(dve.tensor_scalar(var, var, EPS, None, ALU.add))
    newton_rsqrt(dve, step, r2, var, t)
    step(dve.tensor_tensor(r2, r2, core.rstd[:], ALU.mult))


def stream_stats(core, name, src=None, twice=False):
    src = core.X if src is None else src
    chain = core.sem(f"{name}_stats_chain")
    mean, var, t = (core.tmp[:, k, :] for k in range(3))
    with core.nc.Block() as block:
        @block.vector
        def _(dve):
            with dve.Fori(0, TILES // GT) as i:
                for u in range(GT):
                    dve.bn_stats(core.stats[:, bass.ds(i * GT + u, 1), :], src[:, bass.ds(i * GT + u, 1), :])
            step = Chain(dve, chain)
            step(dve.memset(t, 0.0))
            moments(dve, step, core.stats, D, mean, var, t, EPS)
            newton_rsqrt(dve, step, core.rstd[:], var, t)
            if twice:
                step(dve.scalar_tensor_tensor(out=core.shift[:], in0=mean, scalar=-1.0, in1=core.rstd[:],
                                              op0=ALU.mult, op1=ALU.mult))
                second_norm(dve, step, core, var, t)
            scale = core.rstd2 if twice else core.rstd
            out = core.shift2 if twice else core.shift
            step(dve.scalar_tensor_tensor(out=out[:], in0=mean, scalar=-1.0, in1=scale[:], op0=ALU.mult, op1=ALU.mult))


def normalise(dve, core, out, g, last_inc=None):
    for j in range(GT):
        k = bass.ds(g * GT + j, 1)
        ins = dve.tensor_scalar(out[:, j, :], core.X[:, k, :], core.rstd[:, k], core.shift[:, k], ALU.mult, ALU.add)
    return ins


def ffn(core, name, w, bias, a_t, b):
    nc = core.nc
    with ExitStack() as ctx:
        sb = lambda n, s, dt=F32: core.sb(f"{name}_{n}", s, dt, ctx)
        ps = lambda n, s: core.ps(f"{name}_{n}", s, F32, ctx)
        sem = lambda n: core.sem(f"{name}_{n}")
        W, aT, B = sb("W", [D, D]), sb("aT", [16, D]), sb("B", [16, D])
        bias4, ones = sb("bias4", [1, GT, D]), sb("ones", [1, P])
        amax, top, scale, inv = sb("amax", [P, 1]), sb("top", [P, 1]), sb("scale", [P, 1]), sb("inv", [P, 1])
        q = sb("q", [D, D])
        weff = sb("weff", [D, D])
        nrm, uT = sb("nrm", [P, 2, GT, D]), sb("uT", [P, 2, GT * P])
        pT, pY = ps("pT", [P, 2, GT * P]), ps("pY", [P, 2, GT * P])
        pW = ps("pW", [P, D])
        loaded, chain, absmax, allmax, ones_made, ab_made, weff_made = map(
            sem, ("loaded", "chain", "absmax", "allmax", "ones_made", "ab_made", "weff_made"))
        normed, turned, copied, product, added = map(sem, ("normed", "turned", "copied", "product", "added"))
        flat = core.X[:].rearrange("p t d -> p (t d)")
        with nc.Block() as block:
            @block.sync
            def _(sp):
                sp.dma_start(W[:], w).then_inc(loaded, 16)
                sp.dma_start(aT[:], a_t).then_inc(loaded, 16)
                sp.dma_start(B[:], b).then_inc(loaded, 16)
                for j in range(GT):
                    sp.dma_start(bias4[:, j, :], bias.rearrange("(o n) -> o n", o=1)).then_inc(loaded, 16)

            @block.gpsimd
            def _(pool):
                pool.memset(ones[:], 1.0).then_inc(ones_made, 1)
                pool.wait_ge(absmax, 1)
                pool.partition_all_reduce(top[:], amax[:], P, RMAX).then_inc(allmax, 1)

            @block.vector
            def _(dve):
                dve.sem_inc(added, 2)
                step = Chain(dve, chain)
                dve.wait_ge(loaded, 16 * 7)
                dve.tensor_reduce(amax[:], W[:], AX.X, ALU.max, apply_absolute_value=True).then_inc(absmax, 1)
                dve.wait_ge(allmax, 1)
                step(dve.reciprocal(inv[:], top[:]))
                step(dve.tensor_scalar(scale[:], top[:], 1.0 / 7.0, None, ALU.mult))
                step(dve.reciprocal(inv[:], scale[:]))
                step(dve.tensor_scalar(q[:], W[:], inv[:, 0:1], 12582912.0, ALU.mult, ALU.add))
                step(dve.tensor_scalar(q[:], q[:], 12582912.0, -8.0, ALU.subtract, ALU.max))
                step(dve.tensor_scalar(q[:], q[:], 7.0, scale[:, 0:1], ALU.min, ALU.mult))
                dve.wait_ge(ab_made, 1)
                dve.tensor_tensor(weff[:], q[:], pW[:], ALU.add).then_inc(weff_made, 1)

                def norm(g, u):
                    dve.wait_ge(turned, g + 1)
                    normalise(dve, core, nrm[:, u], g).then_inc(normed, 1)

                norm(0, 0)

                def body(g, u, last):
                    if not last:
                        norm(g + 1, 1 - u)
                    dve.wait_ge(product, g + 3)
                    cols = bass.ds(g * GT * D, GT * D)
                    dve.tensor_tensor(flat[:, cols], flat[:, cols], pY[:, u, :], ALU.add).then_inc(added, 1)
                steps(dve, GROUPS, 2, 2, body)

            @block.tensor
            def _(pe):
                pe.sem_inc(turned, 2)
                pe.sem_inc(product, 2)
                pe.wait_ge(loaded, 16 * 7)
                pe.matmul(pW[:], aT[:], B[:], start=True, stop=True).then_inc(ab_made, 1)
                pe.wait_ge(ones_made, 1)
                pe.wait_ge(weff_made, 1)

                def turn(g, u):
                    pe.wait_ge(normed, g + 1)
                    pe.wait_ge(copied, g + 1)
                    for j in range(GT):
                        ins = pe.transpose(pT[:, u, bass.ts(j, P)], nrm[:, u, j, :], core.ident[:])
                    ins.then_inc(turned, 1)

                turn(0, 0)

                def body(g, u, last):
                    if not last:
                        turn(g + 1, 1 - u)
                    pe.wait_ge(copied, g + 3)
                    pe.wait_ge(added, g + 1)
                    pe.matmul(pY[:, u, :], ones[:], bias4[:], start=True, stop=False, skip_group_check=True)
                    for j in range(GT):
                        ins = pe.matmul(pY[:, u, bass.ts(j, P)], uT[:, u, bass.ts(j, P)], weff[:],
                                        start=False, stop=(j == GT - 1), skip_group_check=True)
                    ins.then_inc(product, 1)
                steps(pe, GROUPS, 2, 2, body)

            @block.scalar
            def _(act):
                act.sem_inc(copied, 2)

                def body(g, u, last):
                    act.wait_ge(turned, g + 3)
                    act.wait_ge(product, g + 1)
                    act.activation(uT[:, u, :], pT[:, u, :], ACT.Copy).then_inc(copied, 1)
                steps(act, GROUPS, 2, 0, body)


def scan_block(core, name, wbc, wdt, dtw, dtb, a_log, dvec):
    nc = core.nc
    NS = 16
    with ExitStack() as ctx:
        sb = lambda n, s, dt=F32: core.sb(f"{name}_{n}", s, dt, ctx)
        ps = lambda n, s: core.ps(f"{name}_{n}", s, F32, ctx)
        sem = lambda n: core.sem(f"{name}_{n}")
        Wbc, Wdt, Wz = sb("Wbc", [D, 96]), sb("Wdt", [D, 64]), sb("Wz", [64, D])
        zbias, dcol, A = sb("zbias", [P, 1]), sb("dcol", [P, 1]), sb("A", [P, NS])
        diagD = sb("diagD", [P, P])
        sel = sb("sel", [96, 2 * NS, P], BF16)
        nrm = sb("nrm", [P, BTILES, D])
        uT, dtT, zc, zabs, zexp, zpos = (sb(n, [P, SEQ]) for n in ("uT", "dtT", "zc", "zabs", "zexp", "zpos"))
        delta, du, yT = (sb(n, [P, SEQ]) for n in ("delta", "du", "yT"))
        hi, mid, rest, rest2 = sb("hi", [96, SEQ], BF16), sb("mid", [96, SEQ], BF16), sb("rest", [96, SEQ]), sb("rest2", [96, SEQ])
        bc3 = sb("bc3", [96, SEQ], BF16)
        dA, Bs, dBu, state, yc = (sb(n, [P, 2, SEQ]) for n in ("dA", "Bs", "dBu", "state", "yc"))
        pM, pB, pC, pY = (ps(n, [P, SEQ]) for n in ("pM", "pB", "pC", "pY"))
        names = ("loaded chain a_made sel_made diag_made normed turned u_copied bc_made hi_made rest_made split_made "
                 "dt_made dt_copied z_made z_copied act_chain log_made pos_made delta_made du_made "
                 "b_made b_copied c_made multiplied da_made scanned weighted summed y_copied y_turned added").split()
        s = dict(zip(names, map(sem, names)))
        flat = core.X[:].rearrange("p t d -> p (t d)")
        H = SEQ // 2
        with nc.Block() as block:
            @block.sync
            def _(sp):
                sp.dma_start(Wbc[:], wbc).then_inc(s["loaded"], 16)
                sp.dma_start(Wdt[:], wdt).then_inc(s["loaded"], 16)
                sp.dma_start(Wz[:], dtw).then_inc(s["loaded"], 16)
                sp.dma_start(zbias[:], dtb.rearrange("(d o) -> d o", o=1)).then_inc(s["loaded"], 16)
                sp.dma_start(dcol[:], dvec.rearrange("(d o) -> d o", o=1)).then_inc(s["loaded"], 16)
                sp.dma_start(A[:], a_log.rearrange("(o n) -> o n", o=1).to_broadcast([P, NS])).then_inc(s["loaded"], 16)

            @block.gpsimd
            def _(pool):
                pool.memset(sel[:], 0.0).then_inc(s["sel_made"], 1)
                for k in range(3):
                    pool.wait_ge(s["sel_made"], k + 1)
                    pool.affine_select(out=sel[:], in_=sel[:], compare_op=ALU.not_equal, fill=1.0, base=-32 * k,
                                       pattern=[[-1, 2 * NS], [0, P]], channel_multiplier=1).then_inc(s["sel_made"], 1)
                pool.sem_inc(s["multiplied"], 2)
                with pool.Fori(0, BATCH) as b:
                    def body(n, u, last):
                        it = b * NS + n
                        pool.wait_ge(s["du_made"], b + 1)
                        pool.wait_ge(s["b_copied"], it + 2)
                        pool.wait_ge(s["scanned"], it + 1)
                        pool.tensor_tensor(dBu[:, u, :], Bs[:, u, :], du[:], ALU.mult).then_inc(s["multiplied"], 1)
                    steps(pool, NS, 2, 0, body)

            @block.vector
            def _(dve):
                dve.sem_inc(s["scanned"], 2)
                dve.sem_inc(s["weighted"], 1)
                dve.sem_inc(s["added"], 1)
                dve.wait_ge(s["loaded"], 16 * 6)
                dve.tensor_scalar(diagD[:], core.ident[:], dcol[:, 0:1], None, ALU.mult).then_inc(s["diag_made"], 1)
                with dve.Fori(0, BATCH) as b:
                    step = Chain(dve, s["chain"], b * 3)
                    for k in range(BTILES):
                        t = bass.ds(b * BTILES + k, 1)
                        ins = dve.tensor_scalar(nrm[:, k, :], core.X[:, t, :], core.rstd[:, t], core.shift[:, t],
                                                ALU.mult, ALU.add)
                    ins.then_inc(s["normed"], 1)
                    dve.wait_ge(s["hi_made"], b + 1)
                    dve.tensor_tensor(rest[:], pM[0:96, :], hi[:], ALU.subtract).then_inc(s["rest_made"], 1)
                    dve.wait_ge(s["rest_made"], b + 1)
                    step(dve.tensor_copy(mid[:], rest[:]))
                    step(dve.tensor_tensor(rest2[:], rest[:], mid[:], ALU.subtract))
                    dve.tensor_copy(bc3[0:32, :], hi[0:32, :])
                    dve.tensor_copy(bc3[32:64, :], mid[32:64, :])
                    dve.tensor_copy(bc3[64:96, :], rest2[64:96, :]).then_inc(s["split_made"], 1)
                    dve.wait_ge(s["z_copied"], b + 1)
                    step(dve.tensor_scalar(zpos[:], zc[:], 0.0, None, ALU.max))
                    dve.wait_ge(s["log_made"], b + 1)
                    dve.tensor_tensor(delta[:], zpos[:], zexp[:], ALU.add).then_inc(s["delta_made"], 1)
                    dve.wait_ge(s["delta_made"], b + 1)
                    dve.tensor_tensor(du[:], delta[:], uT[:], ALU.mult).then_inc(s["du_made"], 1)

                    def body(n, u, last):
                        it = b * NS + n
                        dve.wait_ge(s["da_made"], it + 1)
                        dve.wait_ge(s["multiplied"], it + 3)
                        dve.tensor_tensor_scan(state[:, u, :], dA[:, u, :], dBu[:, u, :], 0.0, ALU.mult,
                                               ALU.add).then_inc(s["scanned"], 1)
                        dve.wait_ge(s["scanned"], it + 3)
                        dve.wait_ge(s["c_made"], it + 1)
                        dve.wait_ge(s["summed"], it + 1)
                        dve.tensor_tensor(yc[:, u, :], state[:, u, :], pC[:], ALU.mult).then_inc(s["weighted"], 1)
                    steps(dve, NS, 2, 0, body)
                    dve.wait_ge(s["y_turned"], b + 1)
                    cols = bass.ds(b * SEQ, SEQ)
                    dve.tensor_tensor(flat[:, cols], flat[:, cols], pM[:], ALU.add).then_inc(s["added"], 1)

            @block.scalar
            def _(act):
                act.wait_ge(s["loaded"], 16 * 6)
                act.activation(A[:], A[:], ACT.Exp).then_inc(s["a_made"], 1)
                act.wait_ge(s["a_made"], 1)
                act.activation(A[:], A[:], ACT.Copy, scale=-1.0).then_inc(s["a_made"], 1)
                act.wait_ge(s["a_made"], 2)
                act.sem_inc(s["b_copied"], 1)
                with act.Fori(0, BATCH) as b:
                    step = Chain(act, s["act_chain"], b * 2)
                    act.wait_ge(s["turned"], b + 1)
                    act.activation(uT[:], pM[:], ACT.Copy).then_inc(s["u_copied"], 1)
                    act.wait_ge(s["bc_made"], b + 1)
                    act.activation(hi[:], pM[0:96, :], ACT.Copy).then_inc(s["hi_made"], 1)
                    act.wait_ge(s["dt_made"], b + 1)
                    act.activation(dtT[0:64, :], pM[0:64, :], ACT.Copy).then_inc(s["dt_copied"], 1)
                    act.wait_ge(s["z_made"], b + 1)
                    act.activation(zc[:], pM[:], ACT.Identity, bias=zbias[:, 0:1]).then_inc(s["z_copied"], 1)
                    act.wait_ge(s["z_copied"], b + 1)
                    step(act.activation(zabs[:], zc[:], ACT.Abs))
                    step(act.activation(zexp[:], zabs[:], ACT.Exp, scale=-1.0))
                    act.activation(zexp[:], zexp[:], ACT.Ln, bias=1.0).then_inc(s["log_made"], 1)
                    act.wait_ge(s["delta_made"], b + 1)

                    def body(n, u, last):
                        it = b * NS + n
                        act.wait_ge(s["b_made"], it + 1)
                        act.wait_ge(s["multiplied"], it + 1)
                        act.activation(Bs[:, u, :], pB[:], ACT.Copy).then_inc(s["b_copied"], 1)
                        act.wait_ge(s["scanned"], it + 1)
                        act.activation(dA[:, u, :], delta[:], ACT.Exp, scale=A[:, bass.ds(n, 1)]).then_inc(s["da_made"], 1)
                    steps(act, NS, 2, 0, body)
                    act.wait_ge(s["summed"], b * NS + NS + 2)
                    act.activation(yT[:], pY[:], ACT.Copy).then_inc(s["y_copied"], 1)

            @block.tensor
            def _(pe):
                halves = (slice(0, H), slice(H, SEQ))
                pe.sem_inc(s["summed"], 2)
                pe.wait_ge(s["loaded"], 16 * 6)
                pe.wait_ge(s["sel_made"], 4)
                pe.wait_ge(s["diag_made"], 1)
                with pe.Fori(0, BATCH) as b:
                    pe.wait_ge(s["normed"], b + 1)
                    pe.wait_ge(s["added"], b + 1)
                    for k in range(BTILES):
                        ins = pe.transpose(pM[:, bass.ts(k, P)], nrm[:, k, :], core.ident[:])
                    ins.then_inc(s["turned"], 1)
                    pe.wait_ge(s["u_copied"], b + 1)
                    for h in halves:
                        ins = pe.matmul(pM[0:96, h], Wbc[:], uT[:, h], start=True, stop=True)
                    ins.then_inc(s["bc_made"], 1)
                    for h in halves:
                        pe.matmul(pY[:, h], diagD[:], uT[:, h], start=True, stop=False, skip_group_check=True)
                    pe.wait_ge(s["rest_made"], b + 1)
                    for h in halves:
                        ins = pe.matmul(pM[0:64, h], Wdt[:], uT[:, h], start=True, stop=True)
                    ins.then_inc(s["dt_made"], 1)
                    pe.wait_ge(s["dt_copied"], b + 1)
                    for h in halves:
                        ins = pe.matmul(pM[:, h], Wz[:], dtT[0:64, h], start=True, stop=True)
                    ins.then_inc(s["z_made"], 1)
                    pe.wait_ge(s["split_made"], b + 1)

                    def spread_b(n):
                        pe.wait_ge(s["b_copied"], b * NS + n + 1)
                        for h in halves:
                            ins = pe.matmul(pB[:, h], sel[:, bass.ds(n, 1), :], bc3[:, h], start=True, stop=True)
                        ins.then_inc(s["b_made"], 1)

                    def spread_c(n):
                        pe.wait_ge(s["weighted"], b * NS + n + 1)
                        for h in halves:
                            ins = pe.matmul(pC[:, h], sel[:, bass.ds(n + NS, 1), :], bc3[:, h], start=True, stop=True)
                        ins.then_inc(s["c_made"], 1)

                    spread_b(0)
                    spread_c(0)

                    def body(n, u, last):
                        if not last:
                            spread_b(n + 1)
                            spread_c(n + 1)
                        pe.wait_ge(s["weighted"], b * NS + n + 2)
                        for h in halves:
                            ins = pe.matmul(pY[:, h], core.ident[:], yc[:, u, h], start=False, stop=last,
                                            skip_group_check=True)
                        ins.then_inc(s["summed"], 1)
                    steps(pe, NS, 2, 2, body)
                    pe.wait_ge(s["y_copied"], b + 1)
                    pe.wait_ge(s["log_made"], b + 1)
                    for k in range(BTILES):
                        ins = pe.transpose(pM[:, bass.ts(k, P)], yT[:, bass.ts(k, P)], core.ident[:])
                    ins.then_inc(s["y_turned"], 1)


def causal_mqa(core, name, g1, wq_t, wkv_t, wout_t, g2, qt_steps=None):
    nc = core.nc
    NH, DH = 16, 64
    NQ = BTILES
    HALVES = NQ * (NQ + 1)
    HB = NH // 2
    PXB = 4 * NQ + 3 * NQ
    RING = 4
    OB = ((0, 7), (7, 14), (14, 16))
    with ExitStack() as ctx:
        sb = lambda n, s, dt=F32: core.sb(f"{name}_{n}", s, dt, ctx)
        ps = lambda n, s: core.ps(f"{name}_{n}", s, F32, ctx)
        sem = lambda n: core.sem(f"{name}_{n}")
        Wq, Wkv, Wout = sb("Wq", [D, NH * DH]), sb("Wkv", [D, 2 * DH]), sb("Wout", [P, 8, D])
        gcol, g2row = sb("gcol", [P, 1]), sb("g2row", [P, D])
        mask = sb("mask", [P, P])
        nrm, uT = sb("nrm", [P, BTILES, D]), sb("uT", [P, SEQ])
        kv, V1 = sb("kv", [P, BTILES, 2 * DH]), sb("V1", [P, BTILES, DH + 1])
        ksq, kss, krs, kt_ = sb("ksq", [P, BTILES, DH]), sb("kss", [P, BTILES]), sb("krs", [P, BTILES]), sb("kt_", [P, BTILES])
        kk, kT = sb("kk", [P, BTILES, 2, DH]), sb("kT", [P, SEQ])
        qraw, qsq, qn = (sb(n, [P, NH, DH]) for n in ("qraw", "qsq", "qn"))
        qss, qrs, qtmp = (sb(n, [P, NH]) for n in ("qss", "qrs", "qtmp"))
        qT = sb("qT", [P, 2, 8, P])
        pT = sb("pT", [P, RING, 2, 4, P])
        osum, on, oT = sb("osum", [P, NH]), sb("on", [P, NH, DH]), sb("oT", [P, 8, P])
        OUT = sb("OUT", [P, TILES, D])
        pS = ps("pS", [P, 2, 2, 512])
        pO = ps("pO", [P, 3, 512])
        pX = ps("pX", [P, 512])
        names = ("loaded folded mask_made ones_made normed turned u_copied kv_made kk_made k_turned k_copied "
                 "s_made exped masked pv_done o_used px_made px_used squared q_scaled q_rs on_made chain").split()
        s = dict(zip(names, map(sem, names)))

        def side_steps(qt):
            out = ["E", "F", "G"] if qt > 0 else []
            return ["Q0", "Q1"] + out + ["T0", "T1"] if qt < NQ - 1 else out

        q_copied, px = {}, 0
        order = [("Q0", 0), ("Q1", 0), ("T0", 0), ("T1", 0)]
        for qt in range(NQ):
            order += [(k, qt + 1 if k[0] in "QT" else qt - 1) for k in side_steps(qt)]
        order += [("E", NQ - 1), ("F", NQ - 1), ("G", NQ - 1)]
        assert len(order) == PXB
        at = {key: n for n, key in enumerate(order)}
        for qt in range(NQ):
            q_copied[qt] = at[("Q1", qt)] + 2

        def sides(qt):
            return [(k, qt + 1 if k[0] in "QT" else qt - 1) for k in side_steps(qt)]

        def oslot(h):
            return pO[:, h // 7, (h % 7) * (DH + 1):(h % 7) * (DH + 1) + DH + 1]

        with nc.Block() as block:
            @block.sync
            def _(sp):
                sp.dma_start(Wq[:], wq_t).then_inc(s["loaded"], 16)
                sp.dma_start(Wkv[:], wkv_t).then_inc(s["loaded"], 16)
                sp.dma_start(Wout[:], wout_t.rearrange("(j p) n -> p j n", p=P)).then_inc(s["loaded"], 16)
                sp.dma_start(gcol[:], g1.rearrange("(d o) -> d o", o=1)).then_inc(s["loaded"], 16)
                sp.dma_start(g2row[:], g2.rearrange("(o d) -> o d", o=1).to_broadcast([P, D])).then_inc(s["loaded"], 16)

            @block.gpsimd
            def _(pool):
                pool.memset(mask[:], 1.0).then_inc(s["mask_made"], 1)
                pool.memset(V1[:, :, DH:DH + 1], 1.0).then_inc(s["ones_made"], 1)
                pool.wait_ge(s["mask_made"], 1)
                pool.affine_select(out=mask[:], in_=mask[:], compare_op=ALU.is_ge, fill=0.0, base=0,
                                   pattern=[[1, P]], channel_multiplier=-1).then_inc(s["mask_made"], 1)
                pool.wait_ge(s["mask_made"], 2)
                pool.sem_inc(s["q_scaled"], 1)
                with pool.Fori(0, BATCH) as b:
                    def queries(qt):
                        pool.wait_ge(s["px_used"], b * PXB + q_copied[qt])
                        pool.tensor_tensor(qsq[:], qraw[:], qraw[:], ALU.mult).then_inc(s["squared"], 1)
                        pool.wait_ge(s["q_rs"], b * NQ + qt + 1)
                        pool.tensor_tensor(qn[:], qraw[:], qrs[:].rearrange("p (h o) -> p h o", o=1).to_broadcast([P, NH, DH]),
                                           ALU.mult).then_inc(s["q_scaled"], 1)
                    queries(0)
                    for qt in range(NQ):
                        if qt < NQ - 1:
                            queries(qt + 1)
                        for half in range(2):
                            h = qt * (qt + 1) + 2 * qt + half
                            pool.wait_ge(s["exped"], b * HALVES + h + 3)
                            part = pT[:, h % RING].rearrange("p a c q -> p (a c) q")
                            pool.tensor_tensor(part, part, mask[:].rearrange("p (o q) -> p o q", o=1).to_broadcast([P, 8, P]),
                                               ALU.mult).then_inc(s["masked"], 1)

            @block.scalar
            def _(act):
                act.sem_inc(s["exped"], 2)
                with act.Fori(0, BATCH) as b:
                    act.wait_ge(s["turned"], b + 1)
                    act.activation(uT[:], pS[:, 0].rearrange("p a c -> p (a c)"), ACT.Copy).then_inc(s["u_copied"], 1)
                    act.wait_ge(s["k_turned"], b + 1)
                    act.activation(kT[:], pS[:, 0].rearrange("p a c -> p (a c)"), ACT.Copy).then_inc(s["k_copied"], 1)
                    for h in range(HALVES):
                        act.wait_ge(s["s_made"], b * HALVES + h + 1)
                        act.wait_ge(s["pv_done"], b * HALVES + h + 1)
                        act.activation(pT[:, h % RING].rearrange("p a c q -> p (a c q)"),
                                       pS[:, h % 2].rearrange("p a c -> p (a c)"), ACT.Exp, scale=16.0)\
                           .then_inc(s["exped"], 1)

            @block.vector
            def _(dve):
                dve.sem_inc(s["px_used"], 1)
                dve.sem_inc(s["o_used"], 1)
                dve.wait_ge(s["loaded"], 16 * 5)
                dve.tensor_scalar(Wkv[:], Wkv[:], gcol[:, 0:1], None, ALU.mult)
                dve.tensor_scalar(Wq[:], Wq[:], gcol[:, 0:1], None, ALU.mult).then_inc(s["folded"], 1)
                CH = 4 + 13 + NQ * (2 + 13 + 1)
                with dve.Fori(0, BATCH) as b:
                    step = Chain(dve, s["chain"], b * CH)
                    for k in range(BTILES):
                        t = bass.ds(b * BTILES + k, 1)
                        ins = dve.tensor_scalar(nrm[:, k, :], core.X[:, t, :], core.rstd2[:, t], core.shift2[:, t],
                                                ALU.mult, ALU.add)
                    ins.then_inc(s["normed"], 1)
                    dve.wait_ge(s["kv_made"], b + 1)
                    step(dve.tensor_copy(kv[:].rearrange("p t c -> p (t c)"), pS[:, 1].rearrange("p a c -> p (a c)")))
                    dve.tensor_copy(V1[:, :, 0:DH], kv[:, :, DH:2 * DH])
                    step(dve.tensor_tensor(ksq[:], kv[:, :, 0:DH], kv[:, :, 0:DH], ALU.mult))
                    step(dve.tensor_reduce(kss[:], ksq[:], AX.X, ALU.add))
                    step(dve.tensor_scalar(kss[:], kss[:], 1e-24, None, ALU.max))
                    newton_rsqrt(dve, step, krs[:], kss[:], kt_[:])
                    for c in range(2):
                        ins = dve.tensor_tensor(kk[:, :, c, :], kv[:, :, 0:DH],
                                                krs[:].rearrange("p (t o) -> p t o", o=1).to_broadcast([P, BTILES, DH]),
                                                ALU.mult)
                    ins.then_inc(s["kk_made"], 1)

                    def side(key):
                        kind, qt = key
                        dve.wait_ge(s["px_made"], b * PXB + at[key] + 1)
                        if kind in ("Q0", "Q1"):
                            c = int(kind[1])
                            if c == 0:
                                dve.wait_ge(s["q_scaled"], b * NQ + qt + 1)
                            dve.tensor_copy(qraw[:, HB * c:HB * c + HB, :].rearrange("p h d -> p (h d)"), pX[:])\
                               .then_inc(s["px_used"], 1)
                            if c == 1:
                                dve.wait_ge(s["squared"], b * NQ + qt + 1)
                                step(dve.tensor_reduce(qss[:], qsq[:], AX.X, ALU.add))
                                step(dve.tensor_scalar(qss[:], qss[:], 3.90625e-27, None, ALU.max))
                                newton_rsqrt(dve, step, qrs[:], qss[:], qtmp[:])
                                dve.tensor_copy(qtmp[:], qrs[:]).then_inc(s["q_rs"], 1)
                        elif kind in ("T0", "T1"):
                            c = int(kind[1])
                            dve.tensor_copy(qT[:, qt % 2, 4 * c:4 * c + 4, :].rearrange("p j q -> p (j q)"), pX[:])\
                               .then_inc(s["px_used"], 1)
                        elif kind in ("E", "F"):
                            c = "EF".index(kind)
                            dve.tensor_copy(oT[:, 4 * c:4 * c + 4, :].rearrange("p j q -> p (j q)"), pX[:])\
                               .then_inc(s["px_used"], 1)
                        else:
                            dve.tensor_copy(OUT[:, bass.ds(b * BTILES + qt, 1), :].rearrange("p t d -> p (t d)"),
                                            pX[:, 0:D]).then_inc(s["px_used"], 1)

                    for key in order[:4]:
                        side(key)
                    for qt in range(NQ):
                        for key in sides(qt):
                            side(key)
                        dve.wait_ge(s["pv_done"], b * HALVES + (qt + 1) * (qt + 2) + RING)
                        for n, (h0, h1) in enumerate(OB):
                            view = pO[:, n, 0:(h1 - h0) * (DH + 1)].rearrange("p (h c) -> p h c", c=DH + 1)
                            ins = dve.reciprocal(osum[:, h0:h1].rearrange("p (h o) -> p h o", o=1), view[:, :, DH:DH + 1])
                        step(ins)
                        for n, (h0, h1) in enumerate(OB):
                            view = pO[:, n, 0:(h1 - h0) * (DH + 1)].rearrange("p (h c) -> p h c", c=DH + 1)
                            r = osum[:, h0:h1].rearrange("p (h o) -> p h o", o=1).to_broadcast([P, h1 - h0, DH])
                            ins = dve.tensor_tensor(on[:, h0:h1, :], view[:, :, 0:DH], r, ALU.mult)
                        ins.then_inc(s["o_used"], 1)
                    for key in order[-3:]:
                        side(key)
                    assert step.n == CH

            @block.tensor
            def _(pe):
                pe.sem_inc(s["pv_done"], RING)
                pe.wait_ge(s["folded"], 1)
                pe.wait_ge(s["ones_made"], 1)
                onf = on[:].rearrange("p h d -> p (h d)")
                qnf = qn[:].rearrange("p h d -> p (h d)")
                with pe.Fori(0, BATCH) as b:
                    def side(key):
                        kind, qt = key
                        pe.wait_ge(s["px_used"], b * PXB + at[key] + 1)
                        if kind in ("Q0", "Q1"):
                            c = int(kind[1])
                            ins = pe.matmul(pX[:], uT[:, bass.ts(qt, P)], Wq[:, bass.ts(c, 512)], start=True, stop=True)
                        elif kind in ("T0", "T1"):
                            pe.wait_ge(s["q_scaled"], b * NQ + qt + 2)
                            for j in range(4):
                                k = 4 * int(kind[1]) + j
                                ins = pe.transpose(pX[:, bass.ts(j, P)], qnf[:, bass.ts(k, P)], core.ident[:])
                        elif kind in ("E", "F"):
                            pe.wait_ge(s["o_used"], b * NQ + qt + 2)
                            for j in range(4):
                                k = 4 * "EF".index(kind) + j
                                ins = pe.transpose(pX[:, bass.ts(j, P)], onf[:, bass.ts(k, P)], core.ident[:])
                        else:
                            for j in range(8):
                                ins = pe.matmul(pX[:, 0:D], oT[:, j, :], Wout[:, j, :], start=(j == 0), stop=(j == 7))
                        ins.then_inc(s["px_made"], 1)

                    pe.wait_ge(s["normed"], b + 1)
                    pe.wait_ge(s["exped"], b * HALVES + 2)
                    flatS = [pS[:, c].rearrange("p a c -> p (a c)") for c in range(2)]
                    for k in range(BTILES):
                        ins = pe.transpose(flatS[0][:, bass.ts(k, P)], nrm[:, k, :], core.ident[:])
                    ins.then_inc(s["turned"], 1)
                    pe.wait_ge(s["u_copied"], b + 1)
                    for k in range(BTILES):
                        ins = pe.matmul(flatS[1][:, bass.ts(k, P)], uT[:, bass.ts(k, P)], Wkv[:], start=True, stop=True)
                    ins.then_inc(s["kv_made"], 1)
                    side(("Q0", 0))
                    side(("Q1", 0))
                    pe.wait_ge(s["kk_made"], b + 1)
                    kkf = kk[:].rearrange("p t c d -> p t (c d)")
                    for k in range(BTILES):
                        ins = pe.transpose(flatS[0][:, bass.ts(k, P)], kkf[:, k, :], core.ident[:])
                    ins.then_inc(s["k_turned"], 1)
                    side(("T0", 0))
                    side(("T1", 0))
                    pe.wait_ge(s["k_copied"], b + 1)

                    def scores(qt, kt, half):
                        h = qt * (qt + 1) + 2 * kt + half
                        pe.wait_ge(s["exped"], b * HALVES + h + 1)
                        for par in range(2):
                            rows = slice(64 * par, 64 * par + 64)
                            ins = pe.matmul(pS[:, half, par, :], kT[rows, bass.ts(kt, P)],
                                            qT[rows, qt % 2, 4 * half:4 * half + 4, :].rearrange("p j q -> p (j q)"),
                                            start=True, stop=True)
                        ins.then_inc(s["s_made"], 1)

                    def values(qt, kt, half):
                        h = qt * (qt + 1) + 2 * kt + half
                        if kt == 0 and half == 0:
                            pe.wait_ge(s["o_used"], b * NQ + qt + 1)
                        pe.wait_ge(s["exped"], b * HALVES + h + 3)
                        if kt == qt:
                            pe.wait_ge(s["masked"], b * 2 * NQ + 2 * qt + half + 1)
                        for j in range(HB):
                            head = HB * half + j
                            ins = pe.matmul(oslot(head), pT[:, h % RING, j % 2, j // 2, :], V1[:, kt, :],
                                            start=(kt == 0 and head % 7 == 0), stop=(kt == qt), skip_group_check=True)
                        ins.then_inc(s["pv_done"], 1)

                    for qt in range(NQ):
                        if qt > 0:
                            pe.wait_ge(s["px_used"], b * PXB + at[("T1", qt)] + 2)
                        else:
                            pe.wait_ge(s["px_used"], b * PXB + at[("T1", 0)] + 2)
                        todo = sides(qt)
                        late = []
                        for kt in range(qt + 1):
                            for half in range(2):
                                scores(qt, kt, half)
                                late.append((qt, kt, half))
                                if len(late) > 2:
                                    values(*late.pop(0))
                                if todo:
                                    side(todo.pop(0))
                        for key in todo:
                            side(key)
                        for args in late:
                            values(*args)
                    for key in order[-3:]:
                        side(key)

        stream_stats(core, f"{name}_out", src=OUT)
        tmp = kv
        chain, scaled, wsem = sem("fin_chain"), sem("fin_scaled"), sem("fin_weighted")
        with nc.Block() as block:
            @block.vector
            def _(dve):
                with dve.Fori(0, GROUPS) as g:
                    for j in range(GT):
                        t = bass.ds(g * GT + j, 1)
                        ins = dve.tensor_scalar(kv[:, j, :], OUT[:, t, :], core.rstd[:, t], core.shift[:, t], ALU.mult, ALU.add)
                    step = Chain(dve, chain, g * 3)
                    step(ins)
                    step(dve.tensor_tensor(kv[:, GT:2 * GT, :], kv[:, 0:GT, :],
                                           g2row[:].rearrange("p (o d) -> p o d", o=1).to_broadcast([P, GT, D]), ALU.mult))
                    ts = bass.ds(g * GT, GT)
                    step(dve.tensor_tensor(core.X[:, ts, :], core.X[:, ts, :], kv[:, GT:2 * GT, :], ALU.add))


def causal_single(core, name, qw, kw, vw):
    nc = core.nc
    NQ = BTILES
    SCALE = float(D) ** -0.5
    with ExitStack() as ctx:
        sb = lambda n, s, dt=F32: core.sb(f"{name}_{n}", s, dt, ctx)
        ps = lambda n, s: core.ps(f"{name}_{n}", s, F32, ctx)
        sem = lambda n: core.sem(f"{name}_{n}")
        Wq, Wk, Wv = sb("Wq", [D, D]), sb("Wk", [D, D]), sb("Wv", [D, D])
        hide = sb("hide", [P, P])
        nrm, uT, qT, kT, V = (sb(n, [P, SEQ]) for n in ("nrm", "uT", "qT", "kT", "V"))
        probs, pT = sb("probs", [P, 2, SEQ]), sb("pT", [P, SEQ])
        top, ntop, rowsum, inv = (sb(n, [P, NQ]) for n in ("top", "ntop", "rowsum", "inv"))
        pS, pT_, pO = ps("pS", [P, 2, SEQ]), ps("pTp", [P, SEQ]), ps("pO", [P, 2, 512])
        names = ("loaded hide_made normed turned u_copied q_made q_copied k_made k_copied v_made v_copied "
                 "s_made maxed scaled exped t_made t_copied o_made inverted added").split()
        s = dict(zip(names, map(sem, names)))
        with nc.Block() as block:
            @block.sync
            def _(sp):
                for t, a in ((Wq, qw), (Wk, kw), (Wv, vw)):
                    sp.dma_start(t[:], a).then_inc(s["loaded"], 16)

            @block.gpsimd
            def _(pool):
                pool.memset(hide[:], 0.0).then_inc(s["hide_made"], 1)
                pool.wait_ge(s["hide_made"], 1)
                pool.affine_select(out=hide[:], in_=hide[:], compare_op=ALU.is_ge, fill=-1e30, base=0,
                                   pattern=[[-1, P]], channel_multiplier=1).then_inc(s["hide_made"], 1)

            @block.vector
            def _(dve):
                dve.sem_inc(s["t_copied"], 1)
                dve.sem_inc(s["added"], 2)
                with dve.Fori(0, BATCH) as b:
                    for k in range(BTILES):
                        t = bass.ds(b * BTILES + k, 1)
                        ins = dve.tensor_scalar(nrm[:, bass.ts(k, D)], core.X[:, t, :].rearrange("p t d -> p (t d)"),
                                                core.rstd[:, t], core.shift[:, t], ALU.mult, ALU.add)
                    ins.then_inc(s["normed"], 1)
                    dve.wait_ge(s["k_made"], b + 1)
                    dve.tensor_copy(kT[:], pS[:, 1, :]).then_inc(s["k_copied"], 1)

                    def biggest(qt):
                        it = b * NQ + qt
                        dve.wait_ge(s["s_made"], it + 1)
                        dve.tensor_reduce(top[:, qt:qt + 1], pS[:, qt % 2, 0:P * (qt + 1)], AX.X, ALU.max)\
                           .then_inc(s["maxed"], 1)
                        dve.wait_ge(s["maxed"], it + 1)
                        dve.tensor_scalar(ntop[:, qt:qt + 1], top[:, qt:qt + 1], -SCALE, None, ALU.mult)\
                           .then_inc(s["scaled"], 1)

                    biggest(0)
                    for qt in range(NQ):
                        it = b * NQ + qt
                        if qt < NQ - 1:
                            biggest(qt + 1)
                        dve.wait_ge(s["t_made"], it + 3)
                        dve.wait_ge(s["o_made"], it + 1)
                        dve.tensor_copy(pT[:, 0:P * (qt + 1)], pT_[:, 0:P * (qt + 1)]).then_inc(s["t_copied"], 1)
                        dve.wait_ge(s["exped"], it + 3)
                        dve.reciprocal(inv[:, qt:qt + 1], rowsum[:, qt:qt + 1]).then_inc(s["inverted"], 1)
                        dve.wait_ge(s["inverted"], it + 1)
                        dve.wait_ge(s["o_made"], it + 2)
                        x = core.X[:, bass.ds(it, 1), :].rearrange("p t d -> p (t d)")
                        dve.scalar_tensor_tensor(out=x, in0=pO[:, qt % 2, 0:D], scalar=inv[:, qt:qt + 1], in1=x,
                                                 op0=ALU.mult, op1=ALU.add).then_inc(s["added"], 1)

            @block.scalar
            def _(act):
                act.sem_inc(s["exped"], 2)
                with act.Fori(0, BATCH) as b:
                    act.wait_ge(s["turned"], b + 1)
                    act.activation(uT[:], pS[:, 0, :], ACT.Copy).then_inc(s["u_copied"], 1)
                    act.wait_ge(s["q_made"], b + 1)
                    act.activation(qT[:], pS[:, 0, :], ACT.Copy).then_inc(s["q_copied"], 1)
                    act.wait_ge(s["v_made"], b + 1)
                    act.activation(V[:], pT_[:], ACT.Copy).then_inc(s["v_copied"], 1)
                    for qt in range(NQ):
                        it = b * NQ + qt
                        act.wait_ge(s["scaled"], it + 1)
                        act.wait_ge(s["t_made"], it + 1)
                        w = P * (qt + 1)
                        act.activation(probs[:, qt % 2, 0:w], pS[:, qt % 2, 0:w], ACT.Exp, bias=ntop[:, qt:qt + 1],
                                       scale=SCALE, accum_out=rowsum[:, qt:qt + 1]).then_inc(s["exped"], 1)

            @block.tensor
            def _(pe):
                pe.sem_inc(s["t_made"], 2)
                pe.sem_inc(s["o_made"], 1)
                pe.wait_ge(s["loaded"], 48)
                pe.wait_ge(s["hide_made"], 2)
                with pe.Fori(0, BATCH) as b:
                    halves = (slice(0, 512), slice(512, SEQ))
                    pe.wait_ge(s["normed"], b + 1)
                    pe.wait_ge(s["exped"], b * NQ + 2)
                    for k in range(BTILES):
                        ins = pe.transpose(pS[:, 0, bass.ts(k, P)], nrm[:, bass.ts(k, P)], core.ident[:])
                    ins.then_inc(s["turned"], 1)
                    pe.wait_ge(s["u_copied"], b + 1)
                    for h in halves:
                        ins = pe.matmul(pS[:, 0, h], Wq[:], uT[:, h], start=True, stop=True)
                    ins.then_inc(s["q_made"], 1)
                    for h in halves:
                        ins = pe.matmul(pS[:, 1, h], Wk[:], uT[:, h], start=True, stop=True)
                    ins.then_inc(s["k_made"], 1)
                    pe.wait_ge(s["t_copied"], b * NQ + 1)
                    for k in range(BTILES):
                        ins = pe.matmul(pT_[:, bass.ts(k, P)], uT[:, bass.ts(k, P)], Wv[:], start=True, stop=True)
                    ins.then_inc(s["v_made"], 1)
                    pe.wait_ge(s["q_copied"], b + 1)
                    pe.wait_ge(s["k_copied"], b + 1)

                    def scores(qt):
                        pe.wait_ge(s["exped"], b * NQ + qt + 1)
                        w = P * (qt + 1)
                        for c in range(0, w, 512):
                            n = min(512, w - c)
                            last = c + n == w
                            ins = pe.matmul(pS[:, qt % 2, c:c + n], qT[:, bass.ts(qt, P)], kT[:, c:c + n],
                                            start=True, stop=not last, skip_group_check=True)
                        pe.matmul(pS[:, qt % 2, w - P:w], core.ident[:], hide[:], start=False, stop=True,
                                  skip_group_check=True).then_inc(s["s_made"], 1)

                    scores(0)
                    for qt in range(NQ):
                        it = b * NQ + qt
                        if qt < NQ - 1:
                            scores(qt + 1)
                        pe.wait_ge(s["exped"], it + 3)
                        if qt == 0:
                            pe.wait_ge(s["v_copied"], b + 1)
                        pe.wait_ge(s["t_copied"], it + 1)
                        for k in range(qt + 1):
                            ins = pe.transpose(pT_[:, bass.ts(k, P)], probs[:, qt % 2, bass.ts(k, P)], core.ident[:])
                        ins.then_inc(s["t_made"], 1)
                        pe.wait_ge(s["t_copied"], it + 2)
                        pe.wait_ge(s["added"], it + 1)
                        for k in range(qt + 1):
                            ins = pe.matmul(pO[:, qt % 2, 0:D], pT[:, bass.ts(k, P)], V[:, bass.ts(k, D)],
                                            start=(k == 0), stop=(k == qt))
                        ins.then_inc(s["o_made"], 1)


class Experts:

    NE, TOP, FFN = 8, 2, 512
    CAP = 1280
    ROWS = NE * CAP
    HD, NKV = 8, 8
    QW = 256

    def __init__(self, core, w):
        nc = core.nc
        self.core = core
        names = ("ln1_weight", "ln1_bias", "ln2_weight", "ln2_bias", "router_weight", "moe_w1", "moe_w2")
        arrays = [w["moe_" + n if n[:4] != "moe_" else n] for n in names]
        self.ln1_weight, self.ln1_bias, self.ln2_weight, self.ln2_bias, self.router_weight, self.moe_w1, self.moe_w2 = arrays
        self.qkv_t = w["moe_qkv_t"]
        self.proj_t = w["moe_proj_t"]
        self.rows_in = nc.dram_tensor("rows_in", (self.ROWS + self.TOP * TOKENS, D), F32, kind="Internal").ap()
        self.rows_out = nc.dram_tensor("rows_out", (self.ROWS, D), F32, kind="Internal").ap()


def clear_rows(core, ex):
    NZ = 20
    with ExitStack() as ctx:
        zeros = core.sb("zeros", [P, NZ * D], F32, ctx)
        made, stored = core.sem("zeros_made"), core.sem("zeros_stored")
        with core.nc.Block() as block:
            @block.vector
            def _(dve):
                dve.memset(zeros[:], 0.0).then_inc(made, 1)

            @block.sync
            def _(sp):
                sp.wait_ge(made, 1)
                n = ex.ROWS // (P * NZ)
                for k in range(n):
                    sp.dma_start(ex.rows_in[k * P * NZ:(k + 1) * P * NZ, :].rearrange("(p t) d -> p (t d)", p=P), zeros[:])\
                      .then_inc(stored, 16)
                sp.wait_ge(stored, 16 * n)


def experts(core, name, ex):
    nc = core.nc
    NE, CAP, HD, NKV, QW = ex.NE, ex.CAP, ex.HD, ex.NKV, ex.QW
    sem = lambda n: core.sem(f"{name}_{n}")
    with ExitStack() as top:
        HA = core.sb(f"{name}_HA", [P, TILES, D], F32, top)
        gate = core.sb(f"{name}_gate", [P, 2, TILES], F32, top)
        slot_in = core.sb(f"{name}_slot_in", [P, 2, TILES], U32, top)
        slot_out = core.sb(f"{name}_slot_out", [P, 2, TILES], U32, top)
        row_attention(core, name, ex, HA)
        stream_stats(core, f"{name}_ha", src=HA)
        with ExitStack() as ctx:
            X2 = core.sb(f"{name}_X2", [P, TILES, D], F32, ctx)
            logits = core.sb(f"{name}_logits", [P, TILES, NE], F32, ctx)
            router(core, name, ex, HA, X2, logits)
            routing(core, name, ex, logits, gate, slot_in, slot_out)
            scattered = sem("scattered")
            with nc.Block() as block:
                @block.gpsimd
                def _(pool):
                    for t in range(TILES):
                        for c in range(2):
                            pool.indirect_dma_start(
                                out=ex.rows_in, out_offset=bass.IndirectOffsetOnAxis(ap=slot_in[:, c, t:t + 1], axis=0),
                                in_=X2[:, t, :], in_offset=None).then_inc(scattered, 16)
                    pool.wait_ge(scattered, 16 * 2 * TILES)
        expert_products(core, name, ex)
        with ExitStack() as ctx:
            G = core.sb(f"{name}_G", [P, 2, TILES, D], F32, ctx)
            gathered, chain = [sem(f"gathered{c}") for c in range(4)], sem("join_chain")
            with nc.Block() as block:
                @block.gpsimd
                def _(pool):
                    for t in range(TILES):
                        for c in range(2):
                            pool.indirect_dma_start(
                                out=G[:, c, t, :], out_offset=None, in_=ex.rows_out,
                                in_offset=bass.IndirectOffsetOnAxis(ap=slot_out[:, c, t:t + 1], axis=0))\
                                .then_inc(gathered[t // 8], 16)
                    for q in gathered:
                        pool.wait_ge(q, 16 * 16)

                @block.vector
                def _(dve):
                    step = Chain(dve, chain)
                    step(dve.tensor_tensor(core.X[:], core.X[:], HA[:], ALU.add))
                    for q in range(4):
                        dve.wait_ge(gathered[q], 16 * 16)
                        for c in range(2):
                            for t in range(8 * q, 8 * q + 8):
                                ins = dve.scalar_tensor_tensor(out=core.X[:, t, :], in0=G[:, c, t, :],
                                                               scalar=gate[:, c, t:t + 1], in1=core.X[:, t, :],
                                                               op0=ALU.mult, op1=ALU.add)
                            step(ins)


def row_attention(core, name, ex, HA):
    nc = core.nc
    HD, NKV, QW = ex.HD, ex.NKV, ex.QW
    with ExitStack() as ctx:
        sb = lambda n, s, dt=F32: core.sb(f"{name}_{n}", s, dt, ctx)
        ps = lambda n, s: core.ps(f"{name}_{n}", s, F32, ctx)
        sem = lambda n: core.sem(f"{name}_{n}")
        W, Wp = sb("Wqkv", [D, QW]), sb("Wproj", [D, D])
        wcol, bcol, bwide = sb("ln1w", [D, 1]), sb("ln1b", [D, 1]), sb("bwide", [D, P])
        bias = sb("qkvbias", [P, QW])
        QKV = sb("QKV", [P, TILES, QW])
        ATT = sb("ATT", [P, TILES, D])
        loaded, widened, bias_made, bias_kept, folded = map(sem, ("loaded", "widened", "bias_made", "bias_kept", "folded"))
        with ExitStack() as sub:
            nrm = core.sb(f"{name}_nrm", [P, 2, GT, D], F32, sub)
            uT = core.sb(f"{name}_uT", [P, 2, GT * P], F32, sub)
            pT = core.ps(f"{name}_pT", [P, 2, GT * P], F32, sub)
            pY = core.ps(f"{name}_pY", [P, 2, GT * QW], F32, sub)
            normed, turned, copied, product, kept = map(sem, ("q_normed", "q_turned", "q_copied", "q_product", "q_kept"))
            with nc.Block() as block:
                @block.sync
                def _(sp):
                    sp.dma_start(W[:], ex.qkv_t).then_inc(loaded, 16)
                    sp.dma_start(Wp[:], ex.proj_t).then_inc(loaded, 16)
                    sp.dma_start(wcol[:], ex.ln1_weight.rearrange("(d o) -> d o", o=1)).then_inc(loaded, 16)
                    sp.dma_start(bcol[:], ex.ln1_bias.rearrange("(d o) -> d o", o=1)).then_inc(loaded, 16)

                @block.vector
                def _(dve):
                    dve.sem_inc(kept, 2)
                    dve.wait_ge(loaded, 64)
                    dve.tensor_copy(bwide[:], bcol[:].to_broadcast([D, P])).then_inc(widened, 1)
                    dve.wait_ge(bias_made, 1)
                    dve.tensor_copy(bias[:], pY[:, 0, 0:QW]).then_inc(bias_kept, 1)
                    dve.wait_ge(bias_kept, 1)
                    dve.tensor_scalar(W[:], W[:], wcol[:, 0:1], None, ALU.mult).then_inc(folded, 1)

                    def norm(g, u):
                        dve.wait_ge(turned, g + 1)
                        for j in range(GT):
                            k = bass.ds(g * GT + j, 1)
                            ins = dve.tensor_scalar(nrm[:, u, j, :], core.X[:, k, :], core.rstd2[:, k], core.shift2[:, k],
                                                    ALU.mult, ALU.add)
                        ins.then_inc(normed, 1)

                    norm(0, 0)

                    def body(g, u, last):
                        if not last:
                            norm(g + 1, 1 - u)
                        dve.wait_ge(product, g + 3)
                        ts = bass.ds(g * GT, GT)
                        dve.tensor_tensor(QKV[:, ts, :], pY[:, u, :].rearrange("p (t c) -> p t c", c=QW),
                                          bias[:].rearrange("p (o c) -> p o c", o=1).to_broadcast([P, GT, QW]), ALU.add)\
                           .then_inc(kept, 1)
                    steps(dve, GROUPS, 2, 2, body)

                @block.tensor
                def _(pe):
                    pe.sem_inc(turned, 2)
                    pe.sem_inc(product, 2)
                    pe.wait_ge(widened, 1)
                    pe.matmul(pY[:, 0, 0:QW], bwide[:], W[:], start=True, stop=True).then_inc(bias_made, 1)
                    pe.wait_ge(folded, 1)

                    def turn(g, u):
                        pe.wait_ge(normed, g + 1)
                        pe.wait_ge(copied, g + 1)
                        for j in range(GT):
                            ins = pe.transpose(pT[:, u, bass.ts(j, P)], nrm[:, u, j, :], core.ident[:])
                        ins.then_inc(turned, 1)

                    turn(0, 0)

                    def body(g, u, last):
                        if not last:
                            turn(g + 1, 1 - u)
                        pe.wait_ge(copied, g + 3)
                        pe.wait_ge(kept, g + 1)
                        for j in range(GT):
                            ins = pe.matmul(pY[:, u, bass.ts(j, QW)], uT[:, u, bass.ts(j, P)], W[:], start=True, stop=True)
                        ins.then_inc(product, 1)
                    steps(pe, GROUPS, 2, 2, body)

                @block.scalar
                def _(act):
                    act.sem_inc(copied, 2)

                    def body(g, u, last):
                        act.wait_ge(turned, g + 3)
                        act.wait_ge(product, g + 1)
                        act.activation(uT[:, u, :], pT[:, u, :], ACT.Copy).then_inc(copied, 1)
                    steps(act, GROUPS, 2, 0, body)

        with ExitStack() as sub:
            prod = core.sb(f"{name}_prod", [P, BATCH, 2, BATCH * NKV * HD], F32, sub)
            vprod = core.sb(f"{name}_vprod", [P, BATCH, 2, BATCH * NKV * HD], F32, sub)
            sc = core.sb(f"{name}_sc", [P, BATCH * 2, BATCH * NKV], F32, sub)
            ew = core.sb(f"{name}_ew", [P, BATCH * 2, BATCH * NKV], F32, sub)
            mx, den = (core.sb(f"{name}_{n}", [P, BATCH * 2, NKV], F32, sub) for n in ("mx", "den"))
            qv = QKV[:].rearrange("p (s j) (g c) -> p s j g c", s=BATCH, c=4 * HD)
            av = ATT[:].rearrange("p (s j) (g r d) -> p s j g r d", s=BATCH, r=2, d=HD)
            chain, shifted, raised = map(sem, ("a_chain", "a_shifted", "a_raised"))
            with nc.Block() as block:
                @block.vector
                def _(dve):
                    dve.memset(sc[:], -1e30).then_inc(chain, 1)
                    dve.wait_ge(chain, 1)
                    K = 9
                    with dve.Fori(0, BTILES) as j:
                        step = Chain(dve, chain, j * K + 1)
                        J = bass.ds(j, 1)
                        for s in range(BATCH):
                            for r in range(2):
                                n = s + 1
                                q = qv[:, s, J, :, r * HD:(r + 1) * HD].to_broadcast([P, n, NKV, HD])
                                k = qv[:, 0:n, J, :, 2 * HD:3 * HD].rearrange("p t j g d -> p (t j) g d")
                                out = prod[:, s, r, 0:n * NKV * HD].rearrange("p (t g d) -> p t g d", t=n, g=NKV)
                                ins = dve.tensor_tensor(out, q, k, ALU.mult)
                        step(ins)
                        for s in range(BATCH):
                            n = s + 1
                            view = prod[:, s, :, 0:n * NKV * HD].rearrange("p r (x d) -> p r x d", d=HD)
                            ins = dve.tensor_reduce(sc[:, 2 * s:2 * s + 2, 0:n * NKV], view, AX.X, ALU.add)
                        step(ins)
                        step(dve.tensor_reduce(mx[:], sc[:].rearrange("p a (t g) -> p a g t", g=NKV), AX.X, ALU.max))
                        mb = mx[:].rearrange("p a (o g) -> p a o g", o=1).to_broadcast([P, BATCH * 2, BATCH, NKV])
                        v4 = lambda t: t[:].rearrange("p a (t g) -> p a t g", g=NKV)
                        dve.tensor_tensor(v4(ew), v4(sc), mb, ALU.subtract).then_inc(shifted, 1)
                        dve.wait_ge(raised, j + 1)
                        step(dve.tensor_reduce(den[:], ew[:].rearrange("p a (t g) -> p a g t", g=NKV), AX.X, ALU.add))
                        step(dve.reciprocal(den[:], den[:]))
                        db = den[:].rearrange("p a (o g) -> p a o g", o=1).to_broadcast([P, BATCH * 2, BATCH, NKV])
                        step(dve.tensor_tensor(v4(ew), v4(ew), db, ALU.mult))
                        for s in range(BATCH):
                            for r in range(2):
                                n = s + 1
                                a = ew[:, 2 * s + r, 0:n * NKV].rearrange("p (t g o) -> p t g o", g=NKV, o=1)\
                                    .to_broadcast([P, n, NKV, HD])
                                v = qv[:, 0:n, J, :, 3 * HD:4 * HD].rearrange("p t j g d -> p (t j) g d")
                                out = vprod[:, s, r, 0:n * NKV * HD].rearrange("p (t g d) -> p t g d", t=n, g=NKV)
                                ins = dve.tensor_tensor(out, a, v, ALU.mult)
                        step(ins)
                        for s in range(BATCH):
                            for r in range(2):
                                n = s + 1
                                view = vprod[:, s, r, 0:n * NKV * HD].rearrange("p (t g d) -> p g d t", t=n, g=NKV)
                                out = av[:, s, J, :, r, :].rearrange("p j g d -> p (j g) d")
                                ins = dve.tensor_reduce(out, view, AX.X, ALU.add)
                        step(ins)
                        step(dve.memset(mx[:, 0, 0:1], 0.0))
                        assert step.n == K, step.n

                @block.scalar
                def _(act):
                    with act.Fori(0, BTILES) as j:
                        act.wait_ge(shifted, j + 1)
                        act.activation(ew[:], ew[:], ACT.Exp, scale=HD ** -0.5).then_inc(raised, 1)

        with ExitStack() as sub:
            att = core.sb(f"{name}_att", [P, 2, GT, D], F32, sub)
            hid = core.sb(f"{name}_hid", [P, 2, GT, D], F32, sub)
            aT = core.sb(f"{name}_attT", [P, 2, GT * P], F32, sub)
            pT = core.ps(f"{name}_pT2", [P, 2, GT * P], F32, sub)
            pY = core.ps(f"{name}_pY2", [P, 2, GT * P], F32, sub)
            staged, turned, copied, product, kept, hidden = map(
                sem, ("p_staged", "p_turned", "p_copied", "p_product", "p_kept", "p_hidden"))
            with nc.Block() as block:
                @block.gpsimd
                def _(pool):
                    def body(g, u, last):
                        pool.wait_ge(turned, g + 1)
                        pool.tensor_copy(att[:, u], ATT[:, bass.ds(g * GT, GT), :]).then_inc(staged, 1)
                    steps(pool, GROUPS, 2, 0, body)

                @block.vector
                def _(dve):
                    dve.sem_inc(kept, 2)

                    def body(g, u, last):
                        dve.wait_ge(kept, g + 1)
                        normalise(dve, core, hid[:, u], g).then_inc(hidden, 1)
                        dve.wait_ge(hidden, g + 1)
                        dve.wait_ge(product, g + 3)
                        dve.tensor_tensor(HA[:, bass.ds(g * GT, GT), :], hid[:, u],
                                          pY[:, u, :].rearrange("p (t d) -> p t d", d=D), ALU.add).then_inc(kept, 1)
                    steps(dve, GROUPS, 2, 0, body)

                @block.tensor
                def _(pe):
                    pe.sem_inc(turned, 2)
                    pe.sem_inc(product, 2)

                    def turn(g, u):
                        pe.wait_ge(staged, g + 1)
                        pe.wait_ge(copied, g + 1)
                        for j in range(GT):
                            ins = pe.transpose(pT[:, u, bass.ts(j, P)], att[:, u, j, :], core.ident[:])
                        ins.then_inc(turned, 1)

                    turn(0, 0)

                    def body(g, u, last):
                        if not last:
                            turn(g + 1, 1 - u)
                        pe.wait_ge(copied, g + 3)
                        pe.wait_ge(kept, g + 1)
                        for j in range(GT):
                            ins = pe.matmul(pY[:, u, bass.ts(j, P)], aT[:, u, bass.ts(j, P)], Wp[:], start=True, stop=True)
                        ins.then_inc(product, 1)
                    steps(pe, GROUPS, 2, 2, body)

                @block.scalar
                def _(act):
                    act.sem_inc(copied, 2)

                    def body(g, u, last):
                        act.wait_ge(turned, g + 3)
                        act.wait_ge(product, g + 1)
                        act.activation(aT[:, u, :], pT[:, u, :], ACT.Copy).then_inc(copied, 1)
                    steps(act, GROUPS, 2, 0, body)


def router(core, name, ex, HA, X2, logits):
    nc, NE = core.nc, ex.NE
    with ExitStack() as ctx:
        wrow, brow = (core.sb(f"{name}_{n}", [P, D], F32, ctx) for n in ("ln2w", "ln2b"))
        R = core.sb(f"{name}_R", [D, NE], F32, ctx)
        nrm = core.sb(f"{name}_rnrm", [P, 2, GT, D], F32, ctx)
        xT = core.sb(f"{name}_rxT", [P, 2, GT * P], F32, ctx)
        pT = core.ps(f"{name}_rpT", [P, 2, GT * P], F32, ctx)
        pL = core.ps(f"{name}_rpL", [P, 2, 512], F32, ctx)
        loaded, turned, copied, product, chain, kept, made = map(
            lambda n: core.sem(f"{name}_{n}"), ("r_loaded", "r_turned", "r_copied", "r_product", "r_chain", "r_kept", "r_made"))
        wide = lambda t: t[:].rearrange("p (o d) -> p o d", o=1).to_broadcast([P, GT, D])
        with nc.Block() as block:
            @block.sync
            def _(sp):
                sp.dma_start(wrow[:], ex.ln2_weight.rearrange("(o d) -> o d", o=1).to_broadcast([P, D])).then_inc(loaded, 16)
                sp.dma_start(brow[:], ex.ln2_bias.rearrange("(o d) -> o d", o=1).to_broadcast([P, D])).then_inc(loaded, 16)
                sp.dma_start(R[:], ex.router_weight).then_inc(loaded, 16)

            @block.vector
            def _(dve):
                dve.sem_inc(kept, 2)
                dve.wait_ge(loaded, 48)

                def make(g, u):
                    step = Chain(dve, chain, g * 2)
                    dve.wait_ge(turned, g + 1)
                    for j in range(GT):
                        k = bass.ds(g * GT + j, 1)
                        ins = dve.tensor_scalar(nrm[:, u, j, :], HA[:, k, :], core.rstd[:, k], core.shift[:, k],
                                                ALU.mult, ALU.add)
                    step(ins)
                    step(dve.tensor_tensor(nrm[:, u], nrm[:, u], wide(wrow), ALU.mult))
                    dve.tensor_tensor(nrm[:, u], nrm[:, u], wide(brow), ALU.add).then_inc(made, 1)

                make(0, 0)

                def body(g, u, last):
                    if not last:
                        make(g + 1, 1 - u)
                    dve.wait_ge(product, g + 3)
                    dve.tensor_copy(logits[:, bass.ds(g * GT, GT), :],
                                    pL[:, u, 0:GT * NE].rearrange("p (t e) -> p t e", e=NE)).then_inc(kept, 1)
                steps(dve, GROUPS, 2, 2, body)

            @block.scalar
            def _(act):
                act.sem_inc(copied, 2)

                def body(g, u, last):
                    act.wait_ge(made, g + 1)
                    act.activation(X2[:, bass.ds(g * GT, GT), :], nrm[:, u], ACT.Copy)
                    act.wait_ge(turned, g + 3)
                    act.wait_ge(product, g + 1)
                    act.activation(xT[:, u, :], pT[:, u, :], ACT.Copy).then_inc(copied, 1)
                steps(act, GROUPS, 2, 0, body)

            @block.tensor
            def _(pe):
                pe.sem_inc(turned, 2)
                pe.sem_inc(product, 2)
                pe.wait_ge(loaded, 48)

                def turn(g, u):
                    pe.wait_ge(made, g + 1)
                    pe.wait_ge(copied, g + 1)
                    for j in range(GT):
                        ins = pe.transpose(pT[:, u, bass.ts(j, P)], nrm[:, u, j, :], core.ident[:])
                    ins.then_inc(turned, 1)

                turn(0, 0)

                def body(g, u, last):
                    if not last:
                        turn(g + 1, 1 - u)
                    pe.wait_ge(copied, g + 3)
                    pe.wait_ge(kept, g + 1)
                    for j in range(GT):
                        ins = pe.matmul(pL[:, u, bass.ts(j, NE)], xT[:, u, bass.ts(j, P)], R[:], start=True, stop=True)
                    ins.then_inc(product, 1)
                steps(pe, GROUPS, 2, 2, body)


def routing(core, name, ex, logits, gate, slot_in, slot_out):
    nc, NE, CAP = core.nc, ex.NE, ex.CAP
    TE = TILES * NE
    with ExitStack() as ctx:
        sb = lambda n, s, dt=F32: core.sb(f"{name}_{n}", s, dt, ctx)
        before, ones = sb("before", [P, P]), sb("ones", [P, P])
        e8i, tri = sb("e8i", [P, NE], I32), sb("tri", [P, 2, TILES], I32)
        e8, trash = sb("e8", [P, NE]), sb("trash", [P, 2, TILES])
        ebase = sb("ebase", [P, NE])
        big = [sb(f"big{k}", [P, TILES, NE]) for k in range(6)]
        p, hot1, hot2, sel, tmp, within = big
        tot, cum, one = sb("tot", [P, NE, TILES]), sb("cum", [P, NE, TILES]), sb("one", [P, TE])
        m = [sb(f"m{k}", [P, TILES]) for k in range(6)]
        m1, m2, idx, total, keep, slot = m
        pB, pA = (core.ps(f"{name}_{n}", [P, 512], F32, ctx) for n in ("pB", "pA"))
        consts, chain, shifted, raised, chosen, counted = map(
            lambda n: core.sem(f"{name}_{n}"), ("g_consts", "g_chain", "g_shifted", "g_raised", "g_chosen", "g_counted"))
        col = lambda t: t[:].rearrange("p (t o) -> p t o", o=1).to_broadcast([P, TILES, NE])
        erow = lambda t: t[:].rearrange("p (o e) -> p o e", o=1).to_broadcast([P, TILES, NE])
        with nc.Block() as block:
            @block.gpsimd
            def _(pool):
                pool.memset(ones[:], 1.0).then_inc(consts, 1)
                pool.memset(before[:], 1.0).then_inc(consts, 1)
                pool.wait_ge(consts, 2)
                pool.affine_select(out=before[:], in_=before[:], compare_op=ALU.is_gt, fill=0.0, base=0,
                                   pattern=[[1, P]], channel_multiplier=-1).then_inc(consts, 1)
                pool.iota(e8i[:], [[1, NE]], base=0, channel_multiplier=0).then_inc(consts, 1)
                pool.iota(tri[:], [[1, 2], [2 * P, TILES]], base=ex.ROWS, channel_multiplier=2).then_inc(consts, 1)

            @block.scalar
            def _(act):
                act.wait_ge(shifted, 1)
                act.activation(p[:], p[:], ACT.Exp).then_inc(raised, 1)

            @block.tensor
            def _(pe):
                pe.wait_ge(chosen, 1)
                pe.matmul(pB[:, 0:TE], before[:], sel[:].rearrange("p t e -> p (t e)"), start=True, stop=True)
                pe.matmul(pA[:, 0:TE], ones[:], sel[:].rearrange("p t e -> p (t e)"), start=True, stop=True)\
                  .then_inc(counted, 1)

            @block.vector
            def _(dve):
                step = Chain(dve, chain)
                dve.wait_ge(consts, 5)
                step(dve.tensor_copy(e8[:], e8i[:]))
                step(dve.tensor_copy(trash[:], tri[:]))
                step(dve.tensor_scalar(ebase[:], e8[:], float(CAP), None, ALU.mult))
                step(dve.tensor_scalar(e8[:], e8[:], float(NE), None, ALU.subtract))
                step(dve.memset(one[:], 1.0))
                step(dve.tensor_reduce(m1[:], logits[:], AX.X, ALU.max))
                dve.tensor_tensor(p[:], logits[:], col(m1), ALU.subtract).then_inc(shifted, 1)
                dve.wait_ge(raised, 1)
                for best, hot in ((m1, hot1), (m2, hot2)):
                    step(dve.tensor_reduce(best[:], p[:], AX.X, ALU.max))
                    step(dve.tensor_tensor(tmp[:], p[:], col(best), ALU.is_equal))
                    step(dve.tensor_tensor(tmp[:], tmp[:], erow(e8), ALU.mult))
                    step(dve.tensor_reduce(idx[:], tmp[:], AX.X, ALU.min))
                    step(dve.tensor_tensor(hot[:], erow(e8), col(idx), ALU.is_equal))
                    if hot is hot1:
                        step(dve.scalar_tensor_tensor(out=p[:].rearrange("p t e -> p (t e)"),
                                                      in0=hot[:].rearrange("p t e -> p (t e)"), scalar=-2.0,
                                                      in1=p[:].rearrange("p t e -> p (t e)"), op0=ALU.mult, op1=ALU.add))
                dve.tensor_tensor(sel[:], hot1[:], hot2[:], ALU.add).then_inc(chosen, 1)
                step(dve.tensor_tensor(total[:], m1[:], m2[:], ALU.add))
                step(dve.reciprocal(total[:], total[:]))
                dve.tensor_tensor(gate[:, 0, :], m1[:], total[:], ALU.mult)
                step(dve.tensor_tensor(gate[:, 1, :], m2[:], total[:], ALU.mult))
                dve.wait_ge(counted, 1)
                step(dve.tensor_copy(tot[:].rearrange("p e t -> p t e"), pA[:, 0:TE].rearrange("p (t e) -> p t e", e=NE)))
                step(dve.tensor_tensor_scan(cum[:].rearrange("p e t -> p (e t)"), one[:],
                                            tot[:].rearrange("p e t -> p (e t)"), 0.0, ALU.mult, ALU.add))
                step(dve.tensor_tensor(cum[:], cum[:], tot[:], ALU.subtract))
                step(dve.tensor_tensor(tot[:], cum[:], cum[:, :, 0:1].to_broadcast([P, NE, TILES]), ALU.subtract))
                step(dve.tensor_tensor(within[:], tot[:].rearrange("p e t -> p t e"),
                                       pB[:, 0:TE].rearrange("p (t e) -> p t e", e=NE), ALU.add))
                step(dve.tensor_scalar(sel[:], within[:], float(CAP), None, ALU.is_lt))
                step(dve.tensor_tensor(within[:], within[:], erow(ebase), ALU.add))
                for c, hot in ((0, hot1), (1, hot2)):
                    step(dve.tensor_tensor(tmp[:], hot[:], sel[:], ALU.mult))
                    step(dve.tensor_reduce(keep[:], tmp[:], AX.X, ALU.add))
                    step(dve.tensor_tensor(tmp[:], tmp[:], within[:], ALU.mult))
                    step(dve.tensor_reduce(slot[:], tmp[:], AX.X, ALU.add))
                    step(dve.tensor_tensor(gate[:, c, :], gate[:, c, :], keep[:], ALU.mult))
                    step(dve.tensor_copy(slot_out[:, c, :], slot[:]))
                    step(dve.tensor_scalar(keep[:], keep[:], -1.0, 1.0, ALU.mult, ALU.add))
                    step(dve.tensor_tensor(keep[:], keep[:], trash[:, c, :], ALU.mult))
                    step(dve.tensor_tensor(slot[:], slot[:], keep[:], ALU.add))
                    step(dve.tensor_copy(slot_in[:, c, :], slot[:]))


def expert_products(core, name, ex):
    nc, NE, CAP, FFN = core.nc, ex.NE, ex.CAP, ex.FFN
    CT, FC = CAP // P, FFN // P
    CH = ((0, 4), (4, 4), (8, 2))
    with ExitStack() as ctx:
        sb = lambda n, s, dt=F32: core.sb(f"{name}_{n}", s, dt, ctx)
        W1, W2 = sb("W1", [P, 2, FFN]), sb("W2", [P, 2, FC, D])
        rows, xT = sb("rows", [P, 2, CT, D]), sb("xT", [P, CAP])
        hT, y = sb("hT", [P, FC, CAP]), sb("y", [P, 2, CT, D])
        pT = core.ps(f"{name}_epT", [P, 2, 512], F32, ctx)
        pH = core.ps(f"{name}_epH", [P, 4, 512], F32, ctx)
        pO = core.ps(f"{name}_epO", [P, 2, 512], F32, ctx)
        s = {n: core.sem(f"{name}_e_{n}") for n in
             "loaded0 loaded1 turned x_copied h_made raised o_made o_copied stored0 stored1 y_free".split()}
        with nc.Block() as block:
            @block.sync
            def _(sp):
                with sp.Fori(0, NE // 2) as i:
                    for u in range(2):
                        e = 2 * i + u
                        sp.wait_ge(s["o_made"], e * 3 + 3)
                        sp.dma_start(rows[:, u], ex.rows_in[bass.ds(e * CAP, CAP), :].rearrange("(t p) d -> p t d", p=P))\
                          .then_inc(s[f"loaded{u}"], 16)
                        sp.dma_start(W1[:, u], ex.moe_w1[bass.ds(e, 1)].rearrange("e p f -> (e p) f"))\
                          .then_inc(s[f"loaded{u}"], 16)
                        sp.dma_start(W2[:, u], ex.moe_w2[bass.ds(e, 1)].rearrange("e (c p) n -> (e p) c n", p=P))\
                          .then_inc(s[f"loaded{u}"], 16)

            @block.gpsimd
            def _(pool):
                pool.sem_inc(s["y_free"], 2)
                with pool.Fori(0, NE // 2) as i:
                    for u in range(2):
                        e = 2 * i + u
                        pool.wait_ge(s["o_copied"], e * 3 + 3 + 2)
                        pool.dma_start(ex.rows_out[bass.ds(e * CAP, CAP), :].rearrange("(t p) d -> p t d", p=P), y[:, u])\
                            .then_inc(s[f"stored{u}"], 16)
                        pool.wait_ge(s[f"stored{u}"], i * 16 + 16)
                        pool.sem_inc(s["y_free"], 1)

            @block.tensor
            def _(pe):
                pe.sem_inc(s["o_made"], 6)
                pe.sem_inc(s["h_made"], 12)
                with pe.Fori(0, NE // 2) as i:
                    for u in range(2):
                        e = 2 * i + u
                        pe.wait_ge(s[f"loaded{u}"], i * 48 + 48)
                        for c, (t0, n) in enumerate(CH):
                            slot = (c + u) % 2
                            pe.wait_ge(s["x_copied"], e * 3 + c + 1)
                            for j in range(n):
                                ins = pe.transpose(pT[:, slot, bass.ts(j, P)], rows[:, u, t0 + j, :], core.ident[:])
                            ins.then_inc(s["turned"], 1)
                        for c, (t0, n) in enumerate(CH):
                            pe.wait_ge(s["x_copied"], e * 3 + c + 3)
                            for f in range(FC):
                                pe.wait_ge(s["raised"], e * 12 + 4 * c + f + 1)
                                pe.matmul(pH[:, f, 0:n * P], W1[:, u, bass.ts(f, P)], xT[:, t0 * P:(t0 + n) * P],
                                          start=True, stop=True).then_inc(s["h_made"], 1)
                        for c, (t0, n) in enumerate(CH):
                            slot = (c + u) % 2
                            pe.wait_ge(s["raised"], e * 12 + 4 * c + 4 + 4)
                            pe.wait_ge(s["o_copied"], e * 3 + c + 1)
                            for j in range(n):
                                for f in range(FC):
                                    ins = pe.matmul(pO[:, slot, bass.ts(j, D)], hT[:, f, bass.ts(t0 + j, P)], W2[:, u, f, :],
                                                    start=(f == 0), stop=(f == FC - 1))
                            ins.then_inc(s["o_made"], 1)

            @block.scalar
            def _(act):
                act.sem_inc(s["raised"], 4)
                with act.Fori(0, NE // 2) as i:
                    for u in range(2):
                        e = 2 * i + u
                        for c, (t0, n) in enumerate(CH):
                            act.wait_ge(s["o_made"], e * 3 + c + 1 + 3)
                            for f in range(FC):
                                act.wait_ge(s["h_made"], e * 12 + 4 * c + f + 1 + 12)
                                act.activation(hT[:, f, t0 * P:(t0 + n) * P], pH[:, f, 0:n * P], ACT.Gelu)\
                                   .then_inc(s["raised"], 1)

            @block.vector
            def _(dve):
                dve.sem_inc(s["x_copied"], 2)
                dve.sem_inc(s["o_copied"], 2)
                with dve.Fori(0, NE // 2) as i:
                    for u in range(2):
                        e = 2 * i + u
                        for c, (t0, n) in enumerate(CH):
                            dve.wait_ge(s["turned"], e * 3 + c + 1)
                            dve.wait_ge(s["h_made"], e * 12 + 4 * c + 4)
                            dve.tensor_copy(xT[:, t0 * P:(t0 + n) * P], pT[:, (c + u) % 2, 0:n * P])\
                               .then_inc(s["x_copied"], 1)
                        for c, (t0, n) in enumerate(CH):
                            dve.wait_ge(s["o_made"], e * 3 + c + 1 + 6)
                            if c == 0:
                                dve.wait_ge(s["y_free"], e + 1)
                            dve.tensor_copy(y[:, u, t0:t0 + n, :].rearrange("p t d -> p (t d)"),
                                            pO[:, (c + u) % 2, 0:n * P]).then_inc(s["o_copied"], 1)


def full_attention(core, name, wqkv_t, bqkv, wo_t, bo, wq, wk):
    nc = core.nc
    NH, DH, SL, NP_ = 16, 8, 64, 8
    NQ = BTILES
    C3 = 3 * D
    AHEAD = 4
    QSLOT = {"h": ((0, 2, 8), (3, 1, 8)), "m": ((2, 1, 8), (5, 1, 8)), "l": 4}
    KSLOT = {"h": ((0, 3, 16),), "m": ((1, 1, 8), (5, 1, 8)), "l": 3}
    with ExitStack() as ctx:
        sb = lambda n, s, dt=F32: core.sb(f"{name}_{n}", s, dt, ctx)
        ps = lambda n, s: core.ps(f"{name}_{n}", s, F32, ctx)
        W, Wo = sb("W", [D, C3]), sb("Wo", [D, D])
        bias, brow = sb("bias", [P, C3]), sb("brow", [P, D])
        wqr, wkr, wqk = sb("wqr", [P, DH]), sb("wkr", [P, DH]), sb("wqk", [P, NH, DH])
        nrm, uT = sb("nrm", [P, BTILES, D]), sb("uT", [P, SEQ])
        qkv = sb("qkv", [P, BTILES, C3])
        sq = sb("sq", [P, BTILES, 2 * D])
        ss, rs, rt = (sb(n, [P, BTILES * 2 * NH]) for n in ("ss", "rs", "rt"))
        Q6, K6 = sb("Q6", [P, BTILES, NH, SL], BF16), sb("K6", [P, BTILES, NH, SL], BF16)
        QT, KZ = sb("QT", [P, NP_, SEQ], BF16), sb("KZ", [P, 2, NP_, SEQ], BF16)
        QM = sb("QM", [P, 2, SEQ], BF16)
        PT = sb("PT", [P, 4, SEQ])
        V1 = sb("V1", [P, BTILES, NH, DH + 1])
        mxh, mx, mr = sb("mxh", [P, 2, NQ, 2, 2]), sb("mx", [P, NQ, 2]), sb("mr", [P, NQ, 2])
        OT, osum = sb("OT", [P, 512]), sb("osum", [P, 16])
        Z, ZT = sb("Z", [P, BTILES, NH, DH]), sb("ZT", [P, BTILES, P])
        p2, p1 = ps("p2", [P, 4, 512]), ps("p1", [P, 2, 512])
        pT, pO = ps("pT", [P, 512]), ps("pO", [P, 512])
        names = ("loaded wqk_made ones_made normed turned u_copied qkv_made qkv_kept normed_qk "
                 "h_cast r_made m_cast l_made kq_turned k_used q_used s1_made s1_used m_made t_made t_used "
                 "s2_made exped pv_done o_used ot_copied z_made chain").split()
        s = {n: core.sem(f"{name}_{n}") for n in names}
        torder = [("QM", 0)]
        for pr in range(NP_):
            if pr > 0:
                torder.append(("O", pr - 1))
            if pr < NP_ - 1:
                torder.append(("QM", pr + 1))
        torder += [("O", NP_ - 1), ("Z", 0), ("Z", 1), ("Y", 0), ("Y", 1)]
        at = {key: n for n, key in enumerate(torder)}
        NT = len(torder)
        q6v = Q6[:].rearrange("p t h c -> p (t h) c")
        k6v = K6[:].rearrange("p t h c -> p (t h) c")
        pTb = pT[:].bitcast(BF16)

        with nc.Block() as block:
            @block.sync
            def _(sp):
                row = lambda a, n: a.rearrange("(o c) -> o c", o=1).to_broadcast([P, n])
                for t, a in ((W[:], wqkv_t), (Wo[:], wo_t), (bias[:], row(bqkv, C3)), (brow[:], row(bo, D)),
                             (wqr[:], row(wq, DH)), (wkr[:], row(wk, DH))):
                    sp.dma_start(t, a).then_inc(s["loaded"], 16)

            @block.gpsimd
            def _(pool):
                for t in (Q6, K6, KZ):
                    pool.memset(t[:], 0.0).then_inc(s["ones_made"], 1)
                pool.memset(V1[:], 1.0).then_inc(s["ones_made"], 1)
                pool.wait_ge(s["ones_made"], 4)
                pool.memset(k6v[:, :, 48:51], 1.0).then_inc(s["ones_made"], 1)

            @block.scalar
            def _(act):
                act.sem_inc(s["exped"], 2)
                act.sem_inc(s["o_used"], 1)
                act.wait_ge(s["ones_made"], 5)
                with act.Fori(0, BATCH) as b:
                    act.wait_ge(s["turned"], b + 1)
                    act.activation(uT[:], p2[:, 0:2, :].rearrange("p a c -> p (a c)"), ACT.Copy).then_inc(s["u_copied"], 1)
                    for w, (v, slots) in enumerate(((q6v, QSLOT), (k6v, KSLOT))):
                        src = qkv[:, :, w * D:(w + 1) * D].rearrange("p t (h d) -> p t h d", d=DH)
                        act.wait_ge(s["normed_qk"], b * 2 + w + 1)
                        for s0, n, st in slots["h"]:
                            for k in range(n):
                                c = s0 * DH + k * st
                                ins = act.activation(v[:, :, c:c + DH].rearrange("p (t h) d -> p t h d", t=BTILES), src, ACT.Copy)
                        ins.then_inc(s["h_cast"], 1)
                    for w, (v, slots) in enumerate(((q6v, QSLOT), (k6v, KSLOT))):
                        r1 = sq[:, :, w * D:(w + 1) * D].rearrange("p t (h d) -> p t h d", d=DH)
                        act.wait_ge(s["r_made"], b * 2 + w + 1)
                        for s0, n, st in slots["m"]:
                            c = s0 * DH
                            ins = act.activation(v[:, :, c:c + DH].rearrange("p (t h) d -> p t h d", t=BTILES), r1, ACT.Copy)
                        ins.then_inc(s["m_cast"], 1)
                    for pr in range(NP_):
                        act.wait_ge(s["kq_turned"], b * 16 + 2 * pr + 2)
                        act.activation(QT[:, pr, :], p2[:, (2 * pr + 1) % 4, :].bitcast(BF16), ACT.Copy)\
                           .then_inc(s["q_used"], 1)

                    def take_queries(pr):
                        act.wait_ge(s["t_made"], b * NT + at[("QM", pr)] + 1)
                        act.activation(QM[:, pr % 2, :], pTb, ACT.Copy).then_inc(s["t_used"], 1)

                    take_queries(0)
                    for pr in range(NP_):
                        for j in range(2 * NQ):
                            k2 = b * 16 * NP_ + 16 * pr + j
                            act.wait_ge(s["s2_made"], k2 + 1)
                            act.wait_ge(s["pv_done"], k2 + 1)
                            act.activation(PT[:, j % 4, :], p2[:, 2 * (j % 2):2 * (j % 2) + 2, :].rearrange("p a c -> p (a c)"),
                                           ACT.Exp).then_inc(s["exped"], 1)
                        if pr < NP_ - 1:
                            take_queries(pr + 1)
                        act.wait_ge(s["pv_done"], b * 16 * NP_ + 16 * (pr + 1) + 4)
                        if pr > 0:
                            act.wait_ge(s["t_made"], b * NT + at[("O", pr - 1)] + 1)
                        act.activation(OT[:], pO[:], ACT.Copy).then_inc(s["o_used"], 1)

            @block.vector
            def _(dve):
                dve.sem_inc(s["s1_used"], 2)
                dve.sem_inc(s["t_used"], 1)
                dve.wait_ge(s["loaded"], 16 * 6)
                dve.wait_ge(s["ones_made"], 5)
                dve.memset(pO[:], 0.0).then_inc(s["wqk_made"], 1)
                dve.wait_ge(s["wqk_made"], 1)
                dve.tensor_tensor(wqr[:], wqr[:], wkr[:], ALU.mult).then_inc(s["wqk_made"], 1)
                dve.wait_ge(s["wqk_made"], 2)
                dve.tensor_copy(wqk[:], wqr[:].rearrange("p (o d) -> p o d", o=1).to_broadcast([P, NH, DH]))\
                   .then_inc(s["wqk_made"], 1)
                dve.wait_ge(s["wqk_made"], 3)
                CH = 3 + 13 + 1 + 5 * NP_ + NP_
                with dve.Fori(0, BATCH) as b:
                    step = Chain(dve, s["chain"], b * CH)
                    for k in range(BTILES):
                        t = bass.ds(b * BTILES + k, 1)
                        ins = dve.tensor_scalar(nrm[:, k, :], core.X[:, t, :].rearrange("p t d -> p (t d)"),
                                                core.rstd[:, t], core.shift[:, t], ALU.mult, ALU.add)
                    ins.then_inc(s["normed"], 1)
                    for half in range(2):
                        dve.wait_ge(s["qkv_made"], b * 2 + half + 1)
                        dve.tensor_tensor(qkv[:, 4 * half:4 * half + 4, :], p2[:, :, 0:C3],
                                          bias[:].rearrange("p (o c) -> p o c", o=1).to_broadcast([P, 4, C3]),
                                          ALU.add).then_inc(s["qkv_kept"], 1)
                    dve.wait_ge(s["qkv_kept"], b * 2 + 2)
                    dve.tensor_copy(V1[:, :, :, 0:DH], qkv[:, :, 2 * D:C3].rearrange("p t (h d) -> p t h d", d=DH))
                    step(dve.tensor_tensor(sq[:], qkv[:, :, 0:2 * D], qkv[:, :, 0:2 * D], ALU.mult))
                    step(dve.tensor_reduce(ss[:].rearrange("p (t h) -> p t h", t=BTILES),
                                           sq[:].rearrange("p t (h d) -> p t h d", d=DH), AX.X, ALU.add))
                    step(dve.tensor_scalar(ss[:], ss[:], 1.0 / DH, 1e-6, ALU.mult, ALU.add))
                    newton_rsqrt(dve, step, rs[:], ss[:], rt[:])
                    for w in range(2):
                        src = qkv[:, :, w * D:(w + 1) * D].rearrange("p t (h d) -> p t h d", d=DH)
                        r = rs[:].rearrange("p (t w h o) -> p t w h o", t=BTILES, w=2, o=1)[:, :, w]\
                            .to_broadcast([P, BTILES, NH, DH])
                        ins = dve.tensor_tensor(src, src, r, ALU.mult)
                        if w == 0:
                            ins.then_inc(s["normed_qk"], 1)
                    step(ins)
                    flat = qkv[:, :, D:2 * D]
                    dve.tensor_tensor(flat, flat, wqk[:].rearrange("p (o h) d -> p o (h d)", o=1).to_broadcast([P, BTILES, D]),
                                      ALU.mult).then_inc(s["normed_qk"], 1)
                    dve.wait_ge(s["normed_qk"], b * 2 + 2)
                    for w, v in enumerate((q6v, k6v)):
                        dve.wait_ge(s["h_cast"], b * 2 + w + 1)
                        src = qkv[:, :, w * D:(w + 1) * D].rearrange("p t (h d) -> p t h d", d=DH)
                        r1 = sq[:, :, w * D:(w + 1) * D].rearrange("p t (h d) -> p t h d", d=DH)
                        dve.tensor_tensor(r1, src, v[:, :, 0:DH].rearrange("p (t h) d -> p t h d", t=BTILES),
                                          ALU.subtract).then_inc(s["r_made"], 1)
                    for w, (v, slots) in enumerate(((q6v, QSLOT), (k6v, KSLOT))):
                        dve.wait_ge(s["m_cast"], b * 2 + w + 1)
                        r1 = sq[:, :, w * D:(w + 1) * D].rearrange("p t (h d) -> p t h d", d=DH)
                        c, m = slots["l"] * DH, slots["m"][0][0] * DH
                        dve.tensor_tensor(v[:, :, c:c + DH].rearrange("p (t h) d -> p t h d", t=BTILES), r1,
                                          v[:, :, m:m + DH].rearrange("p (t h) d -> p t h d", t=BTILES),
                                          ALU.subtract).then_inc(s["l_made"], 1)
                    for pr in range(NP_):
                        dve.wait_ge(s["kq_turned"], b * 16 + 2 * pr + 1)
                        bank = p2[:, (2 * pr) % 4, :].bitcast(BF16)
                        for par in range(2):
                            rows = slice(64 * par, 64 * par + 64)
                            ins = dve.tensor_copy(KZ[rows, par, pr, :], bank[rows, :])
                        ins.then_inc(s["k_used"], 1)

                    def maxima(g):
                        pr, j = g // 16, g % 16
                        for half in range(2):
                            k1 = b * 32 * NP_ + 2 * g + half
                            dve.wait_ge(s["s1_made"], k1 + 1)
                            dve.tensor_reduce(mxh[:, pr % 2, j // 2, j % 2, half:half + 1], p1[:, half, :], AX.X, ALU.max)\
                               .then_inc(s["s1_used"], 1)
                        if j == 15:
                            dve.wait_ge(s["s1_used"], b * 32 * NP_ + 2 * g + 2 + 2)
                            mh = mxh[:, pr % 2]
                            slot = lambda c: Q6[:, :, 2 * pr:2 * pr + 2, 48 + c:49 + c].rearrange("p t h o -> p t (h o)")
                            step(dve.tensor_reduce(mx[:], mh, AX.X, ALU.max, negate=True))
                            step(dve.tensor_copy(slot(0), mx[:]))
                            step(dve.tensor_tensor(mr[:], mx[:], slot(0), ALU.subtract))
                            step(dve.tensor_copy(slot(1), mr[:]))
                            step(dve.tensor_tensor(slot(2), mr[:], slot(1), ALU.subtract))
                            dve.sem_inc(s["m_made"], 1)

                    def outputs(pr):
                        dve.wait_ge(s["t_made"], b * NT + at[("O", pr)] + 1)
                        view = pT[:].rearrange("p (q c d) -> p q c d", q=4, c=4)
                        step(dve.reciprocal(osum[:].rearrange("p (q c o) -> p q c o", q=4, o=1), view[:, :, :, DH:DH + 1]))
                        r = osum[:].rearrange("p (q a h o) -> p h q a o", q=4, a=2, o=1)
                        v = pT[:].rearrange("p (q a h d) -> p h q a d", q=4, a=2, h=2)
                        for half in range(2):
                            ins = dve.tensor_tensor(Z[:, 4 * half:4 * half + 4, 2 * pr:2 * pr + 2, :], v[:, half, :, :, 0:DH],
                                                    r[:, half].to_broadcast([P, 4, 2, DH]), ALU.mult)
                        ins.then_inc(s["t_used"], 1)

                    for g in range(16 + AHEAD):
                        maxima(g)
                    for pr in range(NP_):
                        for j in range(2 * NQ):
                            g = 16 * (pr + 1) + j + AHEAD
                            if g < 16 * NP_:
                                maxima(g)
                            if j == 3 and pr > 0:
                                outputs(pr - 1)
                    outputs(NP_ - 1)
                    for half in range(2):
                        dve.wait_ge(s["t_made"], b * NT + at[("Z", half)] + 1)
                        dve.tensor_copy(ZT[:, 4 * half:4 * half + 4, :].rearrange("p t q -> p (t q)"), pT[:])\
                           .then_inc(s["t_used"], 1)
                    xs = core.X[:, bass.ds(b * BTILES, BTILES), :]
                    step2 = s["z_made"]
                    dve.tensor_tensor(xs, xs, brow[:].rearrange("p (o d) -> p o d", o=1).to_broadcast([P, BTILES, D]),
                                      ALU.add).then_inc(step2, 1)
                    dve.wait_ge(step2, b + 1)
                    for half in range(2):
                        dve.wait_ge(s["t_made"], b * NT + at[("Y", half)] + 1)
                        x4 = core.X[:, bass.ds(b * BTILES + 4 * half, 4), :]
                        dve.tensor_tensor(x4, x4, pT[:].rearrange("p (t d) -> p t d", d=D), ALU.add).then_inc(s["t_used"], 1)
                    assert step.n == CH, (step.n, CH)

            @block.tensor
            def _(pe):
                pe.sem_inc(s["pv_done"], 4)
                pe.wait_ge(s["loaded"], 16 * 6)
                pe.wait_ge(s["ones_made"], 5)
                q6f, k6f = Q6[:].rearrange("p t h c -> p t (h c)"), K6[:].rearrange("p t h c -> p t (h c)")
                pe.wait_ge(s["wqk_made"], 1)
                with pe.Fori(0, BATCH) as b:
                    pe.wait_ge(s["normed"], b + 1)
                    pe.wait_ge(s["exped"], b * 16 * NP_ + 2)
                    f2 = p2[:].rearrange("p a c -> p (a c)")
                    for k in range(BTILES):
                        ins = pe.transpose(f2[:, bass.ts(k, P)], nrm[:, k, :], core.ident[:])
                    ins.then_inc(s["turned"], 1)
                    pe.wait_ge(s["u_copied"], b + 1)
                    for half in range(2):
                        if half == 1:
                            pe.wait_ge(s["qkv_kept"], b * 2 + 1)
                        for k in range(4):
                            ins = pe.matmul(p2[:, k, 0:C3], uT[:, bass.ts(4 * half + k, P)], W[:], start=True, stop=True)
                        ins.then_inc(s["qkv_made"], 1)
                    pe.wait_ge(s["l_made"], b * 2 + 2)
                    pe.wait_ge(s["qkv_kept"], b * 2 + 2)
                    for pr in range(NP_):
                        for w, src in ((0, k6f), (1, q6f)):
                            if pr >= 2:
                                pe.wait_ge(s["q_used" if w else "k_used"], b * NP_ + pr - 1)
                            bank = p2[:, (2 * pr + w) % 4, :].bitcast(BF16)
                            for k in range(BTILES):
                                ins = pe.transpose(bank[:, bass.ts(k, P)], src[:, k, bass.ts(pr, P)], core.identb[:])
                            ins.then_inc(s["kq_turned"], 1)

                    def max_scores(g):
                        pr, j = g // 16, g % 16
                        qt, par = j // 2, j % 2
                        for half in range(2):
                            k1 = b * 32 * NP_ + 2 * g + half
                            pe.wait_ge(s["s1_used"], k1 + 1)
                            pe.matmul(p1[:, half, :], QT[:, pr, bass.ts(qt, P)], KZ[:, par, pr, bass.ts(half, 512)],
                                      start=True, stop=True).then_inc(s["s1_made"], 1)

                    def turn(key):
                        kind, n = key
                        pe.wait_ge(s["t_used"], b * NT + at[key] + 1)
                        if kind == "QM":
                            pe.wait_ge(s["m_made"], b * NP_ + n + 1)
                            for k in range(BTILES):
                                ins = pe.transpose(pTb[:, bass.ts(k, P)], q6f[:, k, bass.ts(n, P)], core.identb[:])
                        elif kind == "O":
                            pe.wait_ge(s["o_used"], b * NP_ + n + 2)
                            for k in range(4):
                                ins = pe.transpose(pT[:, bass.ts(k, P)], OT[:, bass.ts(k, P)], core.ident[:])
                        elif kind == "Z":
                            for k in range(4):
                                ins = pe.transpose(pT[:, bass.ts(k, P)], Z[:, 4 * n + k].rearrange("p h d -> p (h d)"),
                                                   core.ident[:])
                        else:
                            for k in range(4):
                                ins = pe.matmul(pT[:, bass.ts(k, P)], ZT[:, 4 * n + k, :], Wo[:], start=True, stop=True)
                        ins.then_inc(s["t_made"], 1)

                    def scores(pr, j):
                        kt, par = j // 2, j % 2
                        k2 = b * 16 * NP_ + 16 * pr + j
                        pe.wait_ge(s["exped"], k2 + 1)
                        for half in range(2):
                            ins = pe.matmul(p2[:, 2 * par + half, :], KZ[:, par, pr, bass.ts(kt, P)],
                                            QM[:, pr % 2, bass.ts(half, 512)], start=True, stop=True)
                        ins.then_inc(s["s2_made"], 1)

                    def values(pr, j):
                        kt, par = j // 2, j % 2
                        k2 = b * 16 * NP_ + 16 * pr + j
                        if j == 0:
                            pe.wait_ge(s["o_used"], b * NP_ + pr + 1)
                        pe.wait_ge(s["exped"], k2 + 3)
                        for half in range(2):
                            c = 2 * par + half
                            ins = pe.matmul(pO[32 * c:32 * c + DH + 1, :], V1[:, kt, 2 * pr + par, :],
                                            PT[:, j % 4, bass.ts(half, 512)], start=(kt == 0), stop=(kt == NQ - 1),
                                            skip_group_check=True)
                        ins.then_inc(s["pv_done"], 1)

                    pe.wait_ge(s["k_used"], b * NP_ + NP_)
                    pe.wait_ge(s["q_used"], b * NP_ + NP_)
                    for g in range(16 + AHEAD):
                        max_scores(g)
                        if g == 16:
                            turn(("QM", 0))
                            pe.wait_ge(s["t_used"], b * NT + at[("QM", 0)] + 2)
                    for pr in range(NP_):
                        for j in range(2 * NQ):
                            scores(pr, j)
                            g = 16 * (pr + 1) + j + AHEAD
                            if g < 16 * NP_:
                                max_scores(g)
                            if j >= 2:
                                values(pr, j - 2)
                            if j == 2 and pr > 0:
                                turn(("O", pr - 1))
                            if j == 14 and pr < NP_ - 1:
                                turn(("QM", pr + 1))
                        values(pr, 2 * NQ - 2)
                        values(pr, 2 * NQ - 1)
                        if pr < NP_ - 1:
                            pe.wait_ge(s["t_used"], b * NT + at[("QM", pr + 1)] + 2)
                    turn(("O", NP_ - 1))
                    pe.wait_ge(s["t_used"], b * NT + at[("O", NP_ - 1)] + 2)
                    turn(("Z", 0))
                    turn(("Z", 1))
                    pe.wait_ge(s["t_used"], b * NT + at[("Z", 1)] + 2)
                    turn(("Y", 0))
                    turn(("Y", 1))


def _as_is(a):
    return a


def _turned(a):
    return a.T


LAYOUT = {
    "x": ("L0_attn_a_u", _as_is),
    "scan_bc": ("L0_attn_a_x_proj_w", lambda a: np.tile(a[64:].T, (1, 3))),
    "scan_dt": ("L0_attn_a_x_proj_w", lambda a: a[:64].T),
    "scan_delta": ("L0_attn_a_dt_proj_w", _turned),
    "scan_delta_bias": ("L0_attn_a_dt_proj_b", _as_is),
    "scan_a_log": ("L0_attn_a_A_log", _as_is),
    "scan_skip": ("L0_attn_a_D", _as_is),
    "ffn_kernel": ("L0_ffn_kernel", _as_is),
    "ffn_bias": ("L0_ffn_bias", _as_is),
    "ffn_a_t": ("L0_ffn_a", _turned),
    "ffn_b": ("L0_ffn_b", _as_is),
    "mqa_g1": ("L0_attn_b_g1", _as_is),
    "mqa_wq_t": ("L0_attn_b_Wq", _turned),
    "mqa_wkv_t": ("L0_attn_b_Wkv", _turned),
    "mqa_wout_t": ("L0_attn_b_Wout", _turned),
    "mqa_g2": ("L0_attn_b_g2", _as_is),
    "single_qw": ("L1_attn_a_Qw", _as_is),
    "single_kw": ("L1_attn_a_Kw", _as_is),
    "single_vw": ("L1_attn_a_Vw", _as_is),
    "full_wqkv_t": ("L1_attn_b_Wqkv", _turned),
    "full_bqkv": ("L1_attn_b_bqkv", _as_is),
    "full_wo_t": ("L1_attn_b_Wo", _turned),
    "full_bo": ("L1_attn_b_bo", _as_is),
    "full_wq": ("L1_attn_b_wq", _as_is),
    "full_wk": ("L1_attn_b_wk", _as_is),
    "moe_ln1_weight": ("L1_ffn_ln1_weight", _as_is),
    "moe_ln1_bias": ("L1_ffn_ln1_bias", _as_is),
    "moe_ln2_weight": ("L1_ffn_ln2_weight", _as_is),
    "moe_ln2_bias": ("L1_ffn_ln2_bias", _as_is),
    "moe_router_weight": ("L1_ffn_router_weight", _as_is),
    "moe_w1": ("L1_ffn_moe_w1", _as_is),
    "moe_w2": ("L1_ffn_moe_w2", _as_is),
    "moe_qkv_t": ("L1_ffn_qkv_weight", _turned),
    "moe_proj_t": ("L1_ffn_proj_weight", _turned),
}


def program(nc, w, out, phases=tuple(range(8))):
    with ExitStack() as ctx:
        core = Core(nc, ctx)
        load_stream(core, w["x"].rearrange("b s d -> (b s) d"))
        ex = Experts(core, w)
        if 5 in phases or 7 in phases:
            clear_rows(core, ex)
        for n in phases:
            stream_stats(core, f"s{n}", twice=n in (2, 5, 7))
            if n == 0:
                scan_block(core, "scan", w["scan_bc"], w["scan_dt"], w["scan_delta"], w["scan_delta_bias"],
                           w["scan_a_log"], w["scan_skip"])
            elif n in (1, 3):
                ffn(core, f"ffn{n}", w["ffn_kernel"], w["ffn_bias"], w["ffn_a_t"], w["ffn_b"])
            elif n == 2:
                causal_mqa(core, "mqa", w["mqa_g1"], w["mqa_wq_t"], w["mqa_wkv_t"], w["mqa_wout_t"], w["mqa_g2"])
            elif n == 4:
                causal_single(core, "single", w["single_qw"], w["single_kw"], w["single_vw"])
            elif n in (5, 7):
                experts(core, f"moe{n}", ex)
            else:
                full_attention(core, "full", w["full_wqkv_t"], w["full_bqkv"], w["full_wo_t"], w["full_bo"],
                               w["full_wq"], w["full_wk"])
            core.end_stage()
        store_stream(core, out.rearrange("b s d -> (b s) d"))


def kernel(**inputs):
    import concourse.bacc as bacc
    from concourse.bass_utils import run_bass_kernel_spmd

    nc = bacc.Bacc("TRN2", target_bir_lowering=False, num_devices=1)
    arrays, given = {}, {}
    for name, (source, lay_out) in LAYOUT.items():
        a = np.ascontiguousarray(lay_out(np.asarray(inputs[source])))
        arrays["in_" + name] = a
        given[name] = nc.dram_tensor("in_" + name, a.shape, mybir.dt.from_np(a.dtype), kind="ExternalInput").ap()
    out = nc.dram_tensor("out", (BATCH, SEQ, D), F32, kind="ExternalOutput").ap()
    program(nc, given, out)
    return run_bass_kernel_spmd(nc, [arrays], core_ids=[0]).results[0]["out"]
```

```python
from contextlib import ExitStack

import numpy as np

import concourse.bass as bass
from concourse import mybir

F32 = mybir.dt.float32
BF16 = mybir.dt.bfloat16
F16 = mybir.dt.float16
I32 = mybir.dt.int32
U32 = mybir.dt.uint32
ALU = mybir.AluOpType
ACT = mybir.ActivationFunctionType
AX = mybir.AxisListType
RMAX = bass.bass_isa.ReduceOp.max

P = 128
D = 128
BATCH, SEQ = 4, 1024
TOKENS = BATCH * SEQ
TILES = TOKENS // P
BTILES = SEQ // P
GT = 4
GROUPS = TILES // GT
EPS = 1e-5


class Chain:

    def __init__(self, eng, sem, base=0):
        self.eng, self.sem, self.base, self.n = eng, sem, base, 0

    def __call__(self, ins):
        ins.then_inc(self.sem, 1)
        self.n += 1
        self.eng.wait_ge(self.sem, self.base + self.n)


def steps(eng, n, unroll, peel, body):
    rounds = (n - peel) // unroll
    with eng.Fori(0, rounds) as i:
        for u in range(unroll):
            body(i * unroll + u, u, False)
    for g in range(rounds * unroll, n):
        body(g, g % unroll, g == n - 1)


def follows(g, ahead):
    return not isinstance(g, int) or g + ahead < GROUPS


def newton_rsqrt(eng, step, y, v, t):
    step(eng.tensor_scalar(y.bitcast(I32), v.bitcast(I32), -0.5, 1597463007.0, ALU.mult, ALU.add))
    for _ in range(3):
        step(eng.scalar_tensor_tensor(out=t, in0=y, scalar=-0.5, in1=y, op0=ALU.mult, op1=ALU.mult))
        step(eng.tensor_tensor(t, t, v, ALU.mult))
        step(eng.scalar_tensor_tensor(out=y, in0=t, scalar=1.5, in1=y, op0=ALU.add, op1=ALU.mult))


class Core:

    def __init__(self, nc, ctx):
        self.nc, self.ctx, self.sems = nc, ctx, []
        self.X = self.sb("X", [P, TILES, D])
        self.ident = self.sb("ident", [P, P])
        self.identb = self.sb("identb", [P, P], BF16)
        self.rstd = self.sb("rstd", [P, TILES])
        self.shift = self.sb("shift", [P, TILES])
        self.rstd2 = self.sb("rstd2", [P, TILES])
        self.shift2 = self.sb("shift2", [P, TILES])
        self.stats = self.sb("stats", [P, TILES, 6])
        self.tmp = self.sb("tmp", [P, 3, TILES])

    def sb(self, name, shape, dt=F32, ctx=None):
        return (ctx or self.ctx).enter_context(self.nc.sbuf_tensor(name, shape, dt))

    def ps(self, name, shape, dt=F32, ctx=None):
        return (ctx or self.ctx).enter_context(self.nc.psum_tensor(name, shape, dt))

    def sem(self, name):
        self.sems.append(self.nc.alloc_semaphore(name=name))
        return self.sems[-1]

    def end_stage(self):
        self.nc.clear_and_free_semaphores(self.sems)
        self.nc.all_engine_barrier()
        self.sems = []


def load_stream(core, x):
    nc = core.nc
    loaded, made = core.sem("x_loaded"), core.sem("ident_made")
    with nc.Block() as block:
        @block.sync
        def _(sp):
            sp.dma_start(core.X[:], x.rearrange("(t p) d -> p t d", p=P)).then_inc(loaded, 16)
            sp.wait_ge(loaded, 16)

        @block.gpsimd
        def _(pool):
            pool.memset(core.ident[:], 0.0).then_inc(made, 1)
            pool.wait_ge(made, 1)
            pool.affine_select(out=core.ident[:], in_=core.ident[:], compare_op=ALU.not_equal, fill=1.0, base=0,
                               pattern=[[-1, P]], channel_multiplier=1).then_inc(made, 1)
            pool.wait_ge(made, 2)
            pool.tensor_copy(core.identb[:], core.ident[:]).then_inc(made, 1)


def store_stream(core, out):
    stored = core.sem("out_stored")
    with core.nc.Block() as block:
        @block.sync
        def _(sp):
            sp.dma_start(out.rearrange("(t p) d -> p t d", p=P), core.X[:]).then_inc(stored, 16)
            sp.wait_ge(stored, 16)


def moments(dve, step, stats, n, mean, var, t, eps):
    me, m2e, mo, m2o = (stats[:, :, k] for k in (1, 2, 4, 5))
    step(dve.tensor_tensor(t, me, mo, ALU.subtract))
    dve.tensor_tensor(mean, me, mo, ALU.add)
    step(dve.tensor_tensor(var, m2e, m2o, ALU.add))
    step(dve.scalar_tensor_tensor(out=t, in0=t, scalar=n / 4.0, in1=t, op0=ALU.mult, op1=ALU.mult))
    step(dve.tensor_tensor(var, var, t, ALU.add))
    dve.tensor_scalar(mean, mean, 0.5, None, ALU.mult)
    step(dve.tensor_scalar(var, var, 1.0 / n, eps, ALU.mult, ALU.add))


def second_norm(dve, step, core, var, t):
    r2 = core.rstd2[:]
    step(dve.tensor_scalar(var, var, EPS, None, ALU.subtract))
    step(dve.tensor_tensor(var, var, core.rstd[:], ALU.mult))
    step(dve.tensor_tensor(var, var, core.rstd[:], ALU.mult))
    step(dve.tensor_scalar(var, var, EPS, None, ALU.add))
    newton_rsqrt(dve, step, r2, var, t)
    step(dve.tensor_tensor(r2, r2, core.rstd[:], ALU.mult))


def stream_stats(core, name, src=None, twice=False):
    src = core.X if src is None else src
    chain = core.sem(f"{name}_stats_chain")
    mean, var, t = (core.tmp[:, k, :] for k in range(3))
    with core.nc.Block() as block:
        @block.vector
        def _(dve):
            with dve.Fori(0, TILES // GT) as i:
                for u in range(GT):
                    dve.bn_stats(core.stats[:, bass.ds(i * GT + u, 1), :], src[:, bass.ds(i * GT + u, 1), :])
            step = Chain(dve, chain)
            step(dve.memset(t, 0.0))
            moments(dve, step, core.stats, D, mean, var, t, EPS)
            newton_rsqrt(dve, step, core.rstd[:], var, t)
            if twice:
                step(dve.scalar_tensor_tensor(out=core.shift[:], in0=mean, scalar=-1.0, in1=core.rstd[:],
                                              op0=ALU.mult, op1=ALU.mult))
                second_norm(dve, step, core, var, t)
            scale = core.rstd2 if twice else core.rstd
            out = core.shift2 if twice else core.shift
            step(dve.scalar_tensor_tensor(out=out[:], in0=mean, scalar=-1.0, in1=scale[:], op0=ALU.mult, op1=ALU.mult))


def normalise(dve, core, out, g, last_inc=None):
    for j in range(GT):
        k = bass.ds(g * GT + j, 1)
        ins = dve.tensor_scalar(out[:, j, :], core.X[:, k, :], core.rstd[:, k], core.shift[:, k], ALU.mult, ALU.add)
    return ins


def ffn(core, name, w, bias, a_t, b):
    nc = core.nc
    with ExitStack() as ctx:
        sb = lambda n, s, dt=F32: core.sb(f"{name}_{n}", s, dt, ctx)
        ps = lambda n, s: core.ps(f"{name}_{n}", s, F32, ctx)
        sem = lambda n: core.sem(f"{name}_{n}")
        W, aT, B = sb("W", [D, D]), sb("aT", [16, D]), sb("B", [16, D])
        bias4, ones = sb("bias4", [1, GT, D]), sb("ones", [1, P])
        amax, top, scale, inv = sb("amax", [P, 1]), sb("top", [P, 1]), sb("scale", [P, 1]), sb("inv", [P, 1])
        q = sb("q", [D, D])
        weff = sb("weff", [D, D])
        nrm, uT = sb("nrm", [P, 2, GT, D]), sb("uT", [P, 2, GT * P])
        pT, pY = ps("pT", [P, 2, GT * P]), ps("pY", [P, 2, GT * P])
        pW = ps("pW", [P, D])
        loaded, chain, absmax, allmax, ones_made, ab_made, weff_made = map(
            sem, ("loaded", "chain", "absmax", "allmax", "ones_made", "ab_made", "weff_made"))
        normed, turned, copied, product, added = map(sem, ("normed", "turned", "copied", "product", "added"))
        flat = core.X[:].rearrange("p t d -> p (t d)")
        with nc.Block() as block:
            @block.sync
            def _(sp):
                sp.dma_start(W[:], w).then_inc(loaded, 16)
                sp.dma_start(aT[:], a_t).then_inc(loaded, 16)
                sp.dma_start(B[:], b).then_inc(loaded, 16)
                for j in range(GT):
                    sp.dma_start(bias4[:, j, :], bias.rearrange("(o n) -> o n", o=1)).then_inc(loaded, 16)

            @block.gpsimd
            def _(pool):
                pool.memset(ones[:], 1.0).then_inc(ones_made, 1)
                pool.wait_ge(absmax, 1)
                pool.partition_all_reduce(top[:], amax[:], P, RMAX).then_inc(allmax, 1)

            @block.vector
            def _(dve):
                dve.sem_inc(added, 2)
                step = Chain(dve, chain)
                dve.wait_ge(loaded, 16 * 7)
                dve.tensor_reduce(amax[:], W[:], AX.X, ALU.max, apply_absolute_value=True).then_inc(absmax, 1)
                dve.wait_ge(allmax, 1)
                step(dve.reciprocal(inv[:], top[:]))
                step(dve.tensor_scalar(scale[:], top[:], 1.0 / 7.0, None, ALU.mult))
                step(dve.reciprocal(inv[:], scale[:]))
                step(dve.tensor_scalar(q[:], W[:], inv[:, 0:1], 12582912.0, ALU.mult, ALU.add))
                step(dve.tensor_scalar(q[:], q[:], 12582912.0, -8.0, ALU.subtract, ALU.max))
                step(dve.tensor_scalar(q[:], q[:], 7.0, scale[:, 0:1], ALU.min, ALU.mult))
                dve.wait_ge(ab_made, 1)
                dve.tensor_tensor(weff[:], q[:], pW[:], ALU.add).then_inc(weff_made, 1)

                def norm(g, u):
                    dve.wait_ge(turned, g + 1)
                    normalise(dve, core, nrm[:, u], g).then_inc(normed, 1)

                norm(0, 0)
                norm(1, 1)

                def body(g, u, last):
                    if follows(g, 2):
                        norm(g + 2, u)
                    dve.wait_ge(product, g + 3)
                    cols = bass.ds(g * GT * D, GT * D)
                    dve.tensor_tensor(flat[:, cols], flat[:, cols], pY[:, u, :], ALU.add).then_inc(added, 1)
                steps(dve, GROUPS, 2, 2, body)

            @block.tensor
            def _(pe):
                pe.sem_inc(turned, 2)
                pe.sem_inc(product, 2)
                pe.wait_ge(loaded, 16 * 7)
                pe.matmul(pW[:], aT[:], B[:], start=True, stop=True).then_inc(ab_made, 1)
                pe.wait_ge(ones_made, 1)
                pe.wait_ge(weff_made, 1)

                def turn(g, u):
                    pe.wait_ge(normed, g + 1)
                    pe.wait_ge(copied, g + 1)
                    for j in range(GT):
                        ins = pe.transpose(pT[:, u, bass.ts(j, P)], nrm[:, u, j, :], core.ident[:])
                    ins.then_inc(turned, 1)

                turn(0, 0)

                def body(g, u, last):
                    if not last:
                        turn(g + 1, 1 - u)
                    pe.wait_ge(copied, g + 3)
                    pe.wait_ge(added, g + 1)
                    pe.matmul(pY[:, u, :], ones[:], bias4[:], start=True, stop=False, skip_group_check=True)
                    for j in range(GT):
                        ins = pe.matmul(pY[:, u, bass.ts(j, P)], uT[:, u, bass.ts(j, P)], weff[:],
                                        start=False, stop=(j == GT - 1), skip_group_check=True)
                    ins.then_inc(product, 1)
                steps(pe, GROUPS, 2, 2, body)

            @block.scalar
            def _(act):
                act.sem_inc(copied, 2)

                def body(g, u, last):
                    act.wait_ge(turned, g + 3)
                    act.wait_ge(product, g + 1)
                    act.activation(uT[:, u, :], pT[:, u, :], ACT.Copy).then_inc(copied, 1)
                steps(act, GROUPS, 2, 0, body)


def scan_block(core, name, wbc, wdt, dtw, dtb, a_log, dvec):
    nc = core.nc
    NS = 16
    with ExitStack() as ctx:
        sb = lambda n, s, dt=F32: core.sb(f"{name}_{n}", s, dt, ctx)
        ps = lambda n, s: core.ps(f"{name}_{n}", s, F32, ctx)
        sem = lambda n: core.sem(f"{name}_{n}")
        Wbc, Wdt, Wz = sb("Wbc", [D, 96]), sb("Wdt", [D, 64]), sb("Wz", [64, D])
        zbias, dcol, A = sb("zbias", [P, 1]), sb("dcol", [P, 1]), sb("A", [P, NS])
        diagD = sb("diagD", [P, P])
        sel = sb("sel", [96, 2 * NS, P], BF16)
        nrm = sb("nrm", [P, BTILES, D])
        uT, dtT, zc, zabs, zexp, zpos = (sb(n, [P, SEQ]) for n in ("uT", "dtT", "zc", "zabs", "zexp", "zpos"))
        delta, du, yT = (sb(n, [P, SEQ]) for n in ("delta", "du", "yT"))
        hi, mid, rest, rest2 = sb("hi", [96, SEQ], BF16), sb("mid", [96, SEQ], BF16), sb("rest", [96, SEQ]), sb("rest2", [96, SEQ])
        bc3 = sb("bc3", [96, SEQ], BF16)
        dA, Bs, dBu, state, yc = (sb(n, [P, 2, SEQ]) for n in ("dA", "Bs", "dBu", "state", "yc"))
        pM, pB, pC, pY = (ps(n, [P, SEQ]) for n in ("pM", "pB", "pC", "pY"))
        names = ("loaded chain a_made sel_made diag_made normed turned u_copied bc_made hi_made rest_made split_made "
                 "dt_made dt_copied z_made z_copied act_chain log_made pos_made delta_made du_made "
                 "b_made b_copied c_made multiplied da_made scanned weighted summed y_copied y_turned added").split()
        s = dict(zip(names, map(sem, names)))
        flat = core.X[:].rearrange("p t d -> p (t d)")
        H = SEQ // 2
        with nc.Block() as block:
            @block.sync
            def _(sp):
                sp.dma_start(Wbc[:], wbc).then_inc(s["loaded"], 16)
                sp.dma_start(Wdt[:], wdt).then_inc(s["loaded"], 16)
                sp.dma_start(Wz[:], dtw).then_inc(s["loaded"], 16)
                sp.dma_start(zbias[:], dtb.rearrange("(d o) -> d o", o=1)).then_inc(s["loaded"], 16)
                sp.dma_start(dcol[:], dvec.rearrange("(d o) -> d o", o=1)).then_inc(s["loaded"], 16)
                sp.dma_start(A[:], a_log.rearrange("(o n) -> o n", o=1).to_broadcast([P, NS])).then_inc(s["loaded"], 16)

            @block.gpsimd
            def _(pool):
                pool.memset(sel[:], 0.0).then_inc(s["sel_made"], 1)
                for k in range(3):
                    pool.wait_ge(s["sel_made"], k + 1)
                    pool.affine_select(out=sel[:], in_=sel[:], compare_op=ALU.not_equal, fill=1.0, base=-32 * k,
                                       pattern=[[-1, 2 * NS], [0, P]], channel_multiplier=1).then_inc(s["sel_made"], 1)
                pool.sem_inc(s["multiplied"], 2)
                with pool.Fori(0, BATCH) as b:
                    def body(n, u, last):
                        it = b * NS + n
                        pool.wait_ge(s["du_made"], b + 1)
                        pool.wait_ge(s["b_copied"], it + 2)
                        pool.wait_ge(s["scanned"], it + 1)
                        pool.tensor_tensor(dBu[:, u, :], Bs[:, u, :], du[:], ALU.mult).then_inc(s["multiplied"], 1)
                    steps(pool, NS, 2, 0, body)

            @block.vector
            def _(dve):
                dve.sem_inc(s["scanned"], 2)
                dve.sem_inc(s["weighted"], 1)
                dve.sem_inc(s["added"], 1)
                dve.wait_ge(s["loaded"], 16 * 6)
                dve.tensor_scalar(diagD[:], core.ident[:], dcol[:, 0:1], None, ALU.mult).then_inc(s["diag_made"], 1)
                with dve.Fori(0, BATCH) as b:
                    step = Chain(dve, s["chain"], b * 3)
                    for k in range(BTILES):
                        t = bass.ds(b * BTILES + k, 1)
                        ins = dve.tensor_scalar(nrm[:, k, :], core.X[:, t, :], core.rstd[:, t], core.shift[:, t],
                                                ALU.mult, ALU.add)
                    ins.then_inc(s["normed"], 1)
                    dve.wait_ge(s["hi_made"], b + 1)
                    dve.tensor_tensor(rest[:], pM[0:96, :], hi[:], ALU.subtract).then_inc(s["rest_made"], 1)
                    dve.wait_ge(s["rest_made"], b + 1)
                    step(dve.tensor_copy(mid[:], rest[:]))
                    step(dve.tensor_tensor(rest2[:], rest[:], mid[:], ALU.subtract))
                    dve.tensor_copy(bc3[0:32, :], hi[0:32, :])
                    dve.tensor_copy(bc3[32:64, :], mid[32:64, :])
                    dve.tensor_copy(bc3[64:96, :], rest2[64:96, :]).then_inc(s["split_made"], 1)
                    dve.wait_ge(s["z_copied"], b + 1)
                    step(dve.tensor_scalar(zpos[:], zc[:], 0.0, None, ALU.max))
                    dve.wait_ge(s["log_made"], b + 1)
                    dve.tensor_tensor(delta[:], zpos[:], zexp[:], ALU.add).then_inc(s["delta_made"], 1)
                    dve.wait_ge(s["delta_made"], b + 1)
                    dve.tensor_tensor(du[:], delta[:], uT[:], ALU.mult).then_inc(s["du_made"], 1)

                    def body(n, u, last):
                        it = b * NS + n
                        dve.wait_ge(s["da_made"], it + 1)
                        dve.wait_ge(s["multiplied"], it + 3)
                        dve.tensor_tensor_scan(state[:, u, :], dA[:, u, :], dBu[:, u, :], 0.0, ALU.mult,
                                               ALU.add).then_inc(s["scanned"], 1)
                        dve.wait_ge(s["scanned"], it + 3)
                        dve.wait_ge(s["c_made"], it + 1)
                        dve.wait_ge(s["summed"], it + 1)
                        dve.tensor_tensor(yc[:, u, :], state[:, u, :], pC[:], ALU.mult).then_inc(s["weighted"], 1)
                    steps(dve, NS, 2, 0, body)
                    dve.wait_ge(s["y_turned"], b + 1)
                    cols = bass.ds(b * SEQ, SEQ)
                    dve.tensor_tensor(flat[:, cols], flat[:, cols], pM[:], ALU.add).then_inc(s["added"], 1)

            @block.scalar
            def _(act):
                act.wait_ge(s["loaded"], 16 * 6)
                act.activation(A[:], A[:], ACT.Exp).then_inc(s["a_made"], 1)
                act.wait_ge(s["a_made"], 1)
                act.activation(A[:], A[:], ACT.Copy, scale=-1.0).then_inc(s["a_made"], 1)
                act.wait_ge(s["a_made"], 2)
                act.sem_inc(s["b_copied"], 1)
                with act.Fori(0, BATCH) as b:
                    step = Chain(act, s["act_chain"], b * 2)
                    act.wait_ge(s["turned"], b + 1)
                    act.activation(uT[:], pM[:], ACT.Copy).then_inc(s["u_copied"], 1)
                    act.wait_ge(s["bc_made"], b + 1)
                    act.activation(hi[:], pM[0:96, :], ACT.Copy).then_inc(s["hi_made"], 1)
                    act.wait_ge(s["dt_made"], b + 1)
                    act.activation(dtT[0:64, :], pM[0:64, :], ACT.Copy).then_inc(s["dt_copied"], 1)
                    act.wait_ge(s["z_made"], b + 1)
                    act.activation(zc[:], pM[:], ACT.Identity, bias=zbias[:, 0:1]).then_inc(s["z_copied"], 1)
                    act.wait_ge(s["z_copied"], b + 1)
                    step(act.activation(zabs[:], zc[:], ACT.Abs))
                    step(act.activation(zexp[:], zabs[:], ACT.Exp, scale=-1.0))
                    act.activation(zexp[:], zexp[:], ACT.Ln, bias=1.0).then_inc(s["log_made"], 1)
                    act.wait_ge(s["delta_made"], b + 1)

                    def body(n, u, last):
                        it = b * NS + n
                        act.wait_ge(s["b_made"], it + 1)
                        act.wait_ge(s["multiplied"], it + 1)
                        act.activation(Bs[:, u, :], pB[:], ACT.Copy).then_inc(s["b_copied"], 1)
                        act.wait_ge(s["scanned"], it + 1)
                        act.activation(dA[:, u, :], delta[:], ACT.Exp, scale=A[:, bass.ds(n, 1)]).then_inc(s["da_made"], 1)
                    steps(act, NS, 2, 0, body)
                    act.wait_ge(s["summed"], b * NS + NS + 2)
                    act.activation(yT[:], pY[:], ACT.Copy).then_inc(s["y_copied"], 1)

            @block.tensor
            def _(pe):
                halves = (slice(0, H), slice(H, SEQ))
                pe.sem_inc(s["summed"], 2)
                pe.wait_ge(s["loaded"], 16 * 6)
                pe.wait_ge(s["sel_made"], 4)
                pe.wait_ge(s["diag_made"], 1)
                with pe.Fori(0, BATCH) as b:
                    pe.wait_ge(s["normed"], b + 1)
                    pe.wait_ge(s["added"], b + 1)
                    for k in range(BTILES):
                        ins = pe.transpose(pM[:, bass.ts(k, P)], nrm[:, k, :], core.ident[:])
                    ins.then_inc(s["turned"], 1)
                    pe.wait_ge(s["u_copied"], b + 1)
                    for h in halves:
                        ins = pe.matmul(pM[0:96, h], Wbc[:], uT[:, h], start=True, stop=True)
                    ins.then_inc(s["bc_made"], 1)
                    for h in halves:
                        pe.matmul(pY[:, h], diagD[:], uT[:, h], start=True, stop=False, skip_group_check=True)
                    pe.wait_ge(s["rest_made"], b + 1)
                    for h in halves:
                        ins = pe.matmul(pM[0:64, h], Wdt[:], uT[:, h], start=True, stop=True)
                    ins.then_inc(s["dt_made"], 1)
                    pe.wait_ge(s["dt_copied"], b + 1)
                    for h in halves:
                        ins = pe.matmul(pM[:, h], Wz[:], dtT[0:64, h], start=True, stop=True)
                    ins.then_inc(s["z_made"], 1)
                    pe.wait_ge(s["split_made"], b + 1)

                    def spread_b(n):
                        pe.wait_ge(s["b_copied"], b * NS + n + 1)
                        for h in halves:
                            ins = pe.matmul(pB[:, h], sel[:, bass.ds(n, 1), :], bc3[:, h], start=True, stop=True)
                        ins.then_inc(s["b_made"], 1)

                    def spread_c(n):
                        pe.wait_ge(s["weighted"], b * NS + n + 1)
                        for h in halves:
                            ins = pe.matmul(pC[:, h], sel[:, bass.ds(n + NS, 1), :], bc3[:, h], start=True, stop=True)
                        ins.then_inc(s["c_made"], 1)

                    spread_b(0)
                    spread_c(0)

                    def body(n, u, last):
                        if not last:
                            spread_b(n + 1)
                            spread_c(n + 1)
                        pe.wait_ge(s["weighted"], b * NS + n + 2)
                        for h in halves:
                            ins = pe.matmul(pY[:, h], core.ident[:], yc[:, u, h], start=False, stop=last,
                                            skip_group_check=True)
                        ins.then_inc(s["summed"], 1)
                    steps(pe, NS, 2, 2, body)
                    pe.wait_ge(s["y_copied"], b + 1)
                    pe.wait_ge(s["log_made"], b + 1)
                    for k in range(BTILES):
                        ins = pe.transpose(pM[:, bass.ts(k, P)], yT[:, bass.ts(k, P)], core.ident[:])
                    ins.then_inc(s["y_turned"], 1)


def causal_mqa(core, name, g1, wq_t, wkv_t, wout_t, g2):
    nc = core.nc
    NH, DH = 16, 64
    NQ = BTILES
    HALVES = NQ * (NQ + 1)
    HB = NH // 2
    RING, LAG = 4, 3
    UNIT = 1024.0
    GAP = 8
    BELOW = -(2.0 ** 23)
    EARLY = 4
    with ExitStack() as ctx:
        sb = lambda n, s, dt=F32: core.sb(f"{name}_{n}", s, dt, ctx)
        ps = lambda n, s: core.ps(f"{name}_{n}", s, F32, ctx)
        sem = lambda n: core.sem(f"{name}_{n}")
        Wq, Wkv, Wout = sb("Wq", [D, NH * DH]), sb("Wkv", [D, 2 * DH]), sb("Wout", [P, 8, D])
        gcol, g2row = sb("gcol", [P, 1]), sb("g2row", [P, D])
        identh = sb("identh", [P, P], F16)
        below = sb("below", [P, 4, P], BF16)
        nrm, uT = sb("nrm", [P, BTILES, D]), sb("uT", [P, SEQ])
        kv, V = sb("kv", [P, BTILES, 2 * DH]), sb("V", [P, BTILES, DH])
        ksq, kss, krs, ktmp = sb("ksq", [P, BTILES, DH]), sb("kss", [P, BTILES]), sb("krs", [P, BTILES]), sb("ktmp", [P, BTILES])
        k2 = sb("k2", [P, BTILES, 2, 2, DH], F16)
        kT = sb("kT", [P, 2, SEQ], F16)
        qraw, qsq, qn = sb("qraw", [P, 2, NH, DH]), sb("qsq", [P, NH, DH]), sb("qn", [P, NH, DH])
        q2 = sb("q2", [P, 2, NH, 2, DH], F16)
        qss, qrs, qtmp = (sb(n, [P, NH]) for n in ("qss", "qrs", "qtmp"))
        qT = sb("qT", [P, NQ, NH, P], F16)
        pT = sb("pT", [P, RING, 2, 512])
        sums, over = sb("sums", [P, 2, 2, 2, 512]), sb("over", [P, 2, P])
        pick, spread = sb("pick", [P, 4, 32]), sb("spread", [P, 2, 4, 2, DH])
        zero = sb("zero", [P, 1])
        oraw, oT = sb("oraw", [P, 2, 512]), sb("oT", [P, 2, 4, P])
        OUT = sb("OUT", [P, TILES, D])
        pS = ps("pS", [P, 2, 2, 512])
        pO = ps("pO", [P, 2, 512])
        pX = ps("pX", [P, 2, 512])
        names = ("loaded folded below_made ones_made normed k_split k_turned k_copied s_made exped pv_done o_taken summed_even summed_odd "
                 "px_made px_dve px_act q_scaled q_split v_copied chain").split()
        s = dict(zip(names, map(sem, names)))

        def queries(tiles):
            out = []
            for n, (tile, row) in enumerate(tiles):
                out += [("Q", tile, row, 0), ("Q", tile, row, 1)]
                if n > 0:
                    out += [("T",) + tiles[n - 1] + (0,), ("T",) + tiles[n - 1] + (1,)]
            return out + [("T",) + tiles[-1] + (0,), ("T",) + tiles[-1] + (1,)]

        def row_start(row):
            return [("U", 0, row, 0), ("U", 0, row, 1), ("KV", 0, row, 0), ("KV", 0, row, 1)]

        def outputs(qt):
            return [("S", qt, 0, 0), ("B", qt, 0, 0), ("B", qt, 0, 1), ("G", qt, 0, 0)]

        first_uses = row_start(0) + queries([(t, 0) for t in range(EARLY)])

        def plan(last):
            prep = queries([(t, 0) for t in range(EARLY, NQ)])
            if not last:
                prep += row_start(1) + queries([(t, 1) for t in range(EARLY)])
            slots, done = [], {}
            for qt in range(NQ):
                outs = outputs(qt - 1) if qt > 0 else []
                for h in range(2 * (qt + 1)):
                    now = len(slots)
                    if outs and (h >= LAG or h == 2 * qt + 1):
                        slots.append([outs.pop(0)] if h < 2 * qt + 1 else outs)
                    elif prep and (prep[0][0] != "T" or now - done[prep[0][1:3]] >= GAP or now >= prep[0][1] * (prep[0][1] + 1) - 3):
                        key = prep.pop(0)
                        if key[0] == "Q":
                            done[key[1:3]] = now
                        slots.append([key])
                    else:
                        slots.append([])
            slots[-1] = slots[-1] + prep
            return slots, outputs(NQ - 1)

        plans = {last: plan(last) for last in (False, True)}
        flat = {last: [u for sl in plans[last][0] for u in sl] + plans[last][1] for last in plans}
        for qt in range(EARLY, NQ):
            assert all(any(("T", qt, 0, 1) in sl for sl in plans[last][0][:qt * (qt + 1)]) for last in plans)
        FIRST, USES = len(first_uses), len(flat[False])

        assert FIRST % 2 == 0 and USES % 2 == 0
        taker = lambda key: "px_act" if key[0] == "T" else "px_dve"
        per_row = {q: sum(taker(u) == q for u in flat[False]) for q in ("px_act", "px_dve")}
        at_first = {q: sum(taker(u) == q for u in first_uses) for q in ("px_act", "px_dve")}

        def wait_taken(eng, b, uses, n):
            q = taker(uses[n])
            count = sum(taker(u) == q for u in uses[:n + 1])
            eng.wait_ge(s[q], count if b is None else at_first[q] + b * per_row[q] + count)

        def norms(last):
            out = {}
            for h, uses in enumerate(plans[last][0]):
                for kind, qt, ahead, c in uses:
                    if kind == "Q" and c == 1:
                        for part in range(3):
                            out.setdefault(min(h + 1 + part, HALVES - 1), []).append((qt, ahead, part))
            return out

        def splits(last):
            out = {}
            for h, uses in enumerate(plans[last][0]):
                for kind, qt, ahead, c in uses:
                    if kind == "Q" and c == 1:
                        turned = next(k for k, u in enumerate(plans[last][0]) if ("T", qt, ahead, 0) in u)
                        out.setdefault(min(h + 5, turned), []).append((qt, ahead))
            return out

        def rows(eng, body):
            with eng.Fori(0, BATCH - 1) as b:
                body(b, False)
            body(BATCH - 1, True)

        def add_up(eng, b, qt, h, done):
            part, total = pT[:, h % RING], sums[:, qt % 2, h % 2]
            if h - qt * (qt + 1) < 2:
                eng.tensor_tensor(total, part, zero[:].rearrange("p (a c) -> p a c", c=1).to_broadcast([P, 2, 512]), ALU.add).then_inc(s[done], 1)
            else:
                eng.wait_ge(s[done], b * (HALVES // 2) + h // 2 + 2)
                eng.tensor_tensor(total, total, part, ALU.add).then_inc(s[done], 1)

        with nc.Block() as block:
            @block.sync
            def _(sp):
                sp.dma_start(Wkv[:], wkv_t).then_inc(s["loaded"], 16)
                sp.dma_start(Wq[:], wq_t).then_inc(s["loaded"], 16)
                sp.dma_start(gcol[:], g1.rearrange("(d o) -> d o", o=1)).then_inc(s["loaded"], 16)
                sp.dma_start(Wout[:], wout_t.rearrange("(j p) n -> p j n", p=P)).then_inc(s["loaded"], 16)
                sp.dma_start(g2row[:], g2.rearrange("(o d) -> o d", o=1).to_broadcast([P, D])).then_inc(s["loaded"], 16)

            @block.gpsimd
            def _(pool):
                pool.memset(zero[:], 0.0).then_inc(s["ones_made"], 1)
                pool.memset(pick[:], 0.0).then_inc(s["ones_made"], 1)
                pool.memset(spread[:], 0.0).then_inc(s["ones_made"], 1)
                pool.wait_ge(s["ones_made"], 3)
                for j in range(4):
                    pool.memset(pick[:, j].rearrange("p (a b) -> p a b", b=4)[:, :, j:j + 1], 1.0)
                for half in range(2):
                    pool.affine_select(out=spread[:, half], in_=spread[:, half], compare_op=ALU.not_equal, fill=1.0,
                                       base=-64 * half, pattern=[[-1, 4], [-32, 2], [0, DH]], channel_multiplier=1)\
                        .then_inc(s["ones_made"], 1)
                pool.memset(below[:], 0.0).then_inc(s["below_made"], 1)
                pool.wait_ge(s["below_made"], 1)
                pool.affine_select(out=below[:], in_=below[:], compare_op=ALU.is_ge, fill=BELOW, base=0,
                                   pattern=[[0, 4], [1, P]], channel_multiplier=-1).then_inc(s["below_made"], 1)

                pool.sem_inc(s["summed_odd"], 2)

                def split(n, par):
                    pool.wait_ge(s["q_scaled"], n + 1)
                    pool.tensor_tensor(q2[:, par, :, 1, :], qn[:], q2[:, par, :, 0, :], ALU.subtract).then_inc(s["q_split"], 1)

                for t in range(EARLY):
                    split(t, t % 2)

                def row(b, last):
                    when = splits(last)
                    for qt in range(NQ):
                        for k in range(2 * (qt + 1)):
                            h = qt * (qt + 1) + k
                            for tile, ahead in when.get(h, []):
                                split((b + ahead) * NQ + tile, tile % 2)
                            if k % 2 == 1:
                                pool.wait_ge(s["exped"], b * HALVES + h + 3)
                                add_up(pool, b, qt, h, "summed_odd")
                rows(pool, row)

            @block.scalar
            def _(act):
                act.sem_inc(s["exped"], 2)
                act.sem_inc(s["o_taken"], 1)

                def keys(b):
                    act.wait_ge(s["k_turned"], b + 1)
                    act.activation(kT[:].rearrange("p a c -> p (a c)"), pS[:, 0].rearrange("p a c -> p (a c)").bitcast(F16),
                                   ACT.Copy).then_inc(s["k_copied"], 1)

                def turned(b, uses, base, n):
                    kind, qt, ahead, c = uses[n]
                    act.wait_ge(s["px_made"], base + n + 1)
                    act.activation(qT[:, qt, HB * c:HB * c + HB, :].rearrange("p h q -> p (h q)"),
                                   pX[:, n % 2].bitcast(F16), ACT.Copy).then_inc(s["px_act"], 1)

                keys(0)
                for n, key in enumerate(first_uses):
                    if key[0] == "T":
                        turned(None, first_uses, 0, n)

                def take(b, last, qt):
                    act.wait_ge(s["pv_done"], b * HALVES + (qt + 1) * (qt + 2) + RING)
                    if qt > 0:
                        wait_taken(act, b, flat[last], flat[last].index(("B", qt - 1, 0, 1)))
                    else:
                        act.wait_ge(s["px_dve"], at_first["px_dve"] + b * per_row["px_dve"])
                    act.activation(oraw[:].rearrange("p a c -> p (a c)"), pO[:].rearrange("p a c -> p (a c)"), ACT.Copy)\
                       .then_inc(s["o_taken"], 1)

                def row(b, last):
                    n = 0
                    for h in range(HALVES):
                        act.wait_ge(s["s_made"], b * HALVES + h + 1)
                        act.wait_ge(s["pv_done"], b * HALVES + h + 1)
                        act.wait_ge(s["summed_odd" if h % 2 else "summed_even"], b * (HALVES // 2) + h // 2 + 1)
                        act.activation(pT[:, h % RING].rearrange("p a c -> p (a c)"),
                                       pS[:, h % 2].rearrange("p a c -> p (a c)"), ACT.Exp, scale=16.0 / UNIT ** 2)\
                           .then_inc(s["exped"], 1)
                        for key in plans[last][0][h]:
                            if key[0] == "T":
                                turned(b, flat[last], FIRST + b * USES, n)
                            n += 1
                        if h in [qt * (qt + 1) + LAG - 1 for qt in range(1, NQ)]:
                            take(b, last, [qt for qt in range(1, NQ) if h == qt * (qt + 1) + LAG - 1][0] - 1)
                    take(b, last, NQ - 1)
                    if not last:
                        keys(b + 1)
                rows(act, row)

            @block.vector
            def _(dve):
                dve.sem_inc(s["summed_even"], 2)
                dve.tensor_copy(identh[:], core.ident[:])
                dve.wait_ge(s["ones_made"], 1)
                dve.wait_ge(s["loaded"], 16 * 5)
                dve.tensor_scalar(Wkv[:], Wkv[:], gcol[:, 0:1], None, ALU.mult)
                dve.tensor_scalar(Wq[:], Wq[:], gcol[:, 0:1], None, ALU.mult).then_inc(s["folded"], 1)
                CH = (3 + 10 + 3) + NQ * (3 + 10 + 2)

                def norm_rows(row):
                    for k in range(BTILES):
                        t = bass.ds(row * BTILES + k, 1)
                        ins = dve.tensor_scalar(nrm[:, k, :], core.X[:, t, :], core.rstd2[:, t], core.shift2[:, t],
                                                ALU.mult, ALU.add)
                    ins.then_inc(s["normed"], 1)

                def side(uses, b, base, n, step):
                    kind, qt, ahead, c = uses[n]
                    if kind == "T":
                        return
                    dve.wait_ge(s["px_made"], base + n + 1)
                    if kind == "U":
                        dve.tensor_copy(uT[:, bass.ts(c, 512)], pX[:, n % 2]).then_inc(s["px_dve"], 1)
                    elif kind == "KV":
                        dve.tensor_copy(kv[:, 4 * c:4 * c + 4, :].rearrange("p t c -> p (t c)"), pX[:, n % 2]).then_inc(s["px_dve"], 1)
                        if c == 1:
                            wait_taken(dve, b, uses, n)
                            step(dve.tensor_tensor(ksq[:], kv[:, :, 0:DH], kv[:, :, 0:DH], ALU.mult))
                            step(dve.tensor_reduce(kss[:], ksq[:], AX.X, ALU.add))
                            step(dve.tensor_scalar(kss[:], kss[:], 1e-24, None, ALU.max))
                            newton_rsqrt(dve, step, krs[:], kss[:], ktmp[:])
                            step(dve.tensor_scalar(krs[:], krs[:], UNIT, None, ALU.mult))
                            step(dve.tensor_tensor(ksq[:], kv[:, :, 0:DH],
                                                   krs[:].rearrange("p (t o) -> p t o", o=1).to_broadcast([P, BTILES, DH]),
                                                   ALU.mult))
                            dve.tensor_copy(k2[:, :, 0, 0, :], ksq[:])
                            step(dve.tensor_copy(k2[:, :, 1, 1, :], ksq[:]))
                            dve.tensor_tensor(k2[:, :, 0, 1, :], ksq[:], k2[:, :, 0, 0, :], ALU.subtract)
                            dve.tensor_tensor(k2[:, :, 1, 0, :], ksq[:], k2[:, :, 1, 1, :], ALU.subtract)\
                               .then_inc(s["k_split"], 1)
                    elif kind == "Q":
                        dve.tensor_copy(qraw[:, qt % 2, HB * c:HB * c + HB, :].rearrange("p h d -> p (h d)"), pX[:, n % 2])\
                           .then_inc(s["px_dve"], 1)
                    elif kind == "S":
                        dve.reciprocal(over[:, qt % 2], pX[:, n % 2, 0:P]).then_inc(s["px_dve"], 1)
                    elif kind == "B":
                        dve.wait_ge(s["o_taken"], b * NQ + qt + 2)
                        dve.tensor_tensor(oT[:, c].rearrange("p j q -> p (j q)"), oraw[:, c], pX[:, n % 2], ALU.mult)\
                           .then_inc(s["px_dve"], 1)
                    else:
                        dve.tensor_copy(OUT[:, bass.ds(b * BTILES + qt, 1), :].rearrange("p t d -> p (t d)"),
                                        pX[:, n % 2, 0:D]).then_inc(s["px_dve"], 1)

                def scale(qt, row, part, step):
                    raw = qraw[:, qt % 2]
                    if part == 0:
                        step(dve.tensor_tensor(qsq[:], raw, raw, ALU.mult))
                        step(dve.tensor_reduce(qss[:], qsq[:], AX.X, ALU.add))
                    elif part == 1:
                        step(dve.tensor_scalar(qss[:], qss[:], 1e-24 / 256, None, ALU.max))
                        newton_rsqrt(dve, step, qrs[:], qss[:], qtmp[:])
                    else:
                        step(dve.tensor_scalar(qrs[:], qrs[:], UNIT, None, ALU.mult))
                        if not (qt == 0 and isinstance(row, int) and row == 0):
                            dve.wait_ge(s["q_split"], row * NQ + qt)
                        step(dve.tensor_tensor(qn[:], raw,
                                               qrs[:].rearrange("p (h o) -> p h o", o=1).to_broadcast([P, NH, DH]),
                                               ALU.mult))
                        dve.tensor_copy(q2[:, qt % 2, :, 0, :], qn[:]).then_inc(s["q_scaled"], 1)

                norm_rows(0)
                step = Chain(dve, s["chain"])
                for n, (kind, qt, ahead, c) in enumerate(first_uses):
                    side(first_uses, None, 0, n, step)
                    if kind == "Q" and c == 1:
                        wait_taken(dve, None, first_uses, n)
                        for part in range(3):
                            scale(qt, 0, part, step)
                BEFORE = step.n
                def row(b, last):
                    step = Chain(dve, s["chain"], BEFORE + b * CH)
                    dve.tensor_copy(V[:], kv[:, :, DH:2 * DH]).then_inc(s["v_copied"], 1)
                    if not last:
                        norm_rows(b + 1)
                    (slots, tail), when = plans[last], norms(last)
                    base, n, h = FIRST + b * USES, 0, 0
                    for qt in range(NQ):
                        for k in range(2 * (qt + 1)):
                            if k % 2 == 1:
                                sum_even(b, qt, h - 1)
                            for key in slots[h]:
                                side(flat[last], b, base, n, step)
                                n += 1
                            for tile, ahead, part in when.get(h, []):
                                if part == 0:
                                    wait_taken(dve, b, flat[last], flat[last].index(("Q", tile, ahead, 1)))
                                scale(tile, b + ahead, part, step)
                            h += 1
                    for key in tail:
                        side(flat[last], b, base, n, step)
                        n += 1
                    assert last or step.n == CH

                def sum_even(b, qt, h):
                    dve.wait_ge(s["exped"], b * HALVES + h + 3)
                    add_up(dve, b, qt, h, "summed_even")

                rows(dve, row)

            @block.tensor
            def _(pe):
                pe.sem_inc(s["pv_done"], RING)
                pe.wait_ge(s["folded"], 1)
                pe.wait_ge(s["ones_made"], 5)
                pe.wait_ge(s["below_made"], 2)

                def side(uses, b, base, n):
                    kind, qt, ahead, c = uses[n]
                    row = 0 if b is None else b + ahead
                    if n >= 2:
                        wait_taken(pe, b, uses, n - 2)
                    bank = pX[:, n % 2]
                    if kind == "U":
                        pe.wait_ge(s["normed"], row + 1)
                        for j in range(4):
                            ins = pe.transpose(bank[:, bass.ts(j, P)], nrm[:, 4 * c + j, :], core.ident[:])
                    elif kind == "KV":
                        for j in range(4):
                            ins = pe.matmul(bank[:, bass.ts(j, P)], uT[:, bass.ts(4 * c + j, P)], Wkv[:], start=True, stop=True)
                    elif kind == "Q":
                        wait_taken(pe, b, uses, uses.index(("U", 0, ahead, qt // 4))) if b is None or ahead else None
                        ins = pe.matmul(bank, uT[:, bass.ts(qt, P)], Wq[:, bass.ts(c, 512)], start=True, stop=True)
                    elif kind == "T":
                        pe.wait_ge(s["q_split"], row * NQ + qt + 1)
                        for j in range(HB):
                            place = j // 2 + 4 * (j % 2)
                            ins = pe.transpose(bank.bitcast(F16)[:, bass.ts(place, P)],
                                               q2[:, qt % 2, HB * c + j].rearrange("p c d -> p (c d)"), identh[:])
                    elif kind == "S":
                        for q in ("summed_even", "summed_odd"):
                            pe.wait_ge(s[q], b * (HALVES // 2) + (qt + 1) * (qt + 2) // 2 + 2)
                        for j in range(4):
                            for g in range(4):
                                ins = pe.matmul(bank[32 * g:32 * g + 32, 0:P], pick[:, j, :],
                                                sums[:, qt % 2, g // 2, g % 2, bass.ts(j, P)],
                                                start=(j == 0), stop=(j == 3), skip_group_check=True)
                    elif kind == "B":
                        wait_taken(pe, b, uses, uses.index(("S", qt, 0, 0)))
                        for j in range(4):
                            ins = pe.matmul(bank[:, bass.ts(j, P)], spread[:, c, j].rearrange("p a d -> p (a d)"),
                                            over[:, qt % 2, :], start=True, stop=True)
                    else:
                        wait_taken(pe, b, uses, n - 1)
                        for j in range(8):
                            ins = pe.matmul(bank[:, 0:D], oT[:, j // 4, j % 4, :], Wout[:, j, :], start=(j == 0), stop=(j == 7))
                    ins.then_inc(s["px_made"], 1)

                def turn_keys(row):
                    pe.wait_ge(s["k_split"], row + 1)
                    pe.wait_ge(s["exped"], row * HALVES + 2)
                    bank = pS[:, 0].rearrange("p a c -> p (a c)").bitcast(F16)
                    for v in range(2):
                        for k in range(BTILES):
                            ins = pe.transpose(bank[:, bass.ts(v * BTILES + k, P)], k2[:, k, v].rearrange("p c d -> p (c d)"),
                                               identh[:])
                    ins.then_inc(s["k_turned"], 1)

                for n, key in enumerate(first_uses):
                    if n == 6:
                        turn_keys(0)
                    side(first_uses, None, 0, n)

                def row(b, last):
                    def scores(qt, kt, half):
                        h = qt * (qt + 1) + 2 * kt + half
                        pe.wait_ge(s["exped"], b * HALVES + h + 1)
                        for v in range(2):
                            for c in range(2):
                                ins = pe.matmul(pS[:, half, c, :], kT[:, v, bass.ts(kt, P)],
                                                qT[:, qt, HB * half + 4 * c:HB * half + 4 * c + 4, :].rearrange("p h q -> p (h q)"),
                                                start=(v == 0), stop=(v == 1 and kt < qt))
                        if kt == qt:
                            for c in range(2):
                                ins = pe.matmul(pS[:, half, c, :], core.identb[:], below[:].rearrange("p a q -> p (a q)"),
                                                start=False, stop=True)
                        ins.then_inc(s["s_made"], 1)

                    def values(qt, kt, half):
                        h = qt * (qt + 1) + 2 * kt + half
                        if kt == 0 and half == 0:
                            pe.wait_ge(s["o_taken"], b * NQ + qt + 1)
                            if qt == 0:
                                pe.wait_ge(s["v_copied"], b + 1)
                        pe.wait_ge(s["exped"], b * HALVES + h + 3)
                        for par in range(2):
                            ins = pe.matmul(pO[64 * par:64 * par + 64, half, :], V[:, kt, :], pT[:, h % RING, par, :],
                                            start=(kt == 0), stop=(kt == qt), skip_group_check=True)
                        ins.then_inc(s["pv_done"], 1)

                    slots, tail = plans[last]
                    base, n, h, late = FIRST + b * USES, 0, 0, []
                    pe.wait_ge(s["k_copied"], b + 1)
                    for q in ("px_dve", "px_act"):
                        pe.wait_ge(s[q], at_first[q] + b * per_row[q])
                    for qt in range(NQ):
                        key = ("T", qt, 0, 1)
                        if qt >= EARLY:
                            wait_taken(pe, b, flat[last], flat[last].index(key))
                        for kt in range(qt + 1):
                            for half in range(2):
                                scores(qt, kt, half)
                                late.append((qt, kt, half))
                                if len(late) > LAG:
                                    values(*late.pop(0))
                                for key in slots[h]:
                                    side(flat[last], b, base, n)
                                    n += 1
                                h += 1
                    for args in late:
                        values(*args)
                    if not last:
                        turn_keys(b + 1)
                    for key in tail:
                        side(flat[last], b, base, n)
                        n += 1
                rows(pe, row)

        stream_stats(core, f"{name}_out", src=OUT)
        chain = sem("last_chain")
        with nc.Block() as block:
            @block.vector
            def _(dve):
                with dve.Fori(0, GROUPS) as g:
                    for j in range(GT):
                        t = bass.ds(g * GT + j, 1)
                        ins = dve.tensor_scalar(kv[:, j, :], OUT[:, t, :], core.rstd[:, t], core.shift[:, t], ALU.mult, ALU.add)
                    step = Chain(dve, chain, g * 3)
                    step(ins)
                    step(dve.tensor_tensor(kv[:, GT:2 * GT, :], kv[:, 0:GT, :],
                                           g2row[:].rearrange("p (o d) -> p o d", o=1).to_broadcast([P, GT, D]), ALU.mult))
                    ts = bass.ds(g * GT, GT)
                    step(dve.tensor_tensor(core.X[:, ts, :], core.X[:, ts, :], kv[:, GT:2 * GT, :], ALU.add))


def causal_single(core, name, qw, kw, vw):
    nc = core.nc
    NQ = BTILES
    SCALE = float(D) ** -0.5
    with ExitStack() as ctx:
        sb = lambda n, s, dt=F32: core.sb(f"{name}_{n}", s, dt, ctx)
        ps = lambda n, s: core.ps(f"{name}_{n}", s, F32, ctx)
        sem = lambda n: core.sem(f"{name}_{n}")
        Wq, Wk, Wv = sb("Wq", [D, D]), sb("Wk", [D, D]), sb("Wv", [D, D])
        hide = sb("hide", [P, P])
        nrm, uT, qT, kT, V = (sb(n, [P, SEQ]) for n in ("nrm", "uT", "qT", "kT", "V"))
        probs, pT = sb("probs", [P, 2, SEQ]), sb("pT", [P, SEQ])
        top, ntop, rowsum, inv = (sb(n, [P, NQ]) for n in ("top", "ntop", "rowsum", "inv"))
        pS, pT_, pO = ps("pS", [P, 2, SEQ]), ps("pTp", [P, SEQ]), ps("pO", [P, 2, 512])
        names = ("loaded hide_made normed turned u_copied q_made q_copied k_made k_copied v_made v_copied "
                 "s_made maxed scaled exped t_made t_copied o_made inverted added").split()
        s = dict(zip(names, map(sem, names)))
        with nc.Block() as block:
            @block.sync
            def _(sp):
                for t, a in ((Wq, qw), (Wk, kw), (Wv, vw)):
                    sp.dma_start(t[:], a).then_inc(s["loaded"], 16)

            @block.gpsimd
            def _(pool):
                pool.memset(hide[:], 0.0).then_inc(s["hide_made"], 1)
                pool.wait_ge(s["hide_made"], 1)
                pool.affine_select(out=hide[:], in_=hide[:], compare_op=ALU.is_ge, fill=-1e30, base=0,
                                   pattern=[[-1, P]], channel_multiplier=1).then_inc(s["hide_made"], 1)

            @block.vector
            def _(dve):
                dve.sem_inc(s["t_copied"], 1)
                dve.sem_inc(s["added"], 2)
                with dve.Fori(0, BATCH) as b:
                    for k in range(BTILES):
                        t = bass.ds(b * BTILES + k, 1)
                        ins = dve.tensor_scalar(nrm[:, bass.ts(k, D)], core.X[:, t, :].rearrange("p t d -> p (t d)"),
                                                core.rstd[:, t], core.shift[:, t], ALU.mult, ALU.add)
                    ins.then_inc(s["normed"], 1)
                    dve.wait_ge(s["k_made"], b + 1)
                    dve.tensor_copy(kT[:], pS[:, 1, :]).then_inc(s["k_copied"], 1)

                    def biggest(qt):
                        it = b * NQ + qt
                        dve.wait_ge(s["s_made"], it + 1)
                        dve.tensor_reduce(top[:, qt:qt + 1], pS[:, qt % 2, 0:P * (qt + 1)], AX.X, ALU.max)\
                           .then_inc(s["maxed"], 1)
                        dve.wait_ge(s["maxed"], it + 1)
                        dve.tensor_scalar(ntop[:, qt:qt + 1], top[:, qt:qt + 1], -SCALE, None, ALU.mult)\
                           .then_inc(s["scaled"], 1)

                    biggest(0)
                    for qt in range(NQ):
                        it = b * NQ + qt
                        if qt < NQ - 1:
                            biggest(qt + 1)
                        dve.wait_ge(s["t_made"], it + 3)
                        dve.wait_ge(s["o_made"], it + 1)
                        dve.tensor_copy(pT[:, 0:P * (qt + 1)], pT_[:, 0:P * (qt + 1)]).then_inc(s["t_copied"], 1)
                        dve.wait_ge(s["exped"], it + 3)
                        dve.reciprocal(inv[:, qt:qt + 1], rowsum[:, qt:qt + 1]).then_inc(s["inverted"], 1)
                        dve.wait_ge(s["inverted"], it + 1)
                        dve.wait_ge(s["o_made"], it + 2)
                        x = core.X[:, bass.ds(it, 1), :].rearrange("p t d -> p (t d)")
                        dve.scalar_tensor_tensor(out=x, in0=pO[:, qt % 2, 0:D], scalar=inv[:, qt:qt + 1], in1=x,
                                                 op0=ALU.mult, op1=ALU.add).then_inc(s["added"], 1)

            @block.scalar
            def _(act):
                act.sem_inc(s["exped"], 2)
                with act.Fori(0, BATCH) as b:
                    act.wait_ge(s["turned"], b + 1)
                    act.activation(uT[:], pS[:, 0, :], ACT.Copy).then_inc(s["u_copied"], 1)
                    act.wait_ge(s["q_made"], b + 1)
                    act.activation(qT[:], pS[:, 0, :], ACT.Copy).then_inc(s["q_copied"], 1)
                    act.wait_ge(s["v_made"], b + 1)
                    act.activation(V[:], pT_[:], ACT.Copy).then_inc(s["v_copied"], 1)
                    for qt in range(NQ):
                        it = b * NQ + qt
                        act.wait_ge(s["scaled"], it + 1)
                        act.wait_ge(s["t_made"], it + 1)
                        w = P * (qt + 1)
                        act.activation(probs[:, qt % 2, 0:w], pS[:, qt % 2, 0:w], ACT.Exp, bias=ntop[:, qt:qt + 1],
                                       scale=SCALE, accum_out=rowsum[:, qt:qt + 1]).then_inc(s["exped"], 1)

            @block.tensor
            def _(pe):
                pe.sem_inc(s["t_made"], 2)
                pe.sem_inc(s["o_made"], 1)
                pe.wait_ge(s["loaded"], 48)
                pe.wait_ge(s["hide_made"], 2)
                with pe.Fori(0, BATCH) as b:
                    halves = (slice(0, 512), slice(512, SEQ))
                    pe.wait_ge(s["normed"], b + 1)
                    pe.wait_ge(s["exped"], b * NQ + 2)
                    for k in range(BTILES):
                        ins = pe.transpose(pS[:, 0, bass.ts(k, P)], nrm[:, bass.ts(k, P)], core.ident[:])
                    ins.then_inc(s["turned"], 1)
                    pe.wait_ge(s["u_copied"], b + 1)
                    for h in halves:
                        ins = pe.matmul(pS[:, 0, h], Wq[:], uT[:, h], start=True, stop=True)
                    ins.then_inc(s["q_made"], 1)
                    for h in halves:
                        ins = pe.matmul(pS[:, 1, h], Wk[:], uT[:, h], start=True, stop=True)
                    ins.then_inc(s["k_made"], 1)
                    pe.wait_ge(s["t_copied"], b * NQ + 1)
                    for k in range(BTILES):
                        ins = pe.matmul(pT_[:, bass.ts(k, P)], uT[:, bass.ts(k, P)], Wv[:], start=True, stop=True)
                    ins.then_inc(s["v_made"], 1)
                    pe.wait_ge(s["q_copied"], b + 1)
                    pe.wait_ge(s["k_copied"], b + 1)

                    def scores(qt):
                        pe.wait_ge(s["exped"], b * NQ + qt + 1)
                        w = P * (qt + 1)
                        for c in range(0, w, 512):
                            n = min(512, w - c)
                            last = c + n == w
                            ins = pe.matmul(pS[:, qt % 2, c:c + n], qT[:, bass.ts(qt, P)], kT[:, c:c + n],
                                            start=True, stop=not last, skip_group_check=True)
                        pe.matmul(pS[:, qt % 2, w - P:w], core.ident[:], hide[:], start=False, stop=True,
                                  skip_group_check=True).then_inc(s["s_made"], 1)

                    scores(0)
                    for qt in range(NQ):
                        it = b * NQ + qt
                        if qt < NQ - 1:
                            scores(qt + 1)
                        pe.wait_ge(s["exped"], it + 3)
                        if qt == 0:
                            pe.wait_ge(s["v_copied"], b + 1)
                        pe.wait_ge(s["t_copied"], it + 1)
                        for k in range(qt + 1):
                            ins = pe.transpose(pT_[:, bass.ts(k, P)], probs[:, qt % 2, bass.ts(k, P)], core.ident[:])
                        ins.then_inc(s["t_made"], 1)
                        pe.wait_ge(s["t_copied"], it + 2)
                        pe.wait_ge(s["added"], it + 1)
                        for k in range(qt + 1):
                            ins = pe.matmul(pO[:, qt % 2, 0:D], pT[:, bass.ts(k, P)], V[:, bass.ts(k, D)],
                                            start=(k == 0), stop=(k == qt))
                        ins.then_inc(s["o_made"], 1)


class Experts:

    NE, TOP, FFN = 8, 2, 512
    CAP = 1280
    ROWS = NE * CAP
    HD, NKV = 8, 8
    QW = 256

    def __init__(self, core, w):
        nc = core.nc
        self.core = core
        names = ("ln1_weight", "ln1_bias", "ln2_weight", "ln2_bias", "router_weight", "moe_w1", "moe_w2")
        arrays = [w["moe_" + n if n[:4] != "moe_" else n] for n in names]
        self.ln1_weight, self.ln1_bias, self.ln2_weight, self.ln2_bias, self.router_weight, self.moe_w1, self.moe_w2 = arrays
        self.qkv_t = w["moe_qkv_t"]
        self.proj_t = w["moe_proj_t"]
        self.rows_in = nc.dram_tensor("rows_in", (self.ROWS + self.TOP * TOKENS, D), F32, kind="Internal").ap()
        self.rows_out = nc.dram_tensor("rows_out", (self.ROWS, D), F32, kind="Internal").ap()


def clear_rows(core, ex):
    NZ = 20
    with ExitStack() as ctx:
        zeros = core.sb("zeros", [P, NZ * D], F32, ctx)
        made, stored = core.sem("zeros_made"), core.sem("zeros_stored")
        with core.nc.Block() as block:
            @block.vector
            def _(dve):
                dve.memset(zeros[:], 0.0).then_inc(made, 1)

            @block.sync
            def _(sp):
                sp.wait_ge(made, 1)
                n = ex.ROWS // (P * NZ)
                for k in range(n):
                    sp.dma_start(ex.rows_in[k * P * NZ:(k + 1) * P * NZ, :].rearrange("(p t) d -> p (t d)", p=P), zeros[:])\
                      .then_inc(stored, 16)
                sp.wait_ge(stored, 16 * n)


def experts(core, name, ex):
    nc = core.nc
    NE, CAP, HD, NKV, QW = ex.NE, ex.CAP, ex.HD, ex.NKV, ex.QW
    sem = lambda n: core.sem(f"{name}_{n}")
    with ExitStack() as top:
        HA = core.sb(f"{name}_HA", [P, TILES, D], F32, top)
        gate = core.sb(f"{name}_gate", [P, 2, TILES], F32, top)
        slot_in = core.sb(f"{name}_slot_in", [P, 2, TILES], U32, top)
        slot_out = core.sb(f"{name}_slot_out", [P, 2, TILES], U32, top)
        row_attention(core, name, ex, HA)
        stream_stats(core, f"{name}_ha", src=HA)
        with ExitStack() as ctx:
            X2 = core.sb(f"{name}_X2", [P, TILES, D], F32, ctx)
            logits = core.sb(f"{name}_logits", [P, TILES, NE], F32, ctx)
            router(core, name, ex, HA, X2, logits)
            routing(core, name, ex, logits, gate, slot_in, slot_out)
            scattered = sem("scattered")
            with nc.Block() as block:
                @block.gpsimd
                def _(pool):
                    for t in range(TILES):
                        for c in range(2):
                            pool.indirect_dma_start(
                                out=ex.rows_in, out_offset=bass.IndirectOffsetOnAxis(ap=slot_in[:, c, t:t + 1], axis=0),
                                in_=X2[:, t, :], in_offset=None).then_inc(scattered, 16)
                    pool.wait_ge(scattered, 16 * 2 * TILES)
        expert_products(core, name, ex)
        with ExitStack() as ctx:
            G = core.sb(f"{name}_G", [P, 2, TILES, D], F32, ctx)
            gathered, chain = [sem(f"gathered{c}") for c in range(4)], sem("join_chain")
            with nc.Block() as block:
                @block.gpsimd
                def _(pool):
                    for t in range(TILES):
                        for c in range(2):
                            pool.indirect_dma_start(
                                out=G[:, c, t, :], out_offset=None, in_=ex.rows_out,
                                in_offset=bass.IndirectOffsetOnAxis(ap=slot_out[:, c, t:t + 1], axis=0))\
                                .then_inc(gathered[t // 8], 16)
                    for q in gathered:
                        pool.wait_ge(q, 16 * 16)

                @block.vector
                def _(dve):
                    step = Chain(dve, chain)
                    step(dve.tensor_tensor(core.X[:], core.X[:], HA[:], ALU.add))
                    for q in range(4):
                        dve.wait_ge(gathered[q], 16 * 16)
                        for c in range(2):
                            for t in range(8 * q, 8 * q + 8):
                                ins = dve.scalar_tensor_tensor(out=core.X[:, t, :], in0=G[:, c, t, :],
                                                               scalar=gate[:, c, t:t + 1], in1=core.X[:, t, :],
                                                               op0=ALU.mult, op1=ALU.add)
                            step(ins)


def row_attention(core, name, ex, HA):
    nc = core.nc
    HD, NKV, QW = ex.HD, ex.NKV, ex.QW
    with ExitStack() as ctx:
        sb = lambda n, s, dt=F32: core.sb(f"{name}_{n}", s, dt, ctx)
        ps = lambda n, s: core.ps(f"{name}_{n}", s, F32, ctx)
        sem = lambda n: core.sem(f"{name}_{n}")
        W, Wp = sb("Wqkv", [D, QW]), sb("Wproj", [D, D])
        wcol, bcol, bwide = sb("ln1w", [D, 1]), sb("ln1b", [D, 1]), sb("bwide", [D, P])
        bias = sb("qkvbias", [P, QW])
        QKV = sb("QKV", [P, TILES, QW])
        ATT = sb("ATT", [P, TILES, D])
        loaded, widened, bias_made, bias_kept, folded = map(sem, ("loaded", "widened", "bias_made", "bias_kept", "folded"))
        with ExitStack() as sub:
            nrm = core.sb(f"{name}_nrm", [P, 2, GT, D], F32, sub)
            uT = core.sb(f"{name}_uT", [P, 2, GT * P], F32, sub)
            pT = core.ps(f"{name}_pT", [P, 2, GT * P], F32, sub)
            pY = core.ps(f"{name}_pY", [P, 2, GT * QW], F32, sub)
            normed, turned, copied, product, kept = map(sem, ("q_normed", "q_turned", "q_copied", "q_product", "q_kept"))
            with nc.Block() as block:
                @block.sync
                def _(sp):
                    sp.dma_start(W[:], ex.qkv_t).then_inc(loaded, 16)
                    sp.dma_start(Wp[:], ex.proj_t).then_inc(loaded, 16)
                    sp.dma_start(wcol[:], ex.ln1_weight.rearrange("(d o) -> d o", o=1)).then_inc(loaded, 16)
                    sp.dma_start(bcol[:], ex.ln1_bias.rearrange("(d o) -> d o", o=1)).then_inc(loaded, 16)

                @block.vector
                def _(dve):
                    dve.sem_inc(kept, 2)
                    dve.wait_ge(loaded, 64)
                    dve.tensor_copy(bwide[:], bcol[:].to_broadcast([D, P])).then_inc(widened, 1)
                    dve.wait_ge(bias_made, 1)
                    dve.tensor_copy(bias[:], pY[:, 0, 0:QW]).then_inc(bias_kept, 1)
                    dve.wait_ge(bias_kept, 1)
                    dve.tensor_scalar(W[:], W[:], wcol[:, 0:1], None, ALU.mult).then_inc(folded, 1)

                    def norm(g, u):
                        dve.wait_ge(turned, g + 1)
                        for j in range(GT):
                            k = bass.ds(g * GT + j, 1)
                            ins = dve.tensor_scalar(nrm[:, u, j, :], core.X[:, k, :], core.rstd2[:, k], core.shift2[:, k],
                                                    ALU.mult, ALU.add)
                        ins.then_inc(normed, 1)

                    norm(0, 0)
                    norm(1, 1)

                    def body(g, u, last):
                        if follows(g, 2):
                            norm(g + 2, u)
                        dve.wait_ge(product, g + 3)
                        ts = bass.ds(g * GT, GT)
                        dve.tensor_tensor(QKV[:, ts, :], pY[:, u, :].rearrange("p (t c) -> p t c", c=QW),
                                          bias[:].rearrange("p (o c) -> p o c", o=1).to_broadcast([P, GT, QW]), ALU.add)\
                           .then_inc(kept, 1)
                    steps(dve, GROUPS, 2, 2, body)

                @block.tensor
                def _(pe):
                    pe.sem_inc(turned, 2)
                    pe.sem_inc(product, 2)
                    pe.wait_ge(widened, 1)
                    pe.matmul(pY[:, 0, 0:QW], bwide[:], W[:], start=True, stop=True).then_inc(bias_made, 1)
                    pe.wait_ge(folded, 1)

                    def turn(g, u):
                        pe.wait_ge(normed, g + 1)
                        pe.wait_ge(copied, g + 1)
                        for j in range(GT):
                            ins = pe.transpose(pT[:, u, bass.ts(j, P)], nrm[:, u, j, :], core.ident[:])
                        ins.then_inc(turned, 1)

                    turn(0, 0)

                    def body(g, u, last):
                        if not last:
                            turn(g + 1, 1 - u)
                        pe.wait_ge(copied, g + 3)
                        pe.wait_ge(kept, g + 1)
                        for j in range(GT):
                            ins = pe.matmul(pY[:, u, bass.ts(j, QW)], uT[:, u, bass.ts(j, P)], W[:], start=True, stop=True)
                        ins.then_inc(product, 1)
                    steps(pe, GROUPS, 2, 2, body)

                @block.scalar
                def _(act):
                    act.sem_inc(copied, 2)

                    def body(g, u, last):
                        act.wait_ge(turned, g + 3)
                        act.wait_ge(product, g + 1)
                        act.activation(uT[:, u, :], pT[:, u, :], ACT.Copy).then_inc(copied, 1)
                    steps(act, GROUPS, 2, 0, body)

        with ExitStack() as sub:
            XW = BATCH * NKV * HD
            prod = core.sb(f"{name}_prod", [P, 2, BATCH, 2, XW], F32, sub)
            vprod = core.sb(f"{name}_vprod", [P, 2, BATCH, 2, XW], F32, sub)
            sc = core.sb(f"{name}_sc", [P, 2, BATCH * 2, BATCH * NKV], F32, sub)
            ew = core.sb(f"{name}_ew", [P, 2, BATCH * 2, BATCH * NKV], F32, sub)
            mx, den = (core.sb(f"{name}_{n}", [P, 2, BATCH * 2, NKV], F32, sub) for n in ("mx", "den"))
            qv = QKV[:].rearrange("p (s j) (g c) -> p s j g c", s=BATCH, c=4 * HD)
            av = ATT[:].rearrange("p (s j) (g r d) -> p s j g r d", s=BATCH, r=2, d=HD)
            chain, multiplied, shifted, raised, weighted, spread = map(
                sem, ("a_chain", "a_multiplied", "a_shifted", "a_raised", "a_weighted", "a_spread"))
            with nc.Block() as block:
                @block.gpsimd
                def _(pool):
                    def multiply(j, u):
                        J = bass.ds(j, 1)
                        for s in range(BATCH):
                            for r in range(2):
                                n = s + 1
                                q = qv[:, s, J, :, r * HD:(r + 1) * HD].to_broadcast([P, n, NKV, HD])
                                k = qv[:, 0:n, J, :, 2 * HD:3 * HD].rearrange("p t j g d -> p (t j) g d")
                                out = prod[:, u, s, r, 0:n * NKV * HD].rearrange("p (t g d) -> p t g d", t=n, g=NKV)
                                ins = pool.tensor_tensor(out, q, k, ALU.mult)
                        ins.then_inc(multiplied, 1)

                    def weigh(j, u):
                        J = bass.ds(j, 1)
                        pool.wait_ge(weighted, j + 1)
                        for s in range(BATCH):
                            for r in range(2):
                                n = s + 1
                                w = ew[:, u, 2 * s + r, 0:n * NKV].rearrange("p (t g o) -> p t g o", g=NKV, o=1)\
                                    .to_broadcast([P, n, NKV, HD])
                                v = qv[:, 0:n, J, :, 3 * HD:4 * HD].rearrange("p t j g d -> p (t j) g d")
                                out = vprod[:, u, s, r, 0:n * NKV * HD].rearrange("p (t g d) -> p t g d", t=n, g=NKV)
                                ins = pool.tensor_tensor(out, w, v, ALU.mult)
                        ins.then_inc(spread, 1)

                    multiply(0, 0)
                    multiply(1, 1)
                    with pool.Fori(0, (BTILES - 2) // 2) as i:
                        for u in range(2):
                            weigh(2 * i + u, u)
                            multiply(2 * i + u + 2, u)
                    weigh(BTILES - 2, 0)
                    weigh(BTILES - 1, 1)

                @block.vector
                def _(dve):
                    dve.memset(sc[:], -1e30).then_inc(chain, 1)
                    dve.wait_ge(chain, 1)
                    v4 = lambda t: t.rearrange("p a (t g) -> p a t g", g=NKV)
                    wide = lambda t: t.rearrange("p a (o g) -> p a o g", o=1).to_broadcast([P, BATCH * 2, BATCH, NKV])

                    def scores(j, u, step):
                        dve.wait_ge(multiplied, j + 1)
                        for s in range(BATCH):
                            n = s + 1
                            view = prod[:, u, s, :, 0:n * NKV * HD].rearrange("p r (x d) -> p r x d", d=HD)
                            ins = dve.tensor_reduce(sc[:, u, 2 * s:2 * s + 2, 0:n * NKV], view, AX.X, ALU.add)
                        step(ins)
                        step(dve.tensor_reduce(mx[:, u], sc[:, u].rearrange("p a (t g) -> p a g t", g=NKV), AX.X, ALU.max))
                        dve.tensor_tensor(v4(ew[:, u]), v4(sc[:, u]), wide(mx[:, u]), ALU.subtract).then_inc(shifted, 1)

                    def weights(j, u, step):
                        dve.wait_ge(raised, j + 1)
                        step(dve.tensor_reduce(den[:, u], ew[:, u].rearrange("p a (t g) -> p a g t", g=NKV), AX.X, ALU.add))
                        step(dve.reciprocal(den[:, u], den[:, u]))
                        dve.tensor_tensor(v4(ew[:, u]), v4(ew[:, u]), wide(den[:, u]), ALU.mult).then_inc(weighted, 1)

                    def gathered(j, u):
                        J = bass.ds(j, 1)
                        dve.wait_ge(spread, j + 1)
                        for s in range(BATCH):
                            for r in range(2):
                                n = s + 1
                                view = vprod[:, u, s, r, 0:n * NKV * HD].rearrange("p (t g d) -> p g d t", t=n, g=NKV)
                                dve.tensor_reduce(av[:, s, J, :, r, :].rearrange("p j g d -> p (j g) d"), view, AX.X, ALU.add)

                    step = Chain(dve, chain, 1)
                    scores(0, 0, step)
                    weights(0, 0, step)
                    scores(1, 1, step)
                    with dve.Fori(0, (BTILES - 2) // 2) as i:
                        for u in range(2):
                            j = 2 * i + u
                            step = Chain(dve, chain, 1 + 6 + 4 * j)
                            weights(j + 1, 1 - u, step)
                            scores(j + 2, u, step)
                            gathered(j, u)
                    step = Chain(dve, chain, 1 + 6 + 4 * (BTILES - 2))
                    weights(BTILES - 1, 1, step)
                    gathered(BTILES - 2, 0)
                    gathered(BTILES - 1, 1)

                @block.scalar
                def _(act):
                    with act.Fori(0, BTILES // 2) as i:
                        for u in range(2):
                            act.wait_ge(shifted, 2 * i + u + 1)
                            act.activation(ew[:, u], ew[:, u], ACT.Exp, scale=HD ** -0.5).then_inc(raised, 1)

        with ExitStack() as sub:
            att = core.sb(f"{name}_att", [P, 2, GT, D], F32, sub)
            hid = core.sb(f"{name}_hid", [P, 2, GT, D], F32, sub)
            aT = core.sb(f"{name}_attT", [P, 2, GT * P], F32, sub)
            pT = core.ps(f"{name}_pT2", [P, 2, GT * P], F32, sub)
            pY = core.ps(f"{name}_pY2", [P, 2, GT * P], F32, sub)
            staged, turned, copied, product, kept, hidden = map(
                sem, ("p_staged", "p_turned", "p_copied", "p_product", "p_kept", "p_hidden"))
            with nc.Block() as block:
                @block.gpsimd
                def _(pool):
                    def body(g, u, last):
                        pool.wait_ge(turned, g + 1)
                        pool.tensor_copy(att[:, u], ATT[:, bass.ds(g * GT, GT), :]).then_inc(staged, 1)
                    steps(pool, GROUPS, 2, 0, body)

                @block.vector
                def _(dve):
                    dve.sem_inc(kept, 2)

                    def body(g, u, last):
                        dve.wait_ge(kept, g + 1)
                        normalise(dve, core, hid[:, u], g).then_inc(hidden, 1)
                        dve.wait_ge(hidden, g + 1)
                        dve.wait_ge(product, g + 3)
                        dve.tensor_tensor(HA[:, bass.ds(g * GT, GT), :], hid[:, u],
                                          pY[:, u, :].rearrange("p (t d) -> p t d", d=D), ALU.add).then_inc(kept, 1)
                    steps(dve, GROUPS, 2, 0, body)

                @block.tensor
                def _(pe):
                    pe.sem_inc(turned, 2)
                    pe.sem_inc(product, 2)

                    def turn(g, u):
                        pe.wait_ge(staged, g + 1)
                        pe.wait_ge(copied, g + 1)
                        for j in range(GT):
                            ins = pe.transpose(pT[:, u, bass.ts(j, P)], att[:, u, j, :], core.ident[:])
                        ins.then_inc(turned, 1)

                    turn(0, 0)

                    def body(g, u, last):
                        if not last:
                            turn(g + 1, 1 - u)
                        pe.wait_ge(copied, g + 3)
                        pe.wait_ge(kept, g + 1)
                        for j in range(GT):
                            ins = pe.matmul(pY[:, u, bass.ts(j, P)], aT[:, u, bass.ts(j, P)], Wp[:], start=True, stop=True)
                        ins.then_inc(product, 1)
                    steps(pe, GROUPS, 2, 2, body)

                @block.scalar
                def _(act):
                    act.sem_inc(copied, 2)

                    def body(g, u, last):
                        act.wait_ge(turned, g + 3)
                        act.wait_ge(product, g + 1)
                        act.activation(aT[:, u, :], pT[:, u, :], ACT.Copy).then_inc(copied, 1)
                    steps(act, GROUPS, 2, 0, body)


def router(core, name, ex, HA, X2, logits):
    nc, NE = core.nc, ex.NE
    with ExitStack() as ctx:
        wrow, brow = (core.sb(f"{name}_{n}", [P, D], F32, ctx) for n in ("ln2w", "ln2b"))
        R = core.sb(f"{name}_R", [D, NE], F32, ctx)
        nrm = core.sb(f"{name}_rnrm", [P, 2, GT, D], F32, ctx)
        xT = core.sb(f"{name}_rxT", [P, 2, GT * P], F32, ctx)
        pT = core.ps(f"{name}_rpT", [P, 2, GT * P], F32, ctx)
        pL = core.ps(f"{name}_rpL", [P, 2, 512], F32, ctx)
        loaded, turned, copied, product, chain, kept, made = map(
            lambda n: core.sem(f"{name}_{n}"), ("r_loaded", "r_turned", "r_copied", "r_product", "r_chain", "r_kept", "r_made"))
        wide = lambda t: t[:].rearrange("p (o d) -> p o d", o=1).to_broadcast([P, GT, D])
        with nc.Block() as block:
            @block.sync
            def _(sp):
                sp.dma_start(wrow[:], ex.ln2_weight.rearrange("(o d) -> o d", o=1).to_broadcast([P, D])).then_inc(loaded, 16)
                sp.dma_start(brow[:], ex.ln2_bias.rearrange("(o d) -> o d", o=1).to_broadcast([P, D])).then_inc(loaded, 16)
                sp.dma_start(R[:], ex.router_weight).then_inc(loaded, 16)

            @block.vector
            def _(dve):
                dve.sem_inc(kept, 2)
                dve.wait_ge(loaded, 48)

                def make(g, u):
                    step = Chain(dve, chain, g * 2)
                    dve.wait_ge(copied, g + 1)
                    for j in range(GT):
                        k = bass.ds(g * GT + j, 1)
                        ins = dve.tensor_scalar(nrm[:, u, j, :], HA[:, k, :], core.rstd[:, k], core.shift[:, k],
                                                ALU.mult, ALU.add)
                    step(ins)
                    step(dve.tensor_tensor(nrm[:, u], nrm[:, u], wide(wrow), ALU.mult))
                    dve.tensor_tensor(nrm[:, u], nrm[:, u], wide(brow), ALU.add).then_inc(made, 1)

                make(0, 0)
                make(1, 1)

                def body(g, u, last):
                    if follows(g, 2):
                        make(g + 2, u)
                    dve.wait_ge(product, g + 3)
                    dve.tensor_copy(logits[:, bass.ds(g * GT, GT), :],
                                    pL[:, u, 0:GT * NE].rearrange("p (t e) -> p t e", e=NE)).then_inc(kept, 1)
                steps(dve, GROUPS, 2, 2, body)

            @block.scalar
            def _(act):
                act.sem_inc(copied, 2)

                def body(g, u, last):
                    act.wait_ge(made, g + 1)
                    act.activation(X2[:, bass.ds(g * GT, GT), :], nrm[:, u], ACT.Copy)
                    act.wait_ge(turned, g + 3)
                    act.wait_ge(product, g + 1)
                    act.activation(xT[:, u, :], pT[:, u, :], ACT.Copy).then_inc(copied, 1)
                steps(act, GROUPS, 2, 0, body)

            @block.tensor
            def _(pe):
                pe.sem_inc(turned, 2)
                pe.sem_inc(product, 2)
                pe.wait_ge(loaded, 48)

                def turn(g, u):
                    pe.wait_ge(made, g + 1)
                    pe.wait_ge(copied, g + 1)
                    for j in range(GT):
                        ins = pe.transpose(pT[:, u, bass.ts(j, P)], nrm[:, u, j, :], core.ident[:])
                    ins.then_inc(turned, 1)

                turn(0, 0)

                def body(g, u, last):
                    if not last:
                        turn(g + 1, 1 - u)
                    pe.wait_ge(copied, g + 3)
                    pe.wait_ge(kept, g + 1)
                    for j in range(GT):
                        ins = pe.matmul(pL[:, u, bass.ts(j, NE)], xT[:, u, bass.ts(j, P)], R[:], start=True, stop=True)
                    ins.then_inc(product, 1)
                steps(pe, GROUPS, 2, 2, body)


def routing(core, name, ex, logits, gate, slot_in, slot_out):
    nc, NE, CAP = core.nc, ex.NE, ex.CAP
    TE = TILES * NE
    with ExitStack() as ctx:
        sb = lambda n, s, dt=F32: core.sb(f"{name}_{n}", s, dt, ctx)
        before, ones = sb("before", [P, P]), sb("ones", [P, P])
        e8i, tri = sb("e8i", [P, NE], I32), sb("tri", [P, 2, TILES], I32)
        e8, trash = sb("e8", [P, NE]), sb("trash", [P, 2, TILES])
        ebase = sb("ebase", [P, NE])
        big = [sb(f"big{k}", [P, TILES, NE]) for k in range(6)]
        p, hot1, hot2, sel, tmp, within = big
        tot, cum, one = sb("tot", [P, NE, TILES]), sb("cum", [P, NE, TILES]), sb("one", [P, TE])
        m = [sb(f"m{k}", [P, TILES]) for k in range(6)]
        m1, m2, idx, total, keep, slot = m
        pB, pA = (core.ps(f"{name}_{n}", [P, 512], F32, ctx) for n in ("pB", "pA"))
        consts, chain, shifted, raised, chosen, counted = map(
            lambda n: core.sem(f"{name}_{n}"), ("g_consts", "g_chain", "g_shifted", "g_raised", "g_chosen", "g_counted"))
        col = lambda t: t[:].rearrange("p (t o) -> p t o", o=1).to_broadcast([P, TILES, NE])
        erow = lambda t: t[:].rearrange("p (o e) -> p o e", o=1).to_broadcast([P, TILES, NE])
        with nc.Block() as block:
            @block.gpsimd
            def _(pool):
                pool.memset(ones[:], 1.0).then_inc(consts, 1)
                pool.memset(before[:], 1.0).then_inc(consts, 1)
                pool.wait_ge(consts, 2)
                pool.affine_select(out=before[:], in_=before[:], compare_op=ALU.is_gt, fill=0.0, base=0,
                                   pattern=[[1, P]], channel_multiplier=-1).then_inc(consts, 1)
                pool.iota(e8i[:], [[1, NE]], base=0, channel_multiplier=0).then_inc(consts, 1)
                pool.iota(tri[:], [[1, 2], [2 * P, TILES]], base=ex.ROWS, channel_multiplier=2).then_inc(consts, 1)

            @block.scalar
            def _(act):
                act.wait_ge(shifted, 1)
                act.activation(p[:], p[:], ACT.Exp).then_inc(raised, 1)

            @block.tensor
            def _(pe):
                pe.wait_ge(chosen, 1)
                pe.matmul(pB[:, 0:TE], before[:], sel[:].rearrange("p t e -> p (t e)"), start=True, stop=True)
                pe.matmul(pA[:, 0:TE], ones[:], sel[:].rearrange("p t e -> p (t e)"), start=True, stop=True)\
                  .then_inc(counted, 1)

            @block.vector
            def _(dve):
                step = Chain(dve, chain)
                dve.wait_ge(consts, 5)
                step(dve.tensor_copy(e8[:], e8i[:]))
                step(dve.tensor_copy(trash[:], tri[:]))
                step(dve.tensor_scalar(ebase[:], e8[:], float(CAP), None, ALU.mult))
                step(dve.tensor_scalar(e8[:], e8[:], float(NE), None, ALU.subtract))
                step(dve.memset(one[:], 1.0))
                step(dve.tensor_reduce(m1[:], logits[:], AX.X, ALU.max))
                dve.tensor_tensor(p[:], logits[:], col(m1), ALU.subtract).then_inc(shifted, 1)
                dve.wait_ge(raised, 1)
                for best, hot in ((m1, hot1), (m2, hot2)):
                    step(dve.tensor_reduce(best[:], p[:], AX.X, ALU.max))
                    step(dve.tensor_tensor(tmp[:], p[:], col(best), ALU.is_equal))
                    step(dve.tensor_tensor(tmp[:], tmp[:], erow(e8), ALU.mult))
                    step(dve.tensor_reduce(idx[:], tmp[:], AX.X, ALU.min))
                    step(dve.tensor_tensor(hot[:], erow(e8), col(idx), ALU.is_equal))
                    if hot is hot1:
                        step(dve.scalar_tensor_tensor(out=p[:].rearrange("p t e -> p (t e)"),
                                                      in0=hot[:].rearrange("p t e -> p (t e)"), scalar=-2.0,
                                                      in1=p[:].rearrange("p t e -> p (t e)"), op0=ALU.mult, op1=ALU.add))
                dve.tensor_tensor(sel[:], hot1[:], hot2[:], ALU.add).then_inc(chosen, 1)
                step(dve.tensor_tensor(total[:], m1[:], m2[:], ALU.add))
                step(dve.reciprocal(total[:], total[:]))
                dve.tensor_tensor(gate[:, 0, :], m1[:], total[:], ALU.mult)
                step(dve.tensor_tensor(gate[:, 1, :], m2[:], total[:], ALU.mult))
                dve.wait_ge(counted, 1)
                step(dve.tensor_copy(tot[:].rearrange("p e t -> p t e"), pA[:, 0:TE].rearrange("p (t e) -> p t e", e=NE)))
                step(dve.tensor_tensor_scan(cum[:].rearrange("p e t -> p (e t)"), one[:],
                                            tot[:].rearrange("p e t -> p (e t)"), 0.0, ALU.mult, ALU.add))
                step(dve.tensor_tensor(cum[:], cum[:], tot[:], ALU.subtract))
                step(dve.tensor_tensor(tot[:], cum[:], cum[:, :, 0:1].to_broadcast([P, NE, TILES]), ALU.subtract))
                step(dve.tensor_tensor(within[:], tot[:].rearrange("p e t -> p t e"),
                                       pB[:, 0:TE].rearrange("p (t e) -> p t e", e=NE), ALU.add))
                step(dve.tensor_scalar(sel[:], within[:], float(CAP), None, ALU.is_lt))
                step(dve.tensor_tensor(within[:], within[:], erow(ebase), ALU.add))
                for c, hot in ((0, hot1), (1, hot2)):
                    step(dve.tensor_tensor(tmp[:], hot[:], sel[:], ALU.mult))
                    step(dve.tensor_reduce(keep[:], tmp[:], AX.X, ALU.add))
                    step(dve.tensor_tensor(tmp[:], tmp[:], within[:], ALU.mult))
                    step(dve.tensor_reduce(slot[:], tmp[:], AX.X, ALU.add))
                    step(dve.tensor_tensor(gate[:, c, :], gate[:, c, :], keep[:], ALU.mult))
                    step(dve.tensor_copy(slot_out[:, c, :], slot[:]))
                    step(dve.tensor_scalar(keep[:], keep[:], -1.0, 1.0, ALU.mult, ALU.add))
                    step(dve.tensor_tensor(keep[:], keep[:], trash[:, c, :], ALU.mult))
                    step(dve.tensor_tensor(slot[:], slot[:], keep[:], ALU.add))
                    step(dve.tensor_copy(slot_in[:, c, :], slot[:]))


def expert_products(core, name, ex):
    nc, NE, CAP, FFN = core.nc, ex.NE, ex.CAP, ex.FFN
    CT, FC = CAP // P, FFN // P
    CH = ((0, 4), (4, 4), (8, 2))
    with ExitStack() as ctx:
        sb = lambda n, s, dt=F32: core.sb(f"{name}_{n}", s, dt, ctx)
        W1, W2 = sb("W1", [P, 2, FFN]), sb("W2", [P, 2, FC, D])
        rows, xT = sb("rows", [P, 2, CT, D]), sb("xT", [P, CAP])
        hT, y = sb("hT", [P, FC, CAP]), sb("y", [P, 2, CT, D])
        pT = core.ps(f"{name}_epT", [P, 2, 512], F32, ctx)
        pH = core.ps(f"{name}_epH", [P, 4, 512], F32, ctx)
        pO = core.ps(f"{name}_epO", [P, 2, 512], F32, ctx)
        s = {n: core.sem(f"{name}_e_{n}") for n in
             "loaded0 loaded1 turned x_copied h_made raised o_made o_copied stored0 stored1 y_free".split()}
        with nc.Block() as block:
            @block.sync
            def _(sp):
                with sp.Fori(0, NE // 2) as i:
                    for u in range(2):
                        e = 2 * i + u
                        sp.wait_ge(s["o_made"], e * 3 + 3)
                        sp.dma_start(rows[:, u], ex.rows_in[bass.ds(e * CAP, CAP), :].rearrange("(t p) d -> p t d", p=P))\
                          .then_inc(s[f"loaded{u}"], 16)
                        sp.dma_start(W1[:, u], ex.moe_w1[bass.ds(e, 1)].rearrange("e p f -> (e p) f"))\
                          .then_inc(s[f"loaded{u}"], 16)
                        sp.dma_start(W2[:, u], ex.moe_w2[bass.ds(e, 1)].rearrange("e (c p) n -> (e p) c n", p=P))\
                          .then_inc(s[f"loaded{u}"], 16)

            @block.gpsimd
            def _(pool):
                pool.sem_inc(s["y_free"], 2)
                with pool.Fori(0, NE // 2) as i:
                    for u in range(2):
                        e = 2 * i + u
                        pool.wait_ge(s["o_copied"], e * 3 + 3 + 2)
                        pool.dma_start(ex.rows_out[bass.ds(e * CAP, CAP), :].rearrange("(t p) d -> p t d", p=P), y[:, u])\
                            .then_inc(s[f"stored{u}"], 16)
                        pool.wait_ge(s[f"stored{u}"], i * 16 + 16)
                        pool.sem_inc(s["y_free"], 1)

            @block.tensor
            def _(pe):
                pe.sem_inc(s["o_made"], 6)
                pe.sem_inc(s["h_made"], 12)
                with pe.Fori(0, NE // 2) as i:
                    for u in range(2):
                        e = 2 * i + u
                        pe.wait_ge(s[f"loaded{u}"], i * 48 + 48)
                        for c, (t0, n) in enumerate(CH):
                            slot = (c + u) % 2
                            pe.wait_ge(s["x_copied"], e * 3 + c + 1)
                            for j in range(n):
                                ins = pe.transpose(pT[:, slot, bass.ts(j, P)], rows[:, u, t0 + j, :], core.ident[:])
                            ins.then_inc(s["turned"], 1)
                        for c, (t0, n) in enumerate(CH):
                            pe.wait_ge(s["x_copied"], e * 3 + c + 3)
                            for f in range(FC):
                                pe.wait_ge(s["raised"], e * 12 + 4 * c + f + 1)
                                pe.matmul(pH[:, f, 0:n * P], W1[:, u, bass.ts(f, P)], xT[:, t0 * P:(t0 + n) * P],
                                          start=True, stop=True).then_inc(s["h_made"], 1)
                        for c, (t0, n) in enumerate(CH):
                            slot = (c + u) % 2
                            pe.wait_ge(s["raised"], e * 12 + 4 * c + 4 + 4)
                            pe.wait_ge(s["o_copied"], e * 3 + c + 1)
                            for j in range(n):
                                for f in range(FC):
                                    ins = pe.matmul(pO[:, slot, bass.ts(j, D)], hT[:, f, bass.ts(t0 + j, P)], W2[:, u, f, :],
                                                    start=(f == 0), stop=(f == FC - 1))
                            ins.then_inc(s["o_made"], 1)

            @block.scalar
            def _(act):
                act.sem_inc(s["raised"], 4)
                with act.Fori(0, NE // 2) as i:
                    for u in range(2):
                        e = 2 * i + u
                        for c, (t0, n) in enumerate(CH):
                            act.wait_ge(s["o_made"], e * 3 + c + 1 + 3)
                            for f in range(FC):
                                act.wait_ge(s["h_made"], e * 12 + 4 * c + f + 1 + 12)
                                act.activation(hT[:, f, t0 * P:(t0 + n) * P], pH[:, f, 0:n * P], ACT.Gelu)\
                                   .then_inc(s["raised"], 1)

            @block.vector
            def _(dve):
                dve.sem_inc(s["x_copied"], 2)
                dve.sem_inc(s["o_copied"], 2)
                with dve.Fori(0, NE // 2) as i:
                    for u in range(2):
                        e = 2 * i + u
                        for c, (t0, n) in enumerate(CH):
                            dve.wait_ge(s["turned"], e * 3 + c + 1)
                            dve.wait_ge(s["h_made"], e * 12 + 4 * c + 4)
                            dve.tensor_copy(xT[:, t0 * P:(t0 + n) * P], pT[:, (c + u) % 2, 0:n * P])\
                               .then_inc(s["x_copied"], 1)
                        for c, (t0, n) in enumerate(CH):
                            dve.wait_ge(s["o_made"], e * 3 + c + 1 + 6)
                            if c == 0:
                                dve.wait_ge(s["y_free"], e + 1)
                            dve.tensor_copy(y[:, u, t0:t0 + n, :].rearrange("p t d -> p (t d)"),
                                            pO[:, (c + u) % 2, 0:n * P]).then_inc(s["o_copied"], 1)


def full_attention(core, name, wqkv_t, bqkv, wo_t, bo, wq, wk):
    nc = core.nc
    NH, DH, SL, NP_ = 16, 8, 64, 8
    NQ = BTILES
    C3 = 3 * D
    AHEAD = 4
    QSLOT = {"h": ((0, 2, 8), (3, 1, 8)), "m": ((2, 1, 8), (5, 1, 8)), "l": 4}
    KSLOT = {"h": ((0, 3, 16),), "m": ((1, 1, 8), (5, 1, 8)), "l": 3}
    with ExitStack() as ctx:
        sb = lambda n, s, dt=F32: core.sb(f"{name}_{n}", s, dt, ctx)
        ps = lambda n, s: core.ps(f"{name}_{n}", s, F32, ctx)
        W, Wo = sb("W", [D, C3]), sb("Wo", [D, D])
        bias, brow = sb("bias", [P, C3]), sb("brow", [P, D])
        wqr, wkr, wqk = sb("wqr", [P, DH]), sb("wkr", [P, DH]), sb("wqk", [P, NH, DH])
        nrm, uT = sb("nrm", [P, BTILES, D]), sb("uT", [P, SEQ])
        qkv = sb("qkv", [P, BTILES, C3])
        sq = sb("sq", [P, BTILES, 2 * D])
        ss, rs, rt = (sb(n, [P, BTILES * 2 * NH]) for n in ("ss", "rs", "rt"))
        Q6, K6 = sb("Q6", [P, BTILES, NH, SL], BF16), sb("K6", [P, BTILES, NH, SL], BF16)
        QT, KZ = sb("QT", [P, NP_, SEQ], BF16), sb("KZ", [P, 2, NP_, SEQ], BF16)
        QM = sb("QM", [P, 2, SEQ], BF16)
        PT = sb("PT", [P, 4, SEQ])
        V1 = sb("V1", [P, BTILES, NH, DH + 1])
        mxh, mx, mr = sb("mxh", [P, 2, NQ, 2, 2]), sb("mx", [P, NQ, 2]), sb("mr", [P, NQ, 2])
        OT, osum = sb("OT", [P, 512]), sb("osum", [P, 16])
        Z, ZT = sb("Z", [P, BTILES, NH, DH]), sb("ZT", [P, BTILES, P])
        p2, p1 = ps("p2", [P, 4, 512]), ps("p1", [P, 2, 512])
        pT, pO = ps("pT", [P, 512]), ps("pO", [P, 512])
        names = ("loaded wqk_made ones_made normed turned u_copied qkv_made qkv_kept normed_qk "
                 "h_cast r_made m_cast l_made kq_turned k_used q_used s1_made s1_used m_made t_made t_used "
                 "s2_made exped pv_done o_used ot_copied z_made chain").split()
        s = {n: core.sem(f"{name}_{n}") for n in names}
        torder = [("QM", 0)]
        for pr in range(NP_):
            if pr > 0:
                torder.append(("O", pr - 1))
            if pr < NP_ - 1:
                torder.append(("QM", pr + 1))
        torder += [("O", NP_ - 1), ("Z", 0), ("Z", 1), ("Y", 0), ("Y", 1)]
        at = {key: n for n, key in enumerate(torder)}
        NT = len(torder)
        q6v = Q6[:].rearrange("p t h c -> p (t h) c")
        k6v = K6[:].rearrange("p t h c -> p (t h) c")
        pTb = pT[:].bitcast(BF16)

        with nc.Block() as block:
            @block.sync
            def _(sp):
                row = lambda a, n: a.rearrange("(o c) -> o c", o=1).to_broadcast([P, n])
                for t, a in ((W[:], wqkv_t), (Wo[:], wo_t), (bias[:], row(bqkv, C3)), (brow[:], row(bo, D)),
                             (wqr[:], row(wq, DH)), (wkr[:], row(wk, DH))):
                    sp.dma_start(t, a).then_inc(s["loaded"], 16)

            @block.gpsimd
            def _(pool):
                for t in (Q6, K6, KZ):
                    pool.memset(t[:], 0.0).then_inc(s["ones_made"], 1)
                pool.memset(V1[:], 1.0).then_inc(s["ones_made"], 1)
                pool.wait_ge(s["ones_made"], 4)
                pool.memset(k6v[:, :, 48:51], 1.0).then_inc(s["ones_made"], 1)

            @block.scalar
            def _(act):
                act.sem_inc(s["exped"], 2)
                act.sem_inc(s["o_used"], 1)
                act.wait_ge(s["ones_made"], 5)
                with act.Fori(0, BATCH) as b:
                    act.wait_ge(s["turned"], b + 1)
                    act.activation(uT[:], p2[:, 0:2, :].rearrange("p a c -> p (a c)"), ACT.Copy).then_inc(s["u_copied"], 1)
                    for w, (v, slots) in enumerate(((q6v, QSLOT), (k6v, KSLOT))):
                        src = qkv[:, :, w * D:(w + 1) * D].rearrange("p t (h d) -> p t h d", d=DH)
                        act.wait_ge(s["normed_qk"], b * 2 + w + 1)
                        for s0, n, st in slots["h"]:
                            for k in range(n):
                                c = s0 * DH + k * st
                                ins = act.activation(v[:, :, c:c + DH].rearrange("p (t h) d -> p t h d", t=BTILES), src, ACT.Copy)
                        ins.then_inc(s["h_cast"], 1)
                    for w, (v, slots) in enumerate(((q6v, QSLOT), (k6v, KSLOT))):
                        r1 = sq[:, :, w * D:(w + 1) * D].rearrange("p t (h d) -> p t h d", d=DH)
                        act.wait_ge(s["r_made"], b * 2 + w + 1)
                        for s0, n, st in slots["m"]:
                            c = s0 * DH
                            ins = act.activation(v[:, :, c:c + DH].rearrange("p (t h) d -> p t h d", t=BTILES), r1, ACT.Copy)
                        ins.then_inc(s["m_cast"], 1)
                    for pr in range(NP_):
                        act.wait_ge(s["kq_turned"], b * 16 + 2 * pr + 2)
                        act.activation(QT[:, pr, :], p2[:, (2 * pr + 1) % 4, :].bitcast(BF16), ACT.Copy)\
                           .then_inc(s["q_used"], 1)

                    def take_queries(pr):
                        act.wait_ge(s["t_made"], b * NT + at[("QM", pr)] + 1)
                        act.activation(QM[:, pr % 2, :], pTb, ACT.Copy).then_inc(s["t_used"], 1)

                    take_queries(0)
                    for pr in range(NP_):
                        for j in range(2 * NQ):
                            k2 = b * 16 * NP_ + 16 * pr + j
                            act.wait_ge(s["s2_made"], k2 + 1)
                            act.wait_ge(s["pv_done"], k2 + 1)
                            act.activation(PT[:, j % 4, :], p2[:, 2 * (j % 2):2 * (j % 2) + 2, :].rearrange("p a c -> p (a c)"),
                                           ACT.Exp).then_inc(s["exped"], 1)
                        if pr < NP_ - 1:
                            take_queries(pr + 1)
                        act.wait_ge(s["pv_done"], b * 16 * NP_ + 16 * (pr + 1) + 4)
                        if pr > 0:
                            act.wait_ge(s["t_made"], b * NT + at[("O", pr - 1)] + 1)
                        act.activation(OT[:], pO[:], ACT.Copy).then_inc(s["o_used"], 1)

            @block.vector
            def _(dve):
                dve.sem_inc(s["s1_used"], 2)
                dve.sem_inc(s["t_used"], 1)
                dve.wait_ge(s["loaded"], 16 * 6)
                dve.wait_ge(s["ones_made"], 5)
                dve.memset(pO[:], 0.0).then_inc(s["wqk_made"], 1)
                dve.wait_ge(s["wqk_made"], 1)
                dve.tensor_tensor(wqr[:], wqr[:], wkr[:], ALU.mult).then_inc(s["wqk_made"], 1)
                dve.wait_ge(s["wqk_made"], 2)
                dve.tensor_copy(wqk[:], wqr[:].rearrange("p (o d) -> p o d", o=1).to_broadcast([P, NH, DH]))\
                   .then_inc(s["wqk_made"], 1)
                dve.wait_ge(s["wqk_made"], 3)
                CH = 3 + 10 + 1 + 5 * NP_ + NP_
                with dve.Fori(0, BATCH) as b:
                    step = Chain(dve, s["chain"], b * CH)
                    for k in range(BTILES):
                        t = bass.ds(b * BTILES + k, 1)
                        ins = dve.tensor_scalar(nrm[:, k, :], core.X[:, t, :].rearrange("p t d -> p (t d)"),
                                                core.rstd[:, t], core.shift[:, t], ALU.mult, ALU.add)
                    ins.then_inc(s["normed"], 1)
                    for half in range(2):
                        dve.wait_ge(s["qkv_made"], b * 2 + half + 1)
                        dve.tensor_tensor(qkv[:, 4 * half:4 * half + 4, :], p2[:, :, 0:C3],
                                          bias[:].rearrange("p (o c) -> p o c", o=1).to_broadcast([P, 4, C3]),
                                          ALU.add).then_inc(s["qkv_kept"], 1)
                    dve.wait_ge(s["qkv_kept"], b * 2 + 2)
                    dve.tensor_copy(V1[:, :, :, 0:DH], qkv[:, :, 2 * D:C3].rearrange("p t (h d) -> p t h d", d=DH))
                    step(dve.tensor_tensor(sq[:], qkv[:, :, 0:2 * D], qkv[:, :, 0:2 * D], ALU.mult))
                    step(dve.tensor_reduce(ss[:].rearrange("p (t h) -> p t h", t=BTILES),
                                           sq[:].rearrange("p t (h d) -> p t h d", d=DH), AX.X, ALU.add))
                    step(dve.tensor_scalar(ss[:], ss[:], 1.0 / DH, 1e-6, ALU.mult, ALU.add))
                    newton_rsqrt(dve, step, rs[:], ss[:], rt[:])
                    for w in range(2):
                        src = qkv[:, :, w * D:(w + 1) * D].rearrange("p t (h d) -> p t h d", d=DH)
                        r = rs[:].rearrange("p (t w h o) -> p t w h o", t=BTILES, w=2, o=1)[:, :, w]\
                            .to_broadcast([P, BTILES, NH, DH])
                        ins = dve.tensor_tensor(src, src, r, ALU.mult)
                        if w == 0:
                            ins.then_inc(s["normed_qk"], 1)
                    step(ins)
                    flat = qkv[:, :, D:2 * D]
                    dve.tensor_tensor(flat, flat, wqk[:].rearrange("p (o h) d -> p o (h d)", o=1).to_broadcast([P, BTILES, D]),
                                      ALU.mult).then_inc(s["normed_qk"], 1)
                    dve.wait_ge(s["normed_qk"], b * 2 + 2)
                    for w, v in enumerate((q6v, k6v)):
                        dve.wait_ge(s["h_cast"], b * 2 + w + 1)
                        src = qkv[:, :, w * D:(w + 1) * D].rearrange("p t (h d) -> p t h d", d=DH)
                        r1 = sq[:, :, w * D:(w + 1) * D].rearrange("p t (h d) -> p t h d", d=DH)
                        dve.tensor_tensor(r1, src, v[:, :, 0:DH].rearrange("p (t h) d -> p t h d", t=BTILES),
                                          ALU.subtract).then_inc(s["r_made"], 1)
                    for w, (v, slots) in enumerate(((q6v, QSLOT), (k6v, KSLOT))):
                        dve.wait_ge(s["m_cast"], b * 2 + w + 1)
                        r1 = sq[:, :, w * D:(w + 1) * D].rearrange("p t (h d) -> p t h d", d=DH)
                        c, m = slots["l"] * DH, slots["m"][0][0] * DH
                        dve.tensor_tensor(v[:, :, c:c + DH].rearrange("p (t h) d -> p t h d", t=BTILES), r1,
                                          v[:, :, m:m + DH].rearrange("p (t h) d -> p t h d", t=BTILES),
                                          ALU.subtract).then_inc(s["l_made"], 1)
                    for pr in range(NP_):
                        dve.wait_ge(s["kq_turned"], b * 16 + 2 * pr + 1)
                        bank = p2[:, (2 * pr) % 4, :].bitcast(BF16)
                        for par in range(2):
                            rows = slice(64 * par, 64 * par + 64)
                            ins = dve.tensor_copy(KZ[rows, par, pr, :], bank[rows, :])
                        ins.then_inc(s["k_used"], 1)

                    def maxima(g):
                        pr, j = g // 16, g % 16
                        for half in range(2):
                            k1 = b * 32 * NP_ + 2 * g + half
                            dve.wait_ge(s["s1_made"], k1 + 1)
                            dve.tensor_reduce(mxh[:, pr % 2, j // 2, j % 2, half:half + 1], p1[:, half, :], AX.X, ALU.max)\
                               .then_inc(s["s1_used"], 1)
                        if j == 15:
                            dve.wait_ge(s["s1_used"], b * 32 * NP_ + 2 * g + 2 + 2)
                            mh = mxh[:, pr % 2]
                            slot = lambda c: Q6[:, :, 2 * pr:2 * pr + 2, 48 + c:49 + c].rearrange("p t h o -> p t (h o)")
                            step(dve.tensor_reduce(mx[:], mh, AX.X, ALU.max, negate=True))
                            step(dve.tensor_copy(slot(0), mx[:]))
                            step(dve.tensor_tensor(mr[:], mx[:], slot(0), ALU.subtract))
                            step(dve.tensor_copy(slot(1), mr[:]))
                            step(dve.tensor_tensor(slot(2), mr[:], slot(1), ALU.subtract))
                            dve.sem_inc(s["m_made"], 1)

                    def outputs(pr):
                        dve.wait_ge(s["t_made"], b * NT + at[("O", pr)] + 1)
                        view = pT[:].rearrange("p (q c d) -> p q c d", q=4, c=4)
                        step(dve.reciprocal(osum[:].rearrange("p (q c o) -> p q c o", q=4, o=1), view[:, :, :, DH:DH + 1]))
                        r = osum[:].rearrange("p (q a h o) -> p h q a o", q=4, a=2, o=1)
                        v = pT[:].rearrange("p (q a h d) -> p h q a d", q=4, a=2, h=2)
                        for half in range(2):
                            ins = dve.tensor_tensor(Z[:, 4 * half:4 * half + 4, 2 * pr:2 * pr + 2, :], v[:, half, :, :, 0:DH],
                                                    r[:, half].to_broadcast([P, 4, 2, DH]), ALU.mult)
                        ins.then_inc(s["t_used"], 1)

                    for g in range(16 + AHEAD):
                        maxima(g)
                    for pr in range(NP_):
                        for j in range(2 * NQ):
                            g = 16 * (pr + 1) + j + AHEAD
                            if g < 16 * NP_:
                                maxima(g)
                            if j == 3 and pr > 0:
                                outputs(pr - 1)
                    outputs(NP_ - 1)
                    for half in range(2):
                        dve.wait_ge(s["t_made"], b * NT + at[("Z", half)] + 1)
                        dve.tensor_copy(ZT[:, 4 * half:4 * half + 4, :].rearrange("p t q -> p (t q)"), pT[:])\
                           .then_inc(s["t_used"], 1)
                    xs = core.X[:, bass.ds(b * BTILES, BTILES), :]
                    step2 = s["z_made"]
                    dve.tensor_tensor(xs, xs, brow[:].rearrange("p (o d) -> p o d", o=1).to_broadcast([P, BTILES, D]),
                                      ALU.add).then_inc(step2, 1)
                    dve.wait_ge(step2, b + 1)
                    for half in range(2):
                        dve.wait_ge(s["t_made"], b * NT + at[("Y", half)] + 1)
                        x4 = core.X[:, bass.ds(b * BTILES + 4 * half, 4), :]
                        dve.tensor_tensor(x4, x4, pT[:].rearrange("p (t d) -> p t d", d=D), ALU.add).then_inc(s["t_used"], 1)
                    assert step.n == CH, (step.n, CH)

            @block.tensor
            def _(pe):
                pe.sem_inc(s["pv_done"], 4)
                pe.wait_ge(s["loaded"], 16 * 6)
                pe.wait_ge(s["ones_made"], 5)
                q6f, k6f = Q6[:].rearrange("p t h c -> p t (h c)"), K6[:].rearrange("p t h c -> p t (h c)")
                pe.wait_ge(s["wqk_made"], 1)
                with pe.Fori(0, BATCH) as b:
                    pe.wait_ge(s["normed"], b + 1)
                    pe.wait_ge(s["exped"], b * 16 * NP_ + 2)
                    f2 = p2[:].rearrange("p a c -> p (a c)")
                    for k in range(BTILES):
                        ins = pe.transpose(f2[:, bass.ts(k, P)], nrm[:, k, :], core.ident[:])
                    ins.then_inc(s["turned"], 1)
                    pe.wait_ge(s["u_copied"], b + 1)
                    for half in range(2):
                        if half == 1:
                            pe.wait_ge(s["qkv_kept"], b * 2 + 1)
                        for k in range(4):
                            ins = pe.matmul(p2[:, k, 0:C3], uT[:, bass.ts(4 * half + k, P)], W[:], start=True, stop=True)
                        ins.then_inc(s["qkv_made"], 1)
                    pe.wait_ge(s["l_made"], b * 2 + 2)
                    pe.wait_ge(s["qkv_kept"], b * 2 + 2)
                    for pr in range(NP_):
                        for w, src in ((0, k6f), (1, q6f)):
                            if pr >= 2:
                                pe.wait_ge(s["q_used" if w else "k_used"], b * NP_ + pr - 1)
                            bank = p2[:, (2 * pr + w) % 4, :].bitcast(BF16)
                            for k in range(BTILES):
                                ins = pe.transpose(bank[:, bass.ts(k, P)], src[:, k, bass.ts(pr, P)], core.identb[:])
                            ins.then_inc(s["kq_turned"], 1)

                    def max_scores(g):
                        pr, j = g // 16, g % 16
                        qt, par = j // 2, j % 2
                        for half in range(2):
                            k1 = b * 32 * NP_ + 2 * g + half
                            pe.wait_ge(s["s1_used"], k1 + 1)
                            pe.matmul(p1[:, half, :], QT[:, pr, bass.ts(qt, P)], KZ[:, par, pr, bass.ts(half, 512)],
                                      start=True, stop=True).then_inc(s["s1_made"], 1)

                    def turn(key):
                        kind, n = key
                        pe.wait_ge(s["t_used"], b * NT + at[key] + 1)
                        if kind == "QM":
                            pe.wait_ge(s["m_made"], b * NP_ + n + 1)
                            for k in range(BTILES):
                                ins = pe.transpose(pTb[:, bass.ts(k, P)], q6f[:, k, bass.ts(n, P)], core.identb[:])
                        elif kind == "O":
                            pe.wait_ge(s["o_used"], b * NP_ + n + 2)
                            for k in range(4):
                                ins = pe.transpose(pT[:, bass.ts(k, P)], OT[:, bass.ts(k, P)], core.ident[:])
                        elif kind == "Z":
                            for k in range(4):
                                ins = pe.transpose(pT[:, bass.ts(k, P)], Z[:, 4 * n + k].rearrange("p h d -> p (h d)"),
                                                   core.ident[:])
                        else:
                            for k in range(4):
                                ins = pe.matmul(pT[:, bass.ts(k, P)], ZT[:, 4 * n + k, :], Wo[:], start=True, stop=True)
                        ins.then_inc(s["t_made"], 1)

                    def scores(pr, j):
                        kt, par = j // 2, j % 2
                        k2 = b * 16 * NP_ + 16 * pr + j
                        pe.wait_ge(s["exped"], k2 + 1)
                        for half in range(2):
                            ins = pe.matmul(p2[:, 2 * par + half, :], KZ[:, par, pr, bass.ts(kt, P)],
                                            QM[:, pr % 2, bass.ts(half, 512)], start=True, stop=True)
                        ins.then_inc(s["s2_made"], 1)

                    def values(pr, j):
                        kt, par = j // 2, j % 2
                        k2 = b * 16 * NP_ + 16 * pr + j
                        if j == 0:
                            pe.wait_ge(s["o_used"], b * NP_ + pr + 1)
                        pe.wait_ge(s["exped"], k2 + 3)
                        for half in range(2):
                            c = 2 * par + half
                            ins = pe.matmul(pO[32 * c:32 * c + DH + 1, :], V1[:, kt, 2 * pr + par, :],
                                            PT[:, j % 4, bass.ts(half, 512)], start=(kt == 0), stop=(kt == NQ - 1),
                                            skip_group_check=True)
                        ins.then_inc(s["pv_done"], 1)

                    pe.wait_ge(s["k_used"], b * NP_ + NP_)
                    pe.wait_ge(s["q_used"], b * NP_ + NP_)
                    for g in range(16 + AHEAD):
                        max_scores(g)
                        if g == 16:
                            turn(("QM", 0))
                            pe.wait_ge(s["t_used"], b * NT + at[("QM", 0)] + 2)
                    for pr in range(NP_):
                        for j in range(2 * NQ):
                            scores(pr, j)
                            g = 16 * (pr + 1) + j + AHEAD
                            if g < 16 * NP_:
                                max_scores(g)
                            if j >= 2:
                                values(pr, j - 2)
                            if j == 2 and pr > 0:
                                turn(("O", pr - 1))
                            if j == 14 and pr < NP_ - 1:
                                turn(("QM", pr + 1))
                        values(pr, 2 * NQ - 2)
                        values(pr, 2 * NQ - 1)
                        if pr < NP_ - 1:
                            pe.wait_ge(s["t_used"], b * NT + at[("QM", pr + 1)] + 2)
                    turn(("O", NP_ - 1))
                    pe.wait_ge(s["t_used"], b * NT + at[("O", NP_ - 1)] + 2)
                    turn(("Z", 0))
                    turn(("Z", 1))
                    pe.wait_ge(s["t_used"], b * NT + at[("Z", 1)] + 2)
                    turn(("Y", 0))
                    turn(("Y", 1))


def _as_is(a):
    return a


def _turned(a):
    return a.T


LAYOUT = {
    "x": ("L0_attn_a_u", _as_is),
    "scan_bc": ("L0_attn_a_x_proj_w", lambda a: np.tile(a[64:].T, (1, 3))),
    "scan_dt": ("L0_attn_a_x_proj_w", lambda a: a[:64].T),
    "scan_delta": ("L0_attn_a_dt_proj_w", _turned),
    "scan_delta_bias": ("L0_attn_a_dt_proj_b", _as_is),
    "scan_a_log": ("L0_attn_a_A_log", _as_is),
    "scan_skip": ("L0_attn_a_D", _as_is),
    "ffn_kernel": ("L0_ffn_kernel", _as_is),
    "ffn_bias": ("L0_ffn_bias", _as_is),
    "ffn_a_t": ("L0_ffn_a", _turned),
    "ffn_b": ("L0_ffn_b", _as_is),
    "mqa_g1": ("L0_attn_b_g1", _as_is),
    "mqa_wq_t": ("L0_attn_b_Wq", _turned),
    "mqa_wkv_t": ("L0_attn_b_Wkv", _turned),
    "mqa_wout_t": ("L0_attn_b_Wout", _turned),
    "mqa_g2": ("L0_attn_b_g2", _as_is),
    "single_qw": ("L1_attn_a_Qw", _as_is),
    "single_kw": ("L1_attn_a_Kw", _as_is),
    "single_vw": ("L1_attn_a_Vw", _as_is),
    "full_wqkv_t": ("L1_attn_b_Wqkv", _turned),
    "full_bqkv": ("L1_attn_b_bqkv", _as_is),
    "full_wo_t": ("L1_attn_b_Wo", _turned),
    "full_bo": ("L1_attn_b_bo", _as_is),
    "full_wq": ("L1_attn_b_wq", _as_is),
    "full_wk": ("L1_attn_b_wk", _as_is),
    "moe_ln1_weight": ("L1_ffn_ln1_weight", _as_is),
    "moe_ln1_bias": ("L1_ffn_ln1_bias", _as_is),
    "moe_ln2_weight": ("L1_ffn_ln2_weight", _as_is),
    "moe_ln2_bias": ("L1_ffn_ln2_bias", _as_is),
    "moe_router_weight": ("L1_ffn_router_weight", _as_is),
    "moe_w1": ("L1_ffn_moe_w1", _as_is),
    "moe_w2": ("L1_ffn_moe_w2", _as_is),
    "moe_qkv_t": ("L1_ffn_qkv_weight", _turned),
    "moe_proj_t": ("L1_ffn_proj_weight", _turned),
}


def program(nc, w, out, phases=tuple(range(8))):
    with ExitStack() as ctx:
        core = Core(nc, ctx)
        load_stream(core, w["x"].rearrange("b s d -> (b s) d"))
        ex = Experts(core, w)
        if 5 in phases or 7 in phases:
            clear_rows(core, ex)
        for n in phases:
            stream_stats(core, f"s{n}", twice=n in (2, 5, 7))
            if n == 0:
                scan_block(core, "scan", w["scan_bc"], w["scan_dt"], w["scan_delta"], w["scan_delta_bias"],
                           w["scan_a_log"], w["scan_skip"])
            elif n in (1, 3):
                ffn(core, f"ffn{n}", w["ffn_kernel"], w["ffn_bias"], w["ffn_a_t"], w["ffn_b"])
            elif n == 2:
                causal_mqa(core, "mqa", w["mqa_g1"], w["mqa_wq_t"], w["mqa_wkv_t"], w["mqa_wout_t"], w["mqa_g2"])
            elif n == 4:
                causal_single(core, "single", w["single_qw"], w["single_kw"], w["single_vw"])
            elif n in (5, 7):
                experts(core, f"moe{n}", ex)
            else:
                full_attention(core, "full", w["full_wqkv_t"], w["full_bqkv"], w["full_wo_t"], w["full_bo"],
                               w["full_wq"], w["full_wk"])
            core.end_stage()
        store_stream(core, out.rearrange("b s d -> (b s) d"))


def kernel(**inputs):
    import concourse.bacc as bacc
    from concourse.bass_utils import run_bass_kernel_spmd

    nc = bacc.Bacc("TRN2", target_bir_lowering=False, num_devices=1)
    arrays, given = {}, {}
    for name, (source, lay_out) in LAYOUT.items():
        a = np.ascontiguousarray(lay_out(np.asarray(inputs[source])))
        arrays["in_" + name] = a
        given[name] = nc.dram_tensor("in_" + name, a.shape, mybir.dt.from_np(a.dtype), kind="ExternalInput").ap()
    out = nc.dram_tensor("out", (BATCH, SEQ, D), F32, kind="ExternalOutput").ap()
    program(nc, given, out)
    return run_bass_kernel_spmd(nc, [arrays], core_ids=[0]).results[0]["out"]
```

```python
from contextlib import ExitStack

import numpy as np

import concourse.bass as bass
from concourse import mybir

F32 = mybir.dt.float32
BF16 = mybir.dt.bfloat16
F16 = mybir.dt.float16
I32 = mybir.dt.int32
U32 = mybir.dt.uint32
ALU = mybir.AluOpType
ACT = mybir.ActivationFunctionType
AX = mybir.AxisListType
RMAX = bass.bass_isa.ReduceOp.max

P = 128
D = 128
BATCH, SEQ = 4, 1024
TOKENS = BATCH * SEQ
TILES = TOKENS // P
BTILES = SEQ // P
GT = 4
GROUPS = TILES // GT
EPS = 1e-5
EXPERTS, CHOICES = 8, 2
CAPACITY = -(-CHOICES * TOKENS * 5 // (4 * EXPERTS))
EXPERT_ROWS = EXPERTS * CAPACITY


class Chain:

    def __init__(self, eng, sem, base=0):
        self.eng, self.sem, self.base, self.n = eng, sem, base, 0

    def __call__(self, ins):
        ins.then_inc(self.sem, 1)
        self.n += 1
        self.eng.wait_ge(self.sem, self.base + self.n)


def steps(eng, n, unroll, peel, body):
    rounds = (n - peel) // unroll
    with eng.Fori(0, rounds) as i:
        for u in range(unroll):
            body(i * unroll + u, u, False)
    for g in range(rounds * unroll, n):
        body(g, g % unroll, g == n - 1)


def batch_rows(eng, body):
    with eng.Fori(0, BATCH - 1) as b:
        body(b, False)
    body(BATCH - 1, True)


def follows(g, ahead, count=GROUPS):
    return not isinstance(g, int) or g + ahead < count


def newton_rsqrt(eng, step, y, v, t):
    step(eng.tensor_scalar(y.bitcast(I32), v.bitcast(I32), -0.5, 1597463007.0, ALU.mult, ALU.add))
    for _ in range(3):
        step(eng.scalar_tensor_tensor(out=t, in0=y, scalar=-0.5, in1=y, op0=ALU.mult, op1=ALU.mult))
        step(eng.tensor_tensor(t, t, v, ALU.mult))
        step(eng.scalar_tensor_tensor(out=y, in0=t, scalar=1.5, in1=y, op0=ALU.add, op1=ALU.mult))


class Core:

    def __init__(self, nc, ctx):
        self.nc, self.ctx, self.sems = nc, ctx, []
        self.X = self.sb("X", [P, TILES, D])
        self.ident = self.sb("ident", [P, P])
        self.identb = self.sb("identb", [P, P], BF16)
        self.rstd = self.sb("rstd", [P, TILES])
        self.shift = self.sb("shift", [P, TILES])
        self.rstd2 = self.sb("rstd2", [P, TILES])
        self.shift2 = self.sb("shift2", [P, TILES])
        self.stats = self.sb("stats", [P, TILES, 6])
        self.tmp = self.sb("tmp", [P, 3, TILES])
        self.zeros = self.sb("zeros", [P, 4 * (D + 1)])
        self.zeros_made, self.cleared = nc.alloc_semaphore(name="zeros_made"), nc.alloc_semaphore(name="rows_cleared")
        self.clears = (EXPERT_ROWS + CHOICES * TOKENS) // (4 * P)

    def sb(self, name, shape, dt=F32, ctx=None):
        return (ctx or self.ctx).enter_context(self.nc.sbuf_tensor(name, shape, dt))

    def ps(self, name, shape, dt=F32, ctx=None):
        return (ctx or self.ctx).enter_context(self.nc.psum_tensor(name, shape, dt))

    def clear(self, sp):
        sp.wait_ge(self.zeros_made, 1)
        for rows, count in ((self.rows_in, EXPERT_ROWS), (self.rows_out, CHOICES * TOKENS)):
            for k in range(0, count, 4 * P):
                to = rows[k:k + 4 * P, :].rearrange("(p t) d -> p (t d)", p=P)
                sp.dma_start(to, self.zeros[:, 0:to.shape[1]]).then_inc(self.cleared, 16)

    def sem(self, name):
        self.sems.append(self.nc.alloc_semaphore(name=name))
        return self.sems[-1]

    def end_stage(self):
        self.nc.clear_and_free_semaphores(self.sems)
        self.nc.all_engine_barrier()
        self.sems = []


def load_stream(core, x, loads=None, constants=None):
    nc = core.nc
    loaded, made = [core.sem(f"x_loaded{b}") for b in range(BATCH)], core.sem("ident_made")
    rows = x.rearrange("(t p) d -> p t d", p=P)
    with nc.Block() as block:
        @block.sync
        def _(sp):
            for b in range(BATCH):
                tiles = slice(b * BTILES, (b + 1) * BTILES)
                sp.dma_start(core.X[:, tiles, :], rows[:, tiles, :]).then_inc(loaded[b], 16)
            if loads is not None:
                loads(sp)
            core.clear(sp)

        @block.vector
        def _(dve):
            dve.memset(core.zeros[:], 0.0).then_inc(core.zeros_made, 1)
            for b in range(BATCH):
                dve.wait_ge(loaded[b], 16)
                row_moments(dve, core, core.X, b * BTILES, BTILES)

        @block.gpsimd
        def _(pool):
            pool.memset(core.ident[:], 0.0).then_inc(made, 1)
            pool.wait_ge(made, 1)
            pool.affine_select(out=core.ident[:], in_=core.ident[:], compare_op=ALU.not_equal, fill=1.0, base=0,
                               pattern=[[-1, P]], channel_multiplier=1).then_inc(made, 1)
            pool.wait_ge(made, 2)
            pool.tensor_copy(core.identb[:], core.ident[:]).then_inc(made, 1)
            if constants is not None:
                constants(pool)


def moments(dve, step, stats, n, mean, var, t, eps):
    me, m2e, mo, m2o = (stats[:, :, k] for k in (1, 2, 4, 5))
    step(dve.tensor_tensor(t, me, mo, ALU.subtract))
    dve.tensor_tensor(mean, me, mo, ALU.add)
    step(dve.tensor_tensor(var, m2e, m2o, ALU.add))
    step(dve.scalar_tensor_tensor(out=t, in0=t, scalar=n / 4.0, in1=t, op0=ALU.mult, op1=ALU.mult))
    step(dve.tensor_tensor(var, var, t, ALU.add))
    dve.tensor_scalar(mean, mean, 0.5, None, ALU.mult)
    step(dve.tensor_scalar(var, var, 1.0 / n, eps, ALU.mult, ALU.add))


def second_norm(dve, step, core, var, t):
    r2 = core.rstd2[:]
    step(dve.tensor_scalar(var, var, EPS, None, ALU.subtract))
    step(dve.tensor_tensor(var, var, core.rstd[:], ALU.mult))
    step(dve.tensor_tensor(var, var, core.rstd[:], ALU.mult))
    step(dve.tensor_scalar(var, var, EPS, None, ALU.add))
    newton_rsqrt(dve, step, r2, var, t)
    step(dve.tensor_tensor(r2, r2, core.rstd[:], ALU.mult))


def row_moments(dve, core, src, first, n):
    for k in range(n):
        dve.bn_stats(core.stats[:, bass.ds(first + k, 1), :], src[:, bass.ds(first + k, 1), :])


def stream_stats(core, name, src=None, twice=False, loads=None):
    chain = core.sem(f"{name}_stats_chain")
    mean, var, t = (core.tmp[:, k, :] for k in range(3))
    with core.nc.Block() as block:
        if loads is not None:
            @block.sync
            def _(sp):
                loads(sp)

        @block.vector
        def _(dve):
            if src is not None:
                with dve.Fori(0, GROUPS) as g:
                    row_moments(dve, core, src, g * GT, GT)
            step = Chain(dve, chain)
            step(dve.memset(t, 0.0))
            moments(dve, step, core.stats, D, mean, var, t, EPS)
            newton_rsqrt(dve, step, core.rstd[:], var, t)
            if twice:
                step(dve.scalar_tensor_tensor(out=core.shift[:], in0=mean, scalar=-1.0, in1=core.rstd[:],
                                              op0=ALU.mult, op1=ALU.mult))
                second_norm(dve, step, core, var, t)
            scale = core.rstd2 if twice else core.rstd
            out = core.shift2 if twice else core.shift
            step(dve.scalar_tensor_tensor(out=out[:], in0=mean, scalar=-1.0, in1=scale[:], op0=ALU.mult, op1=ALU.mult))


def normalise(dve, core, out, g):
    for j in range(GT):
        k = bass.ds(g * GT + j, 1)
        ins = dve.tensor_scalar(out[:, j, :], core.X[:, k, :], core.rstd[:, k], core.shift[:, k], ALU.mult, ALU.add)
    return ins


def ffn(core, name, w, bias, a_t, b):
    nc = core.nc
    with ExitStack() as ctx:
        sb = lambda n, s, dt=F32: core.sb(f"{name}_{n}", s, dt, ctx)
        ps = lambda n, s: core.ps(f"{name}_{n}", s, F32, ctx)
        sem = lambda n: core.sem(f"{name}_{n}")
        W, aT, B = sb("W", [D, D]), sb("aT", [16, D]), sb("B", [16, D])
        bias4, ones = sb("bias4", [1, GT, D]), sb("ones", [1, P])
        amax, top, scale, inv = sb("amax", [P, 1]), sb("top", [P, 1]), sb("scale", [P, 1]), sb("inv", [P, 1])
        q = sb("q", [D, D])
        weff = sb("weff", [D, D])
        nrm, uT = sb("nrm", [P, 2, GT, D]), sb("uT", [P, 2, GT * P])
        pT, pY = ps("pT", [P, 2, GT * P]), ps("pY", [P, 2, GT * P])
        pW = ps("pW", [P, D])
        loaded, chain, absmax, allmax, ones_made, ab_made, weff_made = map(
            sem, ("loaded", "chain", "absmax", "allmax", "ones_made", "ab_made", "weff_made"))
        normed, turned, copied, product, added = map(sem, ("normed", "turned", "copied", "product", "added"))
        flat = core.X[:].rearrange("p t d -> p (t d)")
        def loads(sp):
            sp.dma_start(W[:], w).then_inc(loaded, 16)
            sp.dma_start(aT[:], a_t).then_inc(loaded, 16)
            sp.dma_start(B[:], b).then_inc(loaded, 16)
            for j in range(GT):
                sp.dma_start(bias4[:, j, :], bias.rearrange("(o n) -> o n", o=1)).then_inc(loaded, 16)

        stream_stats(core, f"{name}_in", loads=loads)
        with nc.Block() as block:
            @block.gpsimd
            def _(pool):
                pool.memset(ones[:], 1.0).then_inc(ones_made, 1)
                pool.wait_ge(absmax, 1)
                pool.partition_all_reduce(top[:], amax[:], P, RMAX).then_inc(allmax, 1)

            @block.vector
            def _(dve):
                dve.sem_inc(added, 2)
                step = Chain(dve, chain)
                dve.wait_ge(loaded, 16 * 7)
                dve.tensor_reduce(amax[:], W[:], AX.X, ALU.max, apply_absolute_value=True).then_inc(absmax, 1)
                dve.wait_ge(allmax, 1)
                step(dve.reciprocal(inv[:], top[:]))
                step(dve.tensor_scalar(scale[:], top[:], 1.0 / 7.0, None, ALU.mult))
                step(dve.reciprocal(inv[:], scale[:]))
                step(dve.tensor_scalar(q[:], W[:], inv[:, 0:1], 12582912.0, ALU.mult, ALU.add))
                step(dve.tensor_scalar(q[:], q[:], 12582912.0, -8.0, ALU.subtract, ALU.max))
                step(dve.tensor_scalar(q[:], q[:], 7.0, scale[:, 0:1], ALU.min, ALU.mult))
                dve.wait_ge(ab_made, 1)
                dve.tensor_tensor(weff[:], q[:], pW[:], ALU.add).then_inc(weff_made, 1)

                def norm(g, u):
                    dve.wait_ge(turned, g + 1)
                    normalise(dve, core, nrm[:, u], g).then_inc(normed, 1)

                norm(0, 0)
                norm(1, 1)

                def body(g, u, last):
                    if follows(g, 2):
                        norm(g + 2, u)
                    dve.wait_ge(product, g + 3)
                    cols = bass.ds(g * GT * D, GT * D)
                    dve.tensor_tensor(flat[:, cols], flat[:, cols], pY[:, u, :], ALU.add).then_inc(added, 1)
                    dve.wait_ge(added, g + 3)
                    row_moments(dve, core, core.X, g * GT, GT)
                steps(dve, GROUPS, 2, 2, body)

            @block.tensor
            def _(pe):
                pe.sem_inc(turned, 2)
                pe.sem_inc(product, 2)
                pe.wait_ge(loaded, 16 * 7)
                pe.matmul(pW[:], aT[:], B[:], start=True, stop=True).then_inc(ab_made, 1)
                pe.wait_ge(ones_made, 1)
                pe.wait_ge(weff_made, 1)

                def turn(g, u):
                    pe.wait_ge(normed, g + 1)
                    pe.wait_ge(copied, g + 1)
                    for j in range(GT):
                        ins = pe.transpose(pT[:, u, bass.ts(j, P)], nrm[:, u, j, :], core.ident[:])
                    ins.then_inc(turned, 1)

                turn(0, 0)

                def body(g, u, last):
                    if not last:
                        turn(g + 1, 1 - u)
                    pe.wait_ge(copied, g + 3)
                    pe.wait_ge(added, g + 1)
                    pe.matmul(pY[:, u, :], ones[:], bias4[:], start=True, stop=False, skip_group_check=True)
                    for j in range(GT):
                        ins = pe.matmul(pY[:, u, bass.ts(j, P)], uT[:, u, bass.ts(j, P)], weff[:],
                                        start=False, stop=(j == GT - 1), skip_group_check=True)
                    ins.then_inc(product, 1)
                steps(pe, GROUPS, 2, 2, body)

            @block.scalar
            def _(act):
                act.sem_inc(copied, 2)

                def body(g, u, last):
                    act.wait_ge(turned, g + 3)
                    act.wait_ge(product, g + 1)
                    act.activation(uT[:, u, :], pT[:, u, :], ACT.Copy).then_inc(copied, 1)
                steps(act, GROUPS, 2, 0, body)


def scan_block(core, name, x, wbc, wdt, dtw, dtb, a_log, dvec):
    nc = core.nc
    NS = 16
    with ExitStack() as ctx:
        sb = lambda n, s, dt=F32: core.sb(f"{name}_{n}", s, dt, ctx)
        ps = lambda n, s: core.ps(f"{name}_{n}", s, F32, ctx)
        sem = lambda n: core.sem(f"{name}_{n}")
        Wbc, Wdt, Wz = sb("Wbc", [D, 96]), sb("Wdt", [D, 64]), sb("Wz", [64, D])
        zbias, dcol, A = sb("zbias", [P, 1]), sb("dcol", [P, 1]), sb("A", [P, NS])
        diagD = sb("diagD", [P, P])
        sel = sb("sel", [P, 2 * NS, P], BF16)
        nrm = sb("nrm", [P, BTILES, D])
        uT, dtT, zc, zabs, zexp, zpos = (sb(n, [P, SEQ]) for n in ("uT", "dtT", "zc", "zabs", "zexp", "zpos"))
        delta, du, yT = (sb(n, [P, SEQ]) for n in ("delta", "du", "yT"))
        hi, mid = (sb(n, [96, SEQ], BF16) for n in ("hi", "mid"))
        rest, rest2 = (sb(n, [96, SEQ]) for n in ("rest", "rest2"))
        bc3 = sb("bc3", [P, SEQ], BF16)
        dA, Bs, dBu, state, yc = (sb(n, [P, 2, SEQ]) for n in ("dA", "Bs", "dBu", "state", "yc"))
        pM, pB, pC, pY = (ps(n, [P, SEQ]) for n in ("pM", "pB", "pC", "pY"))
        names = ("loaded chain a_made sel_made diag_made normed turned u_copied bc_made hi_made rest_made split_made "
                 "dt_made dt_copied z_made z_copied act_chain log_made delta_made du_made "
                 "b_made b_copied c_made multiplied da_made scanned weighted summed y_copied y_turned added").split()
        s = dict(zip(names, map(sem, names)))
        flat = core.X[:].rearrange("p t d -> p (t d)")
        H = SEQ // 2
        MADE_AT, TAKEN_AT = {1: "u", 3: "bc", 6: "dt", 8: "z"}, {2: "u", 4: "bc", 7: "dt", 9: "z"}
        def loads(sp):
            sp.dma_start(Wbc[:], wbc).then_inc(s["loaded"], 16)
            sp.dma_start(Wdt[:], wdt).then_inc(s["loaded"], 16)
            sp.dma_start(Wz[:], dtw).then_inc(s["loaded"], 16)
            sp.dma_start(zbias[:], dtb.rearrange("(d o) -> d o", o=1)).then_inc(s["loaded"], 16)
            sp.dma_start(dcol[:], dvec.rearrange("(d o) -> d o", o=1)).then_inc(s["loaded"], 16)
            sp.dma_start(A[:], a_log.rearrange("(o n) -> o n", o=1).to_broadcast([P, NS])).then_inc(s["loaded"], 16)

        def constants(pool):
            pool.memset(sel[:], 0.0).then_inc(s["sel_made"], 1)
            for k in range(3):
                pool.wait_ge(s["sel_made"], k + 1)
                pool.affine_select(out=sel[0:96], in_=sel[0:96], compare_op=ALU.not_equal, fill=1.0, base=-32 * k,
                                   pattern=[[-1, 2 * NS], [0, P]], channel_multiplier=1).then_inc(s["sel_made"], 1)

        load_stream(core, x, loads, constants)
        stream_stats(core, f"{name}_in")
        with nc.Block() as block:
            @block.gpsimd
            def _(pool):
                pool.sem_inc(s["multiplied"], 2)
                with pool.Fori(0, BATCH) as b:
                    for n in range(NS):
                        it = b * NS + n
                        pool.wait_ge(s["du_made"], b + 1)
                        pool.wait_ge(s["b_copied"], it + 2)
                        pool.wait_ge(s["scanned"], it + 1)
                        pool.tensor_tensor(dBu[:, n % 2, :], Bs[:, n % 2, :], du[:], ALU.mult).then_inc(s["multiplied"], 1)

            @block.vector
            def _(dve):
                dve.sem_inc(s["scanned"], 2)
                dve.sem_inc(s["weighted"], 1)
                dve.sem_inc(s["added"], 1)
                dve.memset(bc3[96:P, :], 0.0)
                dve.wait_ge(s["loaded"], 16 * 6)
                dve.tensor_scalar(diagD[:], core.ident[:], dcol[:, 0:1], None, ALU.mult).then_inc(s["diag_made"], 1)

                def norm_rows(row):
                    for k in range(BTILES):
                        t = bass.ds(row * BTILES + k, 1)
                        ins = dve.tensor_scalar(nrm[:, k, :], core.X[:, t, :], core.rstd[:, t], core.shift[:, t],
                                                ALU.mult, ALU.add)
                    ins.then_inc(s["normed"], 1)

                def leave_high(row):
                    dve.wait_ge(s["hi_made"], row + 1)
                    dve.tensor_tensor(rest[:], pM[0:96, :], hi[:], ALU.subtract).then_inc(s["rest_made"], 1)
                    dve.wait_ge(s["rest_made"], row + 1)

                def leave_middle(row, step):
                    step(dve.tensor_copy(mid[:], rest[:]))
                    step(dve.tensor_tensor(rest2[:], rest[:], mid[:], ALU.subtract))

                def positive(row, step):
                    dve.wait_ge(s["z_copied"], row + 1)
                    step(dve.tensor_scalar(zpos[:], zc[:], 0.0, None, ALU.max))

                def start(row, first):
                    if not first:
                        dve.wait_ge(s["c_made"], row * NS)
                        dve.wait_ge(s["b_made"], row * NS)
                    dve.tensor_copy(bc3[0:32, :], hi[0:32, :])
                    dve.tensor_copy(bc3[32:64, :], mid[32:64, :])
                    dve.tensor_copy(bc3[64:96, :], rest2[64:96, :]).then_inc(s["split_made"], 1)
                    dve.wait_ge(s["log_made"], row + 1)
                    dve.tensor_tensor(delta[:], zpos[:], zexp[:], ALU.add).then_inc(s["delta_made"], 1)
                    dve.wait_ge(s["delta_made"], row + 1)
                    dve.tensor_tensor(du[:], delta[:], uT[:], ALU.mult).then_inc(s["du_made"], 1)

                step = Chain(dve, s["chain"])
                norm_rows(0)
                leave_high(0)
                leave_middle(0, step)
                positive(0, step)
                start(0, True)

                def row(b, last):
                    step = Chain(dve, s["chain"], (b + 1) * 3)
                    for n in range(NS):
                        it, u = b * NS + n, n % 2
                        dve.wait_ge(s["da_made"], it + 1)
                        dve.wait_ge(s["multiplied"], it + 3)
                        dve.tensor_tensor_scan(state[:, u, :], dA[:, u, :], dBu[:, u, :], 0.0, ALU.mult,
                                               ALU.add).then_inc(s["scanned"], 1)
                        dve.wait_ge(s["scanned"], it + 3)
                        dve.wait_ge(s["c_made"], it + 1)
                        dve.wait_ge(s["summed"], it + 1)
                        dve.tensor_tensor(yc[:, u, :], state[:, u, :], pC[:], ALU.mult).then_inc(s["weighted"], 1)
                        if not last:
                            if n == 0:
                                norm_rows(b + 1)
                            elif n == 5:
                                leave_high(b + 1)
                            elif n == 6:
                                leave_middle(b + 1, step)
                            elif n == 10:
                                positive(b + 1, step)
                    if not last:
                        start(b + 1, False)
                    dve.wait_ge(s["y_turned"], b + 1)
                    cols = bass.ds(b * SEQ, SEQ)
                    dve.tensor_tensor(flat[:, cols], flat[:, cols], pM[:], ALU.add).then_inc(s["added"], 1)
                    dve.wait_ge(s["added"], b + 2)
                    row_moments(dve, core, core.X, b * BTILES, BTILES)
                batch_rows(dve, row)

            @block.scalar
            def _(act):
                act.wait_ge(s["loaded"], 16 * 6)
                act.activation(A[:], A[:], ACT.Exp).then_inc(s["a_made"], 1)
                act.wait_ge(s["a_made"], 1)
                act.activation(A[:], A[:], ACT.Copy, scale=-1.0).then_inc(s["a_made"], 1)
                act.wait_ge(s["a_made"], 2)
                act.sem_inc(s["b_copied"], 1)

                def take(what, row):
                    if what == "u":
                        act.wait_ge(s["turned"], row + 1)
                        act.activation(uT[:], pM[:], ACT.Copy).then_inc(s["u_copied"], 1)
                    elif what == "bc":
                        act.wait_ge(s["bc_made"], row + 1)
                        act.activation(hi[:], pM[0:96, :], ACT.Copy).then_inc(s["hi_made"], 1)
                    elif what == "dt":
                        act.wait_ge(s["dt_made"], row + 1)
                        act.activation(dtT[0:64, :], pM[0:64, :], ACT.Copy).then_inc(s["dt_copied"], 1)
                    else:
                        step = Chain(act, s["act_chain"], row * 2)
                        act.wait_ge(s["z_made"], row + 1)
                        act.activation(zc[:], pM[:], ACT.Identity, bias=zbias[:, 0:1]).then_inc(s["z_copied"], 1)
                        act.wait_ge(s["z_copied"], row + 1)
                        step(act.activation(zabs[:], zc[:], ACT.Abs))
                        step(act.activation(zexp[:], zabs[:], ACT.Exp, scale=-1.0))

                def log(row):
                    act.activation(zexp[:], zexp[:], ACT.Ln, bias=1.0).then_inc(s["log_made"], 1)

                for what in ("u", "bc", "dt", "z"):
                    take(what, 0)
                log(0)

                def row(b, last):
                    def copy_b(n):
                        act.wait_ge(s["b_made"], b * NS + n + 1)
                        act.wait_ge(s["multiplied"], b * NS + n + 1)
                        act.activation(Bs[:, n % 2, :], pB[:], ACT.Copy).then_inc(s["b_copied"], 1)

                    copy_b(0)
                    act.wait_ge(s["delta_made"], b + 1)
                    for n in range(NS):
                        act.wait_ge(s["scanned"], b * NS + n + 1)
                        act.activation(dA[:, n % 2, :], delta[:], ACT.Exp, scale=A[:, n:n + 1]).then_inc(s["da_made"], 1)
                        if n < NS - 1:
                            copy_b(n + 1)
                        if not last and n in TAKEN_AT:
                            take(TAKEN_AT[n], b + 1)
                    if not last:
                        log(b + 1)
                    act.wait_ge(s["summed"], b * NS + NS + 2)
                    act.activation(yT[:], pY[:], ACT.Copy).then_inc(s["y_copied"], 1)
                batch_rows(act, row)

            @block.tensor
            def _(pe):
                halves = (slice(0, H), slice(H, SEQ))
                pe.sem_inc(s["summed"], 2)
                pe.wait_ge(s["loaded"], 16 * 6)
                pe.wait_ge(s["sel_made"], 4)
                pe.wait_ge(s["diag_made"], 1)

                def make(what, row):
                    if what == "u":
                        pe.wait_ge(s["normed"], row + 1)
                        pe.wait_ge(s["added"], 1 if isinstance(row, int) and row == 0 else row)
                        for k in range(BTILES):
                            ins = pe.transpose(pM[:, bass.ts(k, P)], nrm[:, k, :], core.ident[:])
                        ins.then_inc(s["turned"], 1)
                    elif what == "bc":
                        pe.wait_ge(s["u_copied"], row + 1)
                        for h in halves:
                            ins = pe.matmul(pM[0:96, h], Wbc[:], uT[:, h], start=True, stop=True)
                        ins.then_inc(s["bc_made"], 1)
                    elif what == "dt":
                        pe.wait_ge(s["rest_made"], row + 1)
                        for h in halves:
                            ins = pe.matmul(pM[0:64, h], Wdt[:], uT[:, h], start=True, stop=True)
                        ins.then_inc(s["dt_made"], 1)
                    else:
                        pe.wait_ge(s["dt_copied"], row + 1)
                        for h in halves:
                            ins = pe.matmul(pM[:, h], Wz[:], dtT[0:64, h], start=True, stop=True)
                        ins.then_inc(s["z_made"], 1)

                for what in ("u", "bc", "dt", "z"):
                    make(what, 0)

                def row(b, last):
                    def spread_b(n):
                        pe.wait_ge(s["b_copied"], b * NS + n + 1)
                        for h in halves:
                            ins = pe.matmul(pB[:, h], sel[:, n, :], bc3[:, h], start=True, stop=True)
                        ins.then_inc(s["b_made"], 1)

                    def spread_c(n):
                        pe.wait_ge(s["weighted"], b * NS + n + 1)
                        for h in halves:
                            ins = pe.matmul(pC[:, h], sel[:, n + NS, :], bc3[:, h], start=True, stop=True)
                        ins.then_inc(s["c_made"], 1)

                    for h in halves:
                        pe.matmul(pY[:, h], diagD[:], uT[:, h], start=True, stop=False, skip_group_check=True)
                    pe.wait_ge(s["split_made"], b + 1)
                    spread_b(0)
                    spread_c(0)
                    spread_b(1)
                    for n in range(NS):
                        if n < NS - 2:
                            spread_b(n + 2)
                        if n < NS - 1:
                            spread_c(n + 1)
                        pe.wait_ge(s["weighted"], b * NS + n + 2)
                        for h in halves:
                            ins = pe.matmul(pY[:, h], core.ident[:], yc[:, n % 2, h], start=False, stop=(n == NS - 1),
                                            skip_group_check=True)
                        ins.then_inc(s["summed"], 1)
                        if not last and n in MADE_AT:
                            make(MADE_AT[n], b + 1)
                    pe.wait_ge(s["y_copied"], b + 1)
                    if not last:
                        pe.wait_ge(s["z_copied"], b + 2)
                    else:
                        pe.wait_ge(s["added"], b + 1)
                    for k in range(BTILES):
                        ins = pe.transpose(pM[:, bass.ts(k, P)], yT[:, bass.ts(k, P)], core.ident[:])
                    ins.then_inc(s["y_turned"], 1)
                batch_rows(pe, row)


def causal_mqa(core, name, g1, wq_t, wkv_t, wout_t, g2):
    nc = core.nc
    NH, DH = 16, 64
    NQ = BTILES
    HALVES = NQ * (NQ + 1)
    HB = NH // 2
    RING, LAG = 4, 3
    UNIT = 1024.0
    GAP = 8
    BELOW = -(2.0 ** 23)
    EARLY = 4
    with ExitStack() as ctx:
        sb = lambda n, s, dt=F32: core.sb(f"{name}_{n}", s, dt, ctx)
        ps = lambda n, s: core.ps(f"{name}_{n}", s, F32, ctx)
        sem = lambda n: core.sem(f"{name}_{n}")
        Wq, Wkv, Wout = sb("Wq", [D, NH * DH]), sb("Wkv", [D, 2 * DH]), sb("Wout", [P, 8, D])
        gcol, g2row = sb("gcol", [P, 1]), sb("g2row", [P, D])
        identh = sb("identh", [P, P], F16)
        below = sb("below", [P, 4, P], BF16)
        nrm, uT = sb("nrm", [P, BTILES, D]), sb("uT", [P, SEQ])
        kv, V = sb("kv", [P, BTILES, 2 * DH]), sb("V", [P, BTILES, DH])
        ksq = sb("ksq", [P, BTILES, DH])
        kss, krs, ktmp = (sb(n, [P, BTILES]) for n in ("kss", "krs", "ktmp"))
        k2 = sb("k2", [P, BTILES, 2, 2, DH], F16)
        kT = sb("kT", [P, 2, SEQ], F16)
        qraw, qsq, qn = sb("qraw", [P, 2, NH, DH]), sb("qsq", [P, NH, DH]), sb("qn", [P, NH, DH])
        q2 = sb("q2", [P, 2, NH, 2, DH], F16)
        qss, qrs, qtmp = (sb(n, [P, NH]) for n in ("qss", "qrs", "qtmp"))
        qT = sb("qT", [P, NQ, NH, P], F16)
        pT = sb("pT", [P, RING, 2, 512])
        sums, over = sb("sums", [P, 2, 2, 2, 512]), sb("over", [P, 2, P])
        pick, spread = sb("pick", [P, 4, 32]), sb("spread", [P, 2, 4, 2, DH])
        zero = sb("zero", [P, 1])
        oraw, oT = sb("oraw", [P, 2, 512]), sb("oT", [P, 2, 4, P])
        OUT = sb("OUT", [P, TILES, D])
        pS = ps("pS", [P, 2, 2, 512])
        pO = ps("pO", [P, 2, 512])
        pX = ps("pX", [P, 2, 512])
        names = ("loaded folded below_made ones_made normed k_split k_turned k_copied s_made exped pv_done o_taken "
                 "summed_even summed_odd "
                 "px_made px_dve px_act q_scaled q_split v_copied chain").split()
        s = dict(zip(names, map(sem, names)))

        def queries(tiles):
            out = []
            for n, (tile, row) in enumerate(tiles):
                out += [("Q", tile, row, 0), ("Q", tile, row, 1)]
                if n > 0:
                    out += [("T",) + tiles[n - 1] + (0,), ("T",) + tiles[n - 1] + (1,)]
            return out + [("T",) + tiles[-1] + (0,), ("T",) + tiles[-1] + (1,)]

        def row_start(row):
            return [("U", 0, row, 0), ("U", 0, row, 1), ("KV", 0, row, 0), ("KV", 0, row, 1)]

        def outputs(qt):
            return [("S", qt, 0, 0), ("B", qt, 0, 0), ("B", qt, 0, 1), ("G", qt, 0, 0)]

        first_uses = row_start(0) + queries([(t, 0) for t in range(EARLY)])

        def plan(last):
            prep = queries([(t, 0) for t in range(EARLY, NQ)])
            if not last:
                prep += row_start(1) + queries([(t, 1) for t in range(EARLY)])
            slots, done = [], {}
            for qt in range(NQ):
                outs = outputs(qt - 1) if qt > 0 else []
                for h in range(2 * (qt + 1)):
                    now = len(slots)
                    if outs and (h >= LAG or h == 2 * qt + 1):
                        slots.append([outs.pop(0)] if h < 2 * qt + 1 else outs)
                    elif prep and (prep[0][0] != "T" or now - done[prep[0][1:3]] >= GAP or now >= prep[0][1] * (prep[0][1] + 1) - 3):
                        key = prep.pop(0)
                        if key[0] == "Q":
                            done[key[1:3]] = now
                        slots.append([key])
                    else:
                        slots.append([])
            slots[-1] = slots[-1] + prep
            return slots, outputs(NQ - 1)

        plans = {last: plan(last) for last in (False, True)}
        flat = {last: [u for sl in plans[last][0] for u in sl] + plans[last][1] for last in plans}
        for qt in range(EARLY, NQ):
            assert all(any(("T", qt, 0, 1) in sl for sl in plans[last][0][:qt * (qt + 1)]) for last in plans)
        FIRST, USES = len(first_uses), len(flat[False])

        assert FIRST % 2 == 0 and USES % 2 == 0
        taker = lambda key: "px_act" if key[0] == "T" else "px_dve"
        per_row = {q: sum(taker(u) == q for u in flat[False]) for q in ("px_act", "px_dve")}
        at_first = {q: sum(taker(u) == q for u in first_uses) for q in ("px_act", "px_dve")}

        def wait_taken(eng, b, uses, n):
            q = taker(uses[n])
            count = sum(taker(u) == q for u in uses[:n + 1])
            eng.wait_ge(s[q], count if b is None else at_first[q] + b * per_row[q] + count)

        def norms(last):
            out = {}
            for h, uses in enumerate(plans[last][0]):
                for kind, qt, ahead, c in uses:
                    if kind == "Q" and c == 1:
                        for part in range(3):
                            out.setdefault(min(h + 1 + part, HALVES - 1), []).append((qt, ahead, part))
            return out

        def splits(last):
            out = {}
            for h, uses in enumerate(plans[last][0]):
                for kind, qt, ahead, c in uses:
                    if kind == "Q" and c == 1:
                        turned = next(k for k, u in enumerate(plans[last][0]) if ("T", qt, ahead, 0) in u)
                        out.setdefault(min(h + 5, turned), []).append((qt, ahead))
            return out

        def add_up(eng, b, qt, h, done):
            part, total = pT[:, h % RING], sums[:, qt % 2, h % 2]
            if h - qt * (qt + 1) < 2:
                nothing = zero[:].rearrange("p (a c) -> p a c", c=1).to_broadcast([P, 2, 512])
                eng.tensor_tensor(total, part, nothing, ALU.add).then_inc(s[done], 1)
            else:
                eng.wait_ge(s[done], b * (HALVES // 2) + h // 2 + 2)
                eng.tensor_tensor(total, total, part, ALU.add).then_inc(s[done], 1)

        def loads(sp):
            sp.dma_start(Wkv[:], wkv_t).then_inc(s["loaded"], 16)
            sp.dma_start(Wq[:], wq_t).then_inc(s["loaded"], 16)
            sp.dma_start(gcol[:], g1.rearrange("(d o) -> d o", o=1)).then_inc(s["loaded"], 16)
            sp.dma_start(Wout[:], wout_t.rearrange("(j p) n -> p j n", p=P)).then_inc(s["loaded"], 16)
            sp.dma_start(g2row[:], g2.rearrange("(o d) -> o d", o=1).to_broadcast([P, D])).then_inc(s["loaded"], 16)

        stream_stats(core, f"{name}_in", twice=True, loads=loads)
        with nc.Block() as block:
            @block.gpsimd
            def _(pool):
                pool.memset(zero[:], 0.0).then_inc(s["ones_made"], 1)
                pool.memset(pick[:], 0.0).then_inc(s["ones_made"], 1)
                pool.memset(spread[:], 0.0).then_inc(s["ones_made"], 1)
                pool.wait_ge(s["ones_made"], 3)
                for j in range(4):
                    pool.memset(pick[:, j].rearrange("p (a b) -> p a b", b=4)[:, :, j:j + 1], 1.0)
                for half in range(2):
                    pool.affine_select(out=spread[:, half], in_=spread[:, half], compare_op=ALU.not_equal, fill=1.0,
                                       base=-64 * half, pattern=[[-1, 4], [-32, 2], [0, DH]], channel_multiplier=1)\
                        .then_inc(s["ones_made"], 1)
                pool.memset(below[:], 0.0).then_inc(s["below_made"], 1)
                pool.wait_ge(s["below_made"], 1)
                pool.affine_select(out=below[:], in_=below[:], compare_op=ALU.is_ge, fill=BELOW, base=0,
                                   pattern=[[0, 4], [1, P]], channel_multiplier=-1).then_inc(s["below_made"], 1)

                pool.sem_inc(s["summed_odd"], 2)

                def split(n, par):
                    pool.wait_ge(s["q_scaled"], n + 1)
                    pool.tensor_tensor(q2[:, par, :, 1, :], qn[:], q2[:, par, :, 0, :], ALU.subtract).then_inc(s["q_split"], 1)

                for t in range(EARLY):
                    split(t, t % 2)

                def row(b, last):
                    when = splits(last)
                    for qt in range(NQ):
                        for k in range(2 * (qt + 1)):
                            h = qt * (qt + 1) + k
                            for tile, ahead in when.get(h, []):
                                split((b + ahead) * NQ + tile, tile % 2)
                            if k % 2 == 1:
                                pool.wait_ge(s["exped"], b * HALVES + h + 3)
                                add_up(pool, b, qt, h, "summed_odd")
                batch_rows(pool, row)

            @block.scalar
            def _(act):
                act.sem_inc(s["exped"], 2)
                act.sem_inc(s["o_taken"], 1)

                def keys(b):
                    act.wait_ge(s["k_turned"], b + 1)
                    act.activation(kT[:].rearrange("p a c -> p (a c)"), pS[:, 0].rearrange("p a c -> p (a c)").bitcast(F16),
                                   ACT.Copy).then_inc(s["k_copied"], 1)

                def turned(b, uses, base, n):
                    kind, qt, ahead, c = uses[n]
                    act.wait_ge(s["px_made"], base + n + 1)
                    act.activation(qT[:, qt, HB * c:HB * c + HB, :].rearrange("p h q -> p (h q)"),
                                   pX[:, n % 2].bitcast(F16), ACT.Copy).then_inc(s["px_act"], 1)

                keys(0)
                for n, key in enumerate(first_uses):
                    if key[0] == "T":
                        turned(None, first_uses, 0, n)

                def take(b, last, qt):
                    act.wait_ge(s["pv_done"], b * HALVES + (qt + 1) * (qt + 2) + RING)
                    if qt > 0:
                        wait_taken(act, b, flat[last], flat[last].index(("B", qt - 1, 0, 1)))
                    else:
                        act.wait_ge(s["px_dve"], at_first["px_dve"] + b * per_row["px_dve"])
                    act.activation(oraw[:].rearrange("p a c -> p (a c)"), pO[:].rearrange("p a c -> p (a c)"), ACT.Copy)\
                       .then_inc(s["o_taken"], 1)

                def row(b, last):
                    n = 0
                    for h in range(HALVES):
                        act.wait_ge(s["s_made"], b * HALVES + h + 1)
                        act.wait_ge(s["pv_done"], b * HALVES + h + 1)
                        act.wait_ge(s["summed_odd" if h % 2 else "summed_even"], b * (HALVES // 2) + h // 2 + 1)
                        act.activation(pT[:, h % RING].rearrange("p a c -> p (a c)"),
                                       pS[:, h % 2].rearrange("p a c -> p (a c)"), ACT.Exp, scale=16.0 / UNIT ** 2)\
                           .then_inc(s["exped"], 1)
                        for key in plans[last][0][h]:
                            if key[0] == "T":
                                turned(b, flat[last], FIRST + b * USES, n)
                            n += 1
                        if h in [qt * (qt + 1) + LAG - 1 for qt in range(1, NQ)]:
                            take(b, last, [qt for qt in range(1, NQ) if h == qt * (qt + 1) + LAG - 1][0] - 1)
                    take(b, last, NQ - 1)
                    if not last:
                        keys(b + 1)
                batch_rows(act, row)

            @block.vector
            def _(dve):
                dve.sem_inc(s["summed_even"], 2)
                dve.tensor_copy(identh[:], core.ident[:])
                dve.wait_ge(s["ones_made"], 1)
                dve.wait_ge(s["loaded"], 16 * 5)
                dve.tensor_scalar(Wkv[:], Wkv[:], gcol[:, 0:1], None, ALU.mult)
                dve.tensor_scalar(Wq[:], Wq[:], gcol[:, 0:1], None, ALU.mult).then_inc(s["folded"], 1)
                CH = (3 + 10 + 3) + NQ * (3 + 10 + 2)

                def norm_rows(row):
                    for k in range(BTILES):
                        t = bass.ds(row * BTILES + k, 1)
                        ins = dve.tensor_scalar(nrm[:, k, :], core.X[:, t, :], core.rstd2[:, t], core.shift2[:, t],
                                                ALU.mult, ALU.add)
                    ins.then_inc(s["normed"], 1)

                def side(uses, b, base, n, step):
                    kind, qt, ahead, c = uses[n]
                    if kind == "T":
                        return
                    dve.wait_ge(s["px_made"], base + n + 1)
                    if kind == "U":
                        dve.tensor_copy(uT[:, bass.ts(c, 512)], pX[:, n % 2]).then_inc(s["px_dve"], 1)
                    elif kind == "KV":
                        dve.tensor_copy(kv[:, 4 * c:4 * c + 4, :].rearrange("p t c -> p (t c)"), pX[:, n % 2]).then_inc(s["px_dve"], 1)
                        if c == 1:
                            wait_taken(dve, b, uses, n)
                            step(dve.tensor_tensor(ksq[:], kv[:, :, 0:DH], kv[:, :, 0:DH], ALU.mult))
                            step(dve.tensor_reduce(kss[:], ksq[:], AX.X, ALU.add))
                            step(dve.tensor_scalar(kss[:], kss[:], 1e-24, None, ALU.max))
                            newton_rsqrt(dve, step, krs[:], kss[:], ktmp[:])
                            step(dve.tensor_scalar(krs[:], krs[:], UNIT, None, ALU.mult))
                            step(dve.tensor_tensor(ksq[:], kv[:, :, 0:DH],
                                                   krs[:].rearrange("p (t o) -> p t o", o=1).to_broadcast([P, BTILES, DH]),
                                                   ALU.mult))
                            dve.tensor_copy(k2[:, :, 0, 0, :], ksq[:])
                            step(dve.tensor_copy(k2[:, :, 1, 1, :], ksq[:]))
                            dve.tensor_tensor(k2[:, :, 0, 1, :], ksq[:], k2[:, :, 0, 0, :], ALU.subtract)
                            dve.tensor_tensor(k2[:, :, 1, 0, :], ksq[:], k2[:, :, 1, 1, :], ALU.subtract)\
                               .then_inc(s["k_split"], 1)
                    elif kind == "Q":
                        dve.tensor_copy(qraw[:, qt % 2, HB * c:HB * c + HB, :].rearrange("p h d -> p (h d)"), pX[:, n % 2])\
                           .then_inc(s["px_dve"], 1)
                    elif kind == "S":
                        dve.reciprocal(over[:, qt % 2], pX[:, n % 2, 0:P]).then_inc(s["px_dve"], 1)
                    elif kind == "B":
                        dve.wait_ge(s["o_taken"], b * NQ + qt + 2)
                        dve.tensor_tensor(oT[:, c].rearrange("p j q -> p (j q)"), oraw[:, c], pX[:, n % 2], ALU.mult)\
                           .then_inc(s["px_dve"], 1)
                    else:
                        dve.tensor_copy(OUT[:, bass.ds(b * BTILES + qt, 1), :].rearrange("p t d -> p (t d)"),
                                        pX[:, n % 2, 0:D]).then_inc(s["px_dve"], 1)

                def scale(qt, row, part, step):
                    raw = qraw[:, qt % 2]
                    if part == 0:
                        step(dve.tensor_tensor(qsq[:], raw, raw, ALU.mult))
                        step(dve.tensor_reduce(qss[:], qsq[:], AX.X, ALU.add))
                    elif part == 1:
                        step(dve.tensor_scalar(qss[:], qss[:], 1e-24 / 256, None, ALU.max))
                        newton_rsqrt(dve, step, qrs[:], qss[:], qtmp[:])
                    else:
                        step(dve.tensor_scalar(qrs[:], qrs[:], UNIT, None, ALU.mult))
                        if not (qt == 0 and isinstance(row, int) and row == 0):
                            dve.wait_ge(s["q_split"], row * NQ + qt)
                        step(dve.tensor_tensor(qn[:], raw,
                                               qrs[:].rearrange("p (h o) -> p h o", o=1).to_broadcast([P, NH, DH]),
                                               ALU.mult))
                        dve.tensor_copy(q2[:, qt % 2, :, 0, :], qn[:]).then_inc(s["q_scaled"], 1)

                norm_rows(0)
                step = Chain(dve, s["chain"])
                for n, (kind, qt, ahead, c) in enumerate(first_uses):
                    side(first_uses, None, 0, n, step)
                    if kind == "Q" and c == 1:
                        wait_taken(dve, None, first_uses, n)
                        for part in range(3):
                            scale(qt, 0, part, step)
                BEFORE = step.n
                def row(b, last):
                    step = Chain(dve, s["chain"], BEFORE + b * CH)
                    dve.tensor_copy(V[:], kv[:, :, DH:2 * DH]).then_inc(s["v_copied"], 1)
                    if not last:
                        norm_rows(b + 1)
                    (slots, tail), when = plans[last], norms(last)
                    base, n, h = FIRST + b * USES, 0, 0
                    for qt in range(NQ):
                        for k in range(2 * (qt + 1)):
                            if k % 2 == 1:
                                sum_even(b, qt, h - 1)
                            for key in slots[h]:
                                side(flat[last], b, base, n, step)
                                n += 1
                            for tile, ahead, part in when.get(h, []):
                                if part == 0:
                                    wait_taken(dve, b, flat[last], flat[last].index(("Q", tile, ahead, 1)))
                                scale(tile, b + ahead, part, step)
                            h += 1
                    for key in tail:
                        side(flat[last], b, base, n, step)
                        n += 1
                    wait_taken(dve, b, flat[last], len(flat[last]) - 1)
                    row_moments(dve, core, OUT, b * BTILES, BTILES)
                    assert last or step.n == CH

                def sum_even(b, qt, h):
                    dve.wait_ge(s["exped"], b * HALVES + h + 3)
                    add_up(dve, b, qt, h, "summed_even")

                batch_rows(dve, row)

            @block.tensor
            def _(pe):
                pe.sem_inc(s["pv_done"], RING)
                pe.wait_ge(s["folded"], 1)
                pe.wait_ge(s["ones_made"], 5)
                pe.wait_ge(s["below_made"], 2)

                def side(uses, b, base, n):
                    kind, qt, ahead, c = uses[n]
                    row = 0 if b is None else b + ahead
                    if n >= 2:
                        wait_taken(pe, b, uses, n - 2)
                    bank = pX[:, n % 2]
                    if kind == "U":
                        pe.wait_ge(s["normed"], row + 1)
                        for j in range(4):
                            ins = pe.transpose(bank[:, bass.ts(j, P)], nrm[:, 4 * c + j, :], core.ident[:])
                    elif kind == "KV":
                        for j in range(4):
                            ins = pe.matmul(bank[:, bass.ts(j, P)], uT[:, bass.ts(4 * c + j, P)], Wkv[:], start=True, stop=True)
                    elif kind == "Q":
                        if b is None or ahead:
                            wait_taken(pe, b, uses, uses.index(("U", 0, ahead, qt // 4)))
                        ins = pe.matmul(bank, uT[:, bass.ts(qt, P)], Wq[:, bass.ts(c, 512)], start=True, stop=True)
                    elif kind == "T":
                        pe.wait_ge(s["q_split"], row * NQ + qt + 1)
                        for j in range(HB):
                            place = j // 2 + 4 * (j % 2)
                            ins = pe.transpose(bank.bitcast(F16)[:, bass.ts(place, P)],
                                               q2[:, qt % 2, HB * c + j].rearrange("p c d -> p (c d)"), identh[:])
                    elif kind == "S":
                        for q in ("summed_even", "summed_odd"):
                            pe.wait_ge(s[q], b * (HALVES // 2) + (qt + 1) * (qt + 2) // 2 + 2)
                        for j in range(4):
                            for g in range(4):
                                ins = pe.matmul(bank[32 * g:32 * g + 32, 0:P], pick[:, j, :],
                                                sums[:, qt % 2, g // 2, g % 2, bass.ts(j, P)],
                                                start=(j == 0), stop=(j == 3), skip_group_check=True)
                    elif kind == "B":
                        wait_taken(pe, b, uses, uses.index(("S", qt, 0, 0)))
                        for j in range(4):
                            ins = pe.matmul(bank[:, bass.ts(j, P)], spread[:, c, j].rearrange("p a d -> p (a d)"),
                                            over[:, qt % 2, :], start=True, stop=True)
                    else:
                        wait_taken(pe, b, uses, n - 1)
                        for j in range(8):
                            ins = pe.matmul(bank[:, 0:D], oT[:, j // 4, j % 4, :], Wout[:, j, :], start=(j == 0), stop=(j == 7))
                    ins.then_inc(s["px_made"], 1)

                def turn_keys(row):
                    pe.wait_ge(s["k_split"], row + 1)
                    pe.wait_ge(s["exped"], row * HALVES + 2)
                    bank = pS[:, 0].rearrange("p a c -> p (a c)").bitcast(F16)
                    for v in range(2):
                        for k in range(BTILES):
                            ins = pe.transpose(bank[:, bass.ts(v * BTILES + k, P)], k2[:, k, v].rearrange("p c d -> p (c d)"),
                                               identh[:])
                    ins.then_inc(s["k_turned"], 1)

                for n, key in enumerate(first_uses):
                    if n == 6:
                        turn_keys(0)
                    side(first_uses, None, 0, n)

                def row(b, last):
                    def scores(qt, kt, half):
                        h = qt * (qt + 1) + 2 * kt + half
                        pe.wait_ge(s["exped"], b * HALVES + h + 1)
                        for v in range(2):
                            for c in range(2):
                                ins = pe.matmul(pS[:, half, c, :], kT[:, v, bass.ts(kt, P)],
                                                qT[:, qt, HB * half + 4 * c:HB * half + 4 * c + 4, :].rearrange("p h q -> p (h q)"),
                                                start=(v == 0), stop=(v == 1 and kt < qt))
                        if kt == qt:
                            for c in range(2):
                                ins = pe.matmul(pS[:, half, c, :], core.identb[:], below[:].rearrange("p a q -> p (a q)"),
                                                start=False, stop=True)
                        ins.then_inc(s["s_made"], 1)

                    def values(qt, kt, half):
                        h = qt * (qt + 1) + 2 * kt + half
                        if kt == 0 and half == 0:
                            pe.wait_ge(s["o_taken"], b * NQ + qt + 1)
                            if qt == 0:
                                pe.wait_ge(s["v_copied"], b + 1)
                        pe.wait_ge(s["exped"], b * HALVES + h + 3)
                        for par in range(2):
                            ins = pe.matmul(pO[64 * par:64 * par + 64, half, :], V[:, kt, :], pT[:, h % RING, par, :],
                                            start=(kt == 0), stop=(kt == qt), skip_group_check=True)
                        ins.then_inc(s["pv_done"], 1)

                    slots, tail = plans[last]
                    base, n, h, late = FIRST + b * USES, 0, 0, []
                    pe.wait_ge(s["k_copied"], b + 1)
                    for q in ("px_dve", "px_act"):
                        pe.wait_ge(s[q], at_first[q] + b * per_row[q])
                    for qt in range(NQ):
                        key = ("T", qt, 0, 1)
                        if qt >= EARLY:
                            wait_taken(pe, b, flat[last], flat[last].index(key))
                        for kt in range(qt + 1):
                            for half in range(2):
                                scores(qt, kt, half)
                                late.append((qt, kt, half))
                                if len(late) > LAG:
                                    values(*late.pop(0))
                                for key in slots[h]:
                                    side(flat[last], b, base, n)
                                    n += 1
                                h += 1
                    for args in late:
                        values(*args)
                    if not last:
                        turn_keys(b + 1)
                    for key in tail:
                        side(flat[last], b, base, n)
                        n += 1
                batch_rows(pe, row)

        stream_stats(core, f"{name}_out")
        chain, weighted, added = sem("last_chain"), sem("last_weighted"), sem("last_added")
        part = kv[:].rearrange("p (u t) c -> p u t c", u=2)
        with nc.Block() as block:
            @block.vector
            def _(dve):
                def weigh(g, u):
                    dve.wait_ge(added, g + 1)
                    for j in range(GT):
                        t = bass.ds(g * GT + j, 1)
                        ins = dve.tensor_scalar(part[:, u, j, :], OUT[:, t, :], core.rstd[:, t], core.shift[:, t],
                                                ALU.mult, ALU.add)
                    ins.then_inc(chain, 1)
                    dve.wait_ge(chain, g + 1)
                    dve.tensor_tensor(part[:, u], part[:, u], g2row[:].rearrange("p (o d) -> p o d", o=1)
                                      .to_broadcast([P, GT, D]), ALU.mult).then_inc(weighted, 1)

                weigh(0, 0)
                weigh(1, 1)

                def body(g, u, last):
                    if follows(g, 2):
                        weigh(g + 2, u)
                    dve.wait_ge(added, g + 3)
                    row_moments(dve, core, core.X, g * GT, GT)
                steps(dve, GROUPS, 2, 2, body)

            @block.gpsimd
            def _(pool):
                pool.sem_inc(added, 2)

                def body(g, u, last):
                    ts = bass.ds(g * GT, GT)
                    pool.wait_ge(weighted, g + 1)
                    pool.tensor_tensor(core.X[:, ts, :], core.X[:, ts, :], part[:, u], ALU.add).then_inc(added, 1)
                steps(pool, GROUPS, 2, 0, body)


def causal_single(core, name, qw, kw, vw):
    nc = core.nc
    NQ = BTILES
    SCALE = float(D) ** -0.5
    with ExitStack() as ctx:
        sb = lambda n, s, dt=F32: core.sb(f"{name}_{n}", s, dt, ctx)
        ps = lambda n, s: core.ps(f"{name}_{n}", s, F32, ctx)
        sem = lambda n: core.sem(f"{name}_{n}")
        Wq, Wk, Wv = sb("Wq", [D, D]), sb("Wk", [D, D]), sb("Wv", [D, D])
        hide = sb("hide", [P, P])
        nrm, uT, qT, kT, V = (sb(n, [P, SEQ]) for n in ("nrm", "uT", "qT", "kT", "V"))
        probs, pT = sb("probs", [P, 2, SEQ]), sb("pT", [P, SEQ])
        top, ntop, rowsum, inv = (sb(n, [P, NQ]) for n in ("top", "ntop", "rowsum", "inv"))
        pS, pT_, pO = ps("pS", [P, 2, SEQ]), ps("pTp", [P, SEQ]), ps("pO", [P, 2, 512])
        names = ("loaded hide_made normed turned u_copied q_made q_copied k_made k_copied v_made v_copied "
                 "s_made maxed scaled exped t_made t_copied o_made inverted added").split()
        s = dict(zip(names, map(sem, names)))
        def loads(sp):
            for t, a in ((Wq, qw), (Wk, kw), (Wv, vw)):
                sp.dma_start(t[:], a).then_inc(s["loaded"], 16)

        stream_stats(core, f"{name}_in", loads=loads)
        with nc.Block() as block:
            @block.gpsimd
            def _(pool):
                pool.memset(hide[:], 0.0).then_inc(s["hide_made"], 1)
                pool.wait_ge(s["hide_made"], 1)
                pool.affine_select(out=hide[:], in_=hide[:], compare_op=ALU.is_ge, fill=-1e30, base=0,
                                   pattern=[[-1, P]], channel_multiplier=1).then_inc(s["hide_made"], 1)

            @block.vector
            def _(dve):
                dve.sem_inc(s["t_copied"], 1)
                dve.sem_inc(s["added"], 2)
                with dve.Fori(0, BATCH) as b:
                    for k in range(BTILES):
                        t = bass.ds(b * BTILES + k, 1)
                        ins = dve.tensor_scalar(nrm[:, bass.ts(k, D)], core.X[:, t, :].rearrange("p t d -> p (t d)"),
                                                core.rstd[:, t], core.shift[:, t], ALU.mult, ALU.add)
                    ins.then_inc(s["normed"], 1)
                    dve.wait_ge(s["k_made"], b + 1)
                    dve.tensor_copy(kT[:], pS[:, 1, :]).then_inc(s["k_copied"], 1)

                    def biggest(qt):
                        it = b * NQ + qt
                        dve.wait_ge(s["s_made"], it + 1)
                        dve.tensor_reduce(top[:, qt:qt + 1], pS[:, qt % 2, 0:P * (qt + 1)], AX.X, ALU.max)\
                           .then_inc(s["maxed"], 1)
                        dve.wait_ge(s["maxed"], it + 1)
                        dve.tensor_scalar(ntop[:, qt:qt + 1], top[:, qt:qt + 1], -SCALE, None, ALU.mult)\
                           .then_inc(s["scaled"], 1)

                    biggest(0)
                    for qt in range(NQ):
                        it = b * NQ + qt
                        if qt < NQ - 1:
                            biggest(qt + 1)
                        dve.wait_ge(s["t_made"], it + 3)
                        dve.wait_ge(s["o_made"], it + 1)
                        dve.tensor_copy(pT[:, 0:P * (qt + 1)], pT_[:, 0:P * (qt + 1)]).then_inc(s["t_copied"], 1)
                        dve.wait_ge(s["exped"], it + 3)
                        dve.reciprocal(inv[:, qt:qt + 1], rowsum[:, qt:qt + 1]).then_inc(s["inverted"], 1)
                        dve.wait_ge(s["inverted"], it + 1)
                        dve.wait_ge(s["o_made"], it + 2)
                        x = core.X[:, bass.ds(it, 1), :].rearrange("p t d -> p (t d)")
                        dve.scalar_tensor_tensor(out=x, in0=pO[:, qt % 2, 0:D], scalar=inv[:, qt:qt + 1], in1=x,
                                                 op0=ALU.mult, op1=ALU.add).then_inc(s["added"], 1)
                    dve.wait_ge(s["added"], b * NQ + NQ + 2)
                    row_moments(dve, core, core.X, b * NQ, NQ)

            @block.scalar
            def _(act):
                act.sem_inc(s["exped"], 2)
                with act.Fori(0, BATCH) as b:
                    act.wait_ge(s["turned"], b + 1)
                    act.activation(uT[:], pS[:, 0, :], ACT.Copy).then_inc(s["u_copied"], 1)
                    act.wait_ge(s["q_made"], b + 1)
                    act.activation(qT[:], pS[:, 0, :], ACT.Copy).then_inc(s["q_copied"], 1)
                    act.wait_ge(s["v_made"], b + 1)
                    act.activation(V[:], pT_[:], ACT.Copy).then_inc(s["v_copied"], 1)
                    for qt in range(NQ):
                        it = b * NQ + qt
                        act.wait_ge(s["scaled"], it + 1)
                        act.wait_ge(s["t_made"], it + 1)
                        w = P * (qt + 1)
                        act.activation(probs[:, qt % 2, 0:w], pS[:, qt % 2, 0:w], ACT.Exp, bias=ntop[:, qt:qt + 1],
                                       scale=SCALE, accum_out=rowsum[:, qt:qt + 1]).then_inc(s["exped"], 1)

            @block.tensor
            def _(pe):
                pe.sem_inc(s["t_made"], 2)
                pe.sem_inc(s["o_made"], 1)
                pe.wait_ge(s["loaded"], 48)
                pe.wait_ge(s["hide_made"], 2)
                with pe.Fori(0, BATCH) as b:
                    halves = (slice(0, 512), slice(512, SEQ))
                    pe.wait_ge(s["normed"], b + 1)
                    pe.wait_ge(s["exped"], b * NQ + 2)
                    for k in range(BTILES):
                        ins = pe.transpose(pS[:, 0, bass.ts(k, P)], nrm[:, bass.ts(k, P)], core.ident[:])
                    ins.then_inc(s["turned"], 1)
                    pe.wait_ge(s["u_copied"], b + 1)
                    for h in halves:
                        ins = pe.matmul(pS[:, 0, h], Wq[:], uT[:, h], start=True, stop=True)
                    ins.then_inc(s["q_made"], 1)
                    for h in halves:
                        ins = pe.matmul(pS[:, 1, h], Wk[:], uT[:, h], start=True, stop=True)
                    ins.then_inc(s["k_made"], 1)
                    pe.wait_ge(s["t_copied"], b * NQ + 1)
                    for k in range(BTILES):
                        ins = pe.matmul(pT_[:, bass.ts(k, P)], uT[:, bass.ts(k, P)], Wv[:], start=True, stop=True)
                    ins.then_inc(s["v_made"], 1)
                    pe.wait_ge(s["q_copied"], b + 1)
                    pe.wait_ge(s["k_copied"], b + 1)

                    def scores(qt):
                        pe.wait_ge(s["exped"], b * NQ + qt + 1)
                        w = P * (qt + 1)
                        for c in range(0, w, 512):
                            n = min(512, w - c)
                            last = c + n == w
                            ins = pe.matmul(pS[:, qt % 2, c:c + n], qT[:, bass.ts(qt, P)], kT[:, c:c + n],
                                            start=True, stop=not last, skip_group_check=True)
                        pe.matmul(pS[:, qt % 2, w - P:w], core.ident[:], hide[:], start=False, stop=True,
                                  skip_group_check=True).then_inc(s["s_made"], 1)

                    scores(0)
                    for qt in range(NQ):
                        it = b * NQ + qt
                        if qt < NQ - 1:
                            scores(qt + 1)
                        pe.wait_ge(s["exped"], it + 3)
                        if qt == 0:
                            pe.wait_ge(s["v_copied"], b + 1)
                        pe.wait_ge(s["t_copied"], it + 1)
                        for k in range(qt + 1):
                            ins = pe.transpose(pT_[:, bass.ts(k, P)], probs[:, qt % 2, bass.ts(k, P)], core.ident[:])
                        ins.then_inc(s["t_made"], 1)
                        pe.wait_ge(s["t_copied"], it + 2)
                        pe.wait_ge(s["added"], it + 1)
                        for k in range(qt + 1):
                            ins = pe.matmul(pO[:, qt % 2, 0:D], pT[:, bass.ts(k, P)], V[:, bass.ts(k, D)],
                                            start=(k == 0), stop=(k == qt))
                        ins.then_inc(s["o_made"], 1)


class Experts:

    NE, TOP, FFN = EXPERTS, CHOICES, 512
    CAP = CAPACITY
    ROWS = EXPERT_ROWS
    HD, NKV = 8, 8
    QW = 256

    def __init__(self, core, w):
        nc = core.nc
        self.ln1_weight, self.ln1_bias = w["moe_ln1_weight"], w["moe_ln1_bias"]
        self.ln2_weight, self.ln2_bias = w["moe_ln2_weight"], w["moe_ln2_bias"]
        self.qkv_t, self.proj_t, self.router_weight = w["moe_qkv_t"], w["moe_proj_t"], w["moe_router_weight"]
        self.moe_w1, self.moe_w2 = w["moe_w1"], w["moe_w2"]
        self.rows_in = nc.dram_tensor("rows_in", (self.ROWS + self.TOP * TOKENS, D + 1), F32, kind="Internal").ap()
        self.rows_out = nc.dram_tensor("rows_out", (self.TOP * TOKENS + self.CAP, D), F32, kind="Internal").ap()
        core.rows_in, core.rows_out = self.rows_in, self.rows_out


def experts(core, name, ex, out=None):
    nc = core.nc
    NE = ex.NE
    sem = lambda n: core.sem(f"{name}_{n}")
    with ExitStack() as top:
        HA = core.sb(f"{name}_HA", [P, TILES, D], F32, top)
        gate = core.sb(f"{name}_gate", [P, 2, TILES], F32, top)
        slot_in = core.sb(f"{name}_slot_in", [P, 2, TILES], U32, top)
        choice = core.sb(f"{name}_choice", [P, 2, TILES], F32, top)
        count = core.sb(f"{name}_count", [P, NE], F32, top)
        wrow, brow = (core.sb(f"{name}_{n}", [P, D], F32, top) for n in ("ln2w", "ln2b"))
        R = core.sb(f"{name}_R", [D, NE], F32, top)
        routing_loaded = sem("routing_loaded")

        def routing_loads(sp):
            sp.dma_start(wrow[:], ex.ln2_weight.rearrange("(o d) -> o d", o=1).to_broadcast([P, D])).then_inc(routing_loaded, 16)
            sp.dma_start(brow[:], ex.ln2_bias.rearrange("(o d) -> o d", o=1).to_broadcast([P, D])).then_inc(routing_loaded, 16)
            sp.dma_start(R[:], ex.router_weight).then_inc(routing_loaded, 16)

        row_attention(core, name, ex, HA, routing_loads)
        stream_stats(core, f"{name}_ha")
        with ExitStack() as ctx:
            X2 = core.sb(f"{name}_X2", [P, TILES, D + 1], F32, ctx)
            logits = core.sb(f"{name}_logits", [P, TILES, NE], F32, ctx)
            route = Routing(core, name, ex, ctx, logits, gate, slot_in, choice, count)
            sent = [[[sem(f"sent{h}{c}{q}") for q in range(2)] for c in range(2)] for h in range(2)]
            numbered = sem("numbered")
            HALF, PART = TILES // 2, TILES // 4

            def send(pool, h, c):
                for q in range(2):
                    first = h * HALF + q * PART
                    tiles = slice(first, first + PART)
                    if c == 1:
                        pool.wait_ge(sent[h][0][q], 16 * PART)
                    pool.tensor_copy(X2[:, tiles, D:D + 1], choice[:, c, tiles].rearrange("p (t o) -> p t o", o=1))\
                        .then_inc(numbered, 1)
                    pool.wait_ge(numbered, 4 * h + 2 * c + q + 1)
                    for t in range(first, first + PART):
                        pool.indirect_dma_start(
                            out=ex.rows_in, out_offset=bass.IndirectOffsetOnAxis(ap=slot_in[:, c, t:t + 1], axis=0),
                            in_=X2[:, t, :], in_offset=None).then_inc(sent[h][c][q], 16)

            def send_first_choices(pool):
                pool.wait_ge(core.cleared, 16 * core.clears)
                send(pool, 0, 0)

            router(core, name, ex, HA, X2, logits, wrow, brow, R, routing_loaded, 0, route.constants)
            route.half(0)
            router(core, name, ex, HA, X2, logits, wrow, brow, R, routing_loaded, 1, send_first_choices)
            route.half(1, lambda pool: send(pool, 0, 1))
            with nc.Block() as block:
                @block.gpsimd
                def _(pool):
                    send(pool, 1, 0)
                    send(pool, 1, 1)
                    for h in range(2):
                        for q in range(2):
                            pool.wait_ge(sent[h][1][q], 16 * PART)
        expert_products(core, name, ex, count)
        with ExitStack() as ctx:
            G = core.sb(f"{name}_G", [P, TILES, 2, D], F32, ctx)
            fetched, chain = [sem(f"fetched{q}") for q in range(4)], sem("join_chain")
            joined, stored = sem("joined"), sem("stored")
            outputs = ex.rows_out[0:ex.TOP * TOKENS, :].rearrange("(t p c) d -> p t c d", p=P, c=2)
            with nc.Block() as block:
                @block.vector
                def _(dve):
                    step = Chain(dve, chain)
                    step(dve.tensor_tensor(core.X[:], core.X[:], HA[:], ALU.add))
                    for q in range(4):
                        dve.wait_ge(fetched[q], 16)
                        for c in range(2):
                            for t in range(8 * q, 8 * q + 8):
                                ins = dve.scalar_tensor_tensor(out=core.X[:, t, :], in0=G[:, t, c, :],
                                                               scalar=gate[:, c, t:t + 1], in1=core.X[:, t, :],
                                                               op0=ALU.mult, op1=ALU.add)
                            step(ins)
                        if out is None:
                            row_moments(dve, core, core.X, 8 * q, 8)
                        else:
                            dve.sem_inc(joined, 1)

                @block.sync
                def _(sp):
                    for q in range(4):
                        sp.dma_start(G[:, 8 * q:8 * q + 8], outputs[:, 8 * q:8 * q + 8]).then_inc(fetched[q], 16)
                    if out is not None:
                        rows = out.rearrange("(t p) d -> p t d", p=P)
                        for q in range(4):
                            sp.wait_ge(joined, q + 1)
                            sp.dma_start(rows[:, 8 * q:8 * q + 8, :], core.X[:, 8 * q:8 * q + 8, :]).then_inc(stored, 16)
                        sp.wait_ge(stored, 16 * 4)


def row_attention(core, name, ex, HA, routing_loads):
    nc = core.nc
    HD, NKV, QW = ex.HD, ex.NKV, ex.QW
    with ExitStack() as ctx:
        sb = lambda n, s, dt=F32: core.sb(f"{name}_{n}", s, dt, ctx)
        ps = lambda n, s: core.ps(f"{name}_{n}", s, F32, ctx)
        sem = lambda n: core.sem(f"{name}_{n}")
        W, Wp = sb("Wqkv", [D, QW]), sb("Wproj", [D, D])
        wcol, bcol, bwide = sb("ln1w", [D, 1]), sb("ln1b", [D, 1]), sb("bwide", [D, P])
        bias = sb("qkvbias", [P, QW])
        QKV = sb("QKV", [P, TILES, QW])
        ATT = sb("ATT", [P, TILES, D])
        loaded, widened, bias_made, bias_kept, folded = map(sem, ("loaded", "widened", "bias_made", "bias_kept", "folded"))
        with ExitStack() as sub:
            nrm = core.sb(f"{name}_nrm", [P, 2, GT, D], F32, sub)
            uT = core.sb(f"{name}_uT", [P, 2, GT * P], F32, sub)
            pT = core.ps(f"{name}_pT", [P, 2, GT * P], F32, sub)
            pY = core.ps(f"{name}_pY", [P, 2, GT * QW], F32, sub)
            normed, turned, copied, product, kept = map(sem, ("q_normed", "q_turned", "q_copied", "q_product", "q_kept"))
            def loads(sp):
                sp.dma_start(W[:], ex.qkv_t).then_inc(loaded, 16)
                sp.dma_start(Wp[:], ex.proj_t).then_inc(loaded, 16)
                sp.dma_start(wcol[:], ex.ln1_weight.rearrange("(d o) -> d o", o=1)).then_inc(loaded, 16)
                sp.dma_start(bcol[:], ex.ln1_bias.rearrange("(d o) -> d o", o=1)).then_inc(loaded, 16)
                routing_loads(sp)

            stream_stats(core, f"{name}_in", twice=True, loads=loads)
            with nc.Block() as block:
                @block.vector
                def _(dve):
                    dve.sem_inc(kept, 2)
                    dve.wait_ge(loaded, 64)
                    dve.tensor_copy(bwide[:], bcol[:].to_broadcast([D, P])).then_inc(widened, 1)
                    dve.wait_ge(bias_made, 1)
                    dve.tensor_copy(bias[:], pY[:, 0, 0:QW]).then_inc(bias_kept, 1)
                    dve.wait_ge(bias_kept, 1)
                    dve.tensor_scalar(W[:], W[:], wcol[:, 0:1], None, ALU.mult).then_inc(folded, 1)

                    def body(g, u, last):
                        dve.wait_ge(product, g + 3)
                        ts = bass.ds(g * GT, GT)
                        dve.tensor_tensor(QKV[:, ts, :], pY[:, u, :].rearrange("p (t c) -> p t c", c=QW),
                                          bias[:].rearrange("p (o c) -> p o c", o=1).to_broadcast([P, GT, QW]), ALU.add)\
                           .then_inc(kept, 1)
                    steps(dve, GROUPS, 2, 2, body)

                @block.tensor
                def _(pe):
                    pe.sem_inc(turned, 2)
                    pe.sem_inc(product, 2)
                    pe.wait_ge(widened, 1)
                    pe.matmul(pY[:, 0, 0:QW], bwide[:], W[:], start=True, stop=True).then_inc(bias_made, 1)
                    pe.wait_ge(folded, 1)

                    def turn(g, u):
                        pe.wait_ge(normed, g + 1)
                        pe.wait_ge(copied, g + 1)
                        for j in range(GT):
                            ins = pe.transpose(pT[:, u, bass.ts(j, P)], nrm[:, u, j, :], core.ident[:])
                        ins.then_inc(turned, 1)

                    turn(0, 0)

                    def body(g, u, last):
                        if not last:
                            turn(g + 1, 1 - u)
                        pe.wait_ge(copied, g + 3)
                        pe.wait_ge(kept, g + 1)
                        for j in range(GT):
                            ins = pe.matmul(pY[:, u, bass.ts(j, QW)], uT[:, u, bass.ts(j, P)], W[:], start=True, stop=True)
                        ins.then_inc(product, 1)
                    steps(pe, GROUPS, 2, 2, body)

                @block.scalar
                def _(act):
                    act.sem_inc(copied, 2)

                    def norm(g, u):
                        for j in range(GT):
                            k = bass.ds(g * GT + j, 1)
                            ins = act.activation(nrm[:, u, j, :], core.X[:, k, :].rearrange("p o d -> p (o d)"), ACT.Identity,
                                                 bias=core.shift2[:, k], scale=core.rstd2[:, k])
                        ins.then_inc(normed, 1)

                    norm(0, 0)
                    norm(1, 1)

                    def body(g, u, last):
                        act.wait_ge(turned, g + 3)
                        act.wait_ge(product, g + 1)
                        act.activation(uT[:, u, :], pT[:, u, :], ACT.Copy).then_inc(copied, 1)
                        if follows(g, 2):
                            norm(g + 2, u)
                    steps(act, GROUPS, 2, 2, body)

        with ExitStack() as sub:
            XW = BATCH * NKV * HD
            prod = core.sb(f"{name}_prod", [P, 2, BATCH, 2, XW], F32, sub)
            vprod = core.sb(f"{name}_vprod", [P, 2, BATCH, 2, XW], F32, sub)
            sc = core.sb(f"{name}_sc", [P, 2, BATCH * 2, BATCH * NKV], F32, sub)
            ew = core.sb(f"{name}_ew", [P, 2, BATCH * 2, BATCH * NKV], F32, sub)
            mx, den = (core.sb(f"{name}_{n}", [P, 2, BATCH * 2, NKV], F32, sub) for n in ("mx", "den"))
            qv = QKV[:].rearrange("p (s j) (g c) -> p s j g c", s=BATCH, c=4 * HD)
            av = ATT[:].rearrange("p (s j) (g r d) -> p s j g r d", s=BATCH, r=2, d=HD)
            chain, multiplied, shifted, raised, weighted, spread, dve_spread = map(
                sem, ("a_chain", "a_multiplied", "a_shifted", "a_raised", "a_weighted", "a_spread", "a_dve_spread"))

            def weighted_values(eng, j, u, s, r):
                n = s + 1
                w = ew[:, u, 2 * s + r, 0:n * NKV].rearrange("p (t g o) -> p t g o", g=NKV, o=1)\
                    .to_broadcast([P, n, NKV, HD])
                v = qv[:, 0:n, bass.ds(j, 1), :, 3 * HD:4 * HD].rearrange("p t j g d -> p (t j) g d")
                out = vprod[:, u, s, r, 0:n * NKV * HD].rearrange("p (t g d) -> p t g d", t=n, g=NKV)
                return eng.tensor_tensor(out, w, v, ALU.mult)

            rows = [(s, r) for s in range(BATCH) for r in range(2)]
            DVE_ROWS = rows[-1:]
            with nc.Block() as block:
                @block.gpsimd
                def _(pool):
                    def multiply(j, u):
                        J = bass.ds(j, 1)
                        for s in range(BATCH):
                            for r in range(2):
                                n = s + 1
                                q = qv[:, s, J, :, r * HD:(r + 1) * HD].to_broadcast([P, n, NKV, HD])
                                k = qv[:, 0:n, J, :, 2 * HD:3 * HD].rearrange("p t j g d -> p (t j) g d")
                                out = prod[:, u, s, r, 0:n * NKV * HD].rearrange("p (t g d) -> p t g d", t=n, g=NKV)
                                ins = pool.tensor_tensor(out, q, k, ALU.mult)
                        ins.then_inc(multiplied, 1)

                    def weigh(j, u):
                        pool.wait_ge(weighted, j + 1)
                        for s, r in rows:
                            if (s, r) not in DVE_ROWS:
                                ins = weighted_values(pool, j, u, s, r)
                        ins.then_inc(spread, 1)

                    multiply(0, 0)
                    multiply(1, 1)
                    with pool.Fori(0, (BTILES - 2) // 2) as i:
                        for u in range(2):
                            weigh(2 * i + u, u)
                            multiply(2 * i + u + 2, u)
                    weigh(BTILES - 2, 0)
                    weigh(BTILES - 1, 1)

                @block.vector
                def _(dve):
                    dve.memset(sc[:], -1e30).then_inc(chain, 1)
                    dve.wait_ge(chain, 1)
                    v4 = lambda t: t.rearrange("p a (t g) -> p a t g", g=NKV)
                    wide = lambda t: t.rearrange("p a (o g) -> p a o g", o=1).to_broadcast([P, BATCH * 2, BATCH, NKV])

                    def scores(j, u, step):
                        dve.wait_ge(multiplied, j + 1)
                        for s in range(BATCH):
                            n = s + 1
                            view = prod[:, u, s, :, 0:n * NKV * HD].rearrange("p r (x d) -> p r x d", d=HD)
                            ins = dve.tensor_reduce(sc[:, u, 2 * s:2 * s + 2, 0:n * NKV], view, AX.X, ALU.add)
                        step(ins)
                        step(dve.tensor_reduce(mx[:, u], sc[:, u].rearrange("p a (t g) -> p a g t", g=NKV), AX.X, ALU.max))
                        dve.tensor_tensor(v4(ew[:, u]), v4(sc[:, u]), wide(mx[:, u]), ALU.subtract).then_inc(shifted, 1)

                    def weights(j, u, step):
                        dve.wait_ge(raised, j + 1)
                        step(dve.tensor_reduce(den[:, u], ew[:, u].rearrange("p a (t g) -> p a g t", g=NKV), AX.X, ALU.add))
                        step(dve.reciprocal(den[:, u], den[:, u]))
                        dve.tensor_tensor(v4(ew[:, u]), v4(ew[:, u]), wide(den[:, u]), ALU.mult).then_inc(weighted, 1)
                        dve.wait_ge(weighted, j + 1)
                        for s, r in DVE_ROWS:
                            ins = weighted_values(dve, j, u, s, r)
                        ins.then_inc(dve_spread, 1)

                    def gathered(j, u):
                        J = bass.ds(j, 1)
                        dve.wait_ge(spread, j + 1)
                        dve.wait_ge(dve_spread, j + 1)
                        for s in range(BATCH):
                            for r in range(2):
                                n = s + 1
                                view = vprod[:, u, s, r, 0:n * NKV * HD].rearrange("p (t g d) -> p g d t", t=n, g=NKV)
                                dve.tensor_reduce(av[:, s, J, :, r, :].rearrange("p j g d -> p (j g) d"), view, AX.X, ALU.add)

                    step = Chain(dve, chain, 1)
                    scores(0, 0, step)
                    weights(0, 0, step)
                    scores(1, 1, step)
                    with dve.Fori(0, (BTILES - 2) // 2) as i:
                        for u in range(2):
                            j = 2 * i + u
                            step = Chain(dve, chain, 1 + 6 + 4 * j)
                            weights(j + 1, 1 - u, step)
                            scores(j + 2, u, step)
                            gathered(j, u)
                    step = Chain(dve, chain, 1 + 6 + 4 * (BTILES - 2))
                    weights(BTILES - 1, 1, step)
                    gathered(BTILES - 2, 0)
                    gathered(BTILES - 1, 1)

                @block.scalar
                def _(act):
                    with act.Fori(0, BTILES // 2) as i:
                        for u in range(2):
                            act.wait_ge(shifted, 2 * i + u + 1)
                            act.activation(ew[:, u], ew[:, u], ACT.Exp, scale=HD ** -0.5).then_inc(raised, 1)

        with ExitStack() as sub:
            att = core.sb(f"{name}_att", [P, 2, GT, D], F32, sub)
            hid = core.sb(f"{name}_hid", [P, 2, GT, D], F32, sub)
            aT = core.sb(f"{name}_attT", [P, 2, GT * P], F32, sub)
            pT = core.ps(f"{name}_pT2", [P, 2, GT * P], F32, sub)
            pY = core.ps(f"{name}_pY2", [P, 2, GT * P], F32, sub)
            staged, turned, copied, product, kept, hidden = map(
                sem, ("p_staged", "p_turned", "p_copied", "p_product", "p_kept", "p_hidden"))
            with nc.Block() as block:
                @block.gpsimd
                def _(pool):
                    def body(g, u, last):
                        pool.wait_ge(turned, g + 1)
                        pool.tensor_copy(att[:, u], ATT[:, bass.ds(g * GT, GT), :]).then_inc(staged, 1)
                    steps(pool, GROUPS, 2, 0, body)

                @block.vector
                def _(dve):
                    dve.sem_inc(kept, 2)

                    def body(g, u, last):
                        dve.wait_ge(kept, g + 1)
                        normalise(dve, core, hid[:, u], g).then_inc(hidden, 1)
                        dve.wait_ge(hidden, g + 1)
                        dve.wait_ge(product, g + 3)
                        dve.tensor_tensor(HA[:, bass.ds(g * GT, GT), :], hid[:, u],
                                          pY[:, u, :].rearrange("p (t d) -> p t d", d=D), ALU.add).then_inc(kept, 1)
                        dve.wait_ge(kept, g + 3)
                        row_moments(dve, core, HA, g * GT, GT)
                    steps(dve, GROUPS, 2, 0, body)

                @block.tensor
                def _(pe):
                    pe.sem_inc(turned, 2)
                    pe.sem_inc(product, 2)

                    def turn(g, u):
                        pe.wait_ge(staged, g + 1)
                        pe.wait_ge(copied, g + 1)
                        for j in range(GT):
                            ins = pe.transpose(pT[:, u, bass.ts(j, P)], att[:, u, j, :], core.ident[:])
                        ins.then_inc(turned, 1)

                    turn(0, 0)

                    def body(g, u, last):
                        if not last:
                            turn(g + 1, 1 - u)
                        pe.wait_ge(copied, g + 3)
                        pe.wait_ge(kept, g + 1)
                        for j in range(GT):
                            ins = pe.matmul(pY[:, u, bass.ts(j, P)], aT[:, u, bass.ts(j, P)], Wp[:], start=True, stop=True)
                        ins.then_inc(product, 1)
                    steps(pe, GROUPS, 2, 2, body)

                @block.scalar
                def _(act):
                    act.sem_inc(copied, 2)

                    def body(g, u, last):
                        act.wait_ge(turned, g + 3)
                        act.wait_ge(product, g + 1)
                        act.activation(aT[:, u, :], pT[:, u, :], ACT.Copy).then_inc(copied, 1)
                    steps(act, GROUPS, 2, 0, body)


def router(core, name, ex, HA, X2, logits, wrow, brow, R, loaded, half, beside):
    nc, NE = core.nc, ex.NE
    COUNT = GROUPS // 2
    START = half * COUNT
    with ExitStack() as ctx:
        nrm = core.sb(f"{name}_rnrm{half}", [P, 2, GT, D], F32, ctx)
        xT = core.sb(f"{name}_rxT{half}", [P, 2, GT * P], F32, ctx)
        pT = core.ps(f"{name}_rpT{half}", [P, 2, GT * P], F32, ctx)
        pL = core.ps(f"{name}_rpL{half}", [P, 2, 512], F32, ctx)
        turned, copied, product, chain, kept, made = map(
            lambda n: core.sem(f"{name}_r{half}_{n}"), ("turned", "copied", "product", "chain", "kept", "made"))
        wide = lambda t: t[:].rearrange("p (o d) -> p o d", o=1).to_broadcast([P, GT, D])
        with nc.Block() as block:
            @block.gpsimd
            def _(pool):
                beside(pool)

            @block.vector
            def _(dve):
                dve.sem_inc(kept, 2)
                dve.wait_ge(loaded, 48)

                def make(g, u):
                    step = Chain(dve, chain, 2 * g)
                    tiles = bass.ds((START + g) * GT, GT)
                    for j in range(GT):
                        k = bass.ds((START + g) * GT + j, 1)
                        ins = dve.tensor_scalar(nrm[:, u, j, :], HA[:, k, :], core.rstd[:, k], core.shift[:, k],
                                                ALU.mult, ALU.add)
                    step(ins)
                    step(dve.tensor_tensor(nrm[:, u], nrm[:, u], wide(wrow), ALU.mult))
                    dve.tensor_tensor(X2[:, tiles, 0:D], nrm[:, u], wide(brow), ALU.add).then_inc(made, 1)

                make(0, 0)
                make(1, 1)

                def body(g, u, last):
                    if follows(g, 2, COUNT):
                        dve.wait_ge(made, g + 1)
                        make(g + 2, u)
                    dve.wait_ge(product, g + 3)
                    dve.tensor_copy(logits[:, bass.ds((START + g) * GT, GT), :],
                                    pL[:, u, 0:GT * NE].rearrange("p (t e) -> p t e", e=NE)).then_inc(kept, 1)
                steps(dve, COUNT, 2, 2, body)

            @block.scalar
            def _(act):
                act.sem_inc(copied, 2)

                def body(g, u, last):
                    act.wait_ge(turned, g + 3)
                    act.wait_ge(product, g + 1)
                    act.activation(xT[:, u, :], pT[:, u, :], ACT.Copy).then_inc(copied, 1)
                steps(act, COUNT, 2, 0, body)

            @block.tensor
            def _(pe):
                pe.sem_inc(turned, 2)
                pe.sem_inc(product, 2)
                pe.wait_ge(loaded, 48)

                def turn(g, u):
                    pe.wait_ge(made, g + 1)
                    pe.wait_ge(copied, g + 1)
                    for j in range(GT):
                        ins = pe.transpose(pT[:, u, bass.ts(j, P)],
                                           X2[:, bass.ds((START + g) * GT + j, 1), 0:D].rearrange("p o d -> p (o d)"),
                                           core.ident[:])
                    ins.then_inc(turned, 1)

                turn(0, 0)

                def body(g, u, last):
                    if not last:
                        turn(g + 1, 1 - u)
                    pe.wait_ge(copied, g + 3)
                    pe.wait_ge(kept, g + 1)
                    for j in range(GT):
                        ins = pe.matmul(pL[:, u, bass.ts(j, NE)], xT[:, u, bass.ts(j, P)], R[:], start=True, stop=True)
                    ins.then_inc(product, 1)
                steps(pe, COUNT, 2, 2, body)


class Routing:

    def __init__(self, core, name, ex, ctx, logits, gate, slot_in, choice, count):
        sb = lambda n, s, dt=F32: core.sb(f"{name}_{n}", s, dt, ctx)
        self.core, self.name, self.ex = core, name, ex
        self.logits, self.gate, self.slot_in, self.choice, self.count = logits, gate, slot_in, choice, count
        self.before, self.ones = sb("before", [P, P]), sb("ones", [P, P])
        self.e8i, self.tri = sb("e8i", [P, ex.NE], I32), sb("tri", [P, 2, TILES], I32)
        self.e8, self.ebase, self.trash = sb("e8", [P, ex.NE]), sb("ebase", [P, ex.NE]), sb("trash", [P, 2, TILES])
        self.consts = core.sem(f"{name}_g_consts")

    def constants(self, pool):
        ex, ones, before, consts = self.ex, self.ones, self.before, self.consts
        pool.memset(ones[:], 1.0).then_inc(consts, 1)
        pool.memset(before[:], 1.0).then_inc(consts, 1)
        pool.wait_ge(consts, 2)
        pool.affine_select(out=before[:], in_=before[:], compare_op=ALU.is_gt, fill=0.0, base=0,
                           pattern=[[1, P]], channel_multiplier=-1).then_inc(consts, 1)
        pool.iota(self.e8i[:], [[1, ex.NE]], base=0, channel_multiplier=0).then_inc(consts, 1)
        pool.iota(self.tri[:], [[1, 2], [2 * P, TILES]], base=ex.ROWS, channel_multiplier=2).then_inc(consts, 1)

    def half(self, h, beside=None):
        core, name, ex, nc = self.core, self.name, self.ex, self.core.nc
        NE, CAP = ex.NE, ex.CAP
        TH = TILES // 2
        TE = TH * NE
        tiles = slice(h * TH, (h + 1) * TH)
        logits, gate, slot_in, choice, count = self.logits, self.gate, self.slot_in, self.choice, self.count
        before, ones, e8, ebase, trash, consts = self.before, self.ones, self.e8, self.ebase, self.trash, self.consts
        with ExitStack() as ctx:
            sb = lambda n, s, dt=F32: core.sb(f"{name}_{n}{h}", s, dt, ctx)
            big = [sb(f"big{k}_", [P, TH, NE]) for k in range(6)]
            p, hot1, hot2, sel, tmp, within = big
            tot, cum, one = sb("tot", [P, NE, TH]), sb("cum", [P, NE, TH]), sb("one", [P, TE])
            m = [sb(f"m{k}_", [P, TH]) for k in range(6)]
            m1, m2, idx, total, keep, slot = m
            chose = sb("chose", [P, NE])
            pB, pA = (core.ps(f"{name}_{n}{h}", [P, 512], F32, ctx) for n in ("pB", "pA"))
            chain, shifted, raised, chosen, counted = map(
                lambda n: core.sem(f"{name}_g{h}_{n}"), ("chain", "shifted", "raised", "chosen", "counted"))
            col = lambda t: t[:].rearrange("p (t o) -> p t o", o=1).to_broadcast([P, TH, NE])
            erow = lambda t: t[:].rearrange("p (o e) -> p o e", o=1).to_broadcast([P, TH, NE])
            with nc.Block() as block:
                if beside is not None:
                    @block.gpsimd
                    def _(pool):
                        beside(pool)

                @block.scalar
                def _(act):
                    act.wait_ge(shifted, 1)
                    act.activation(p[:], p[:], ACT.Exp).then_inc(raised, 1)

                @block.tensor
                def _(pe):
                    pe.wait_ge(chosen, 1)
                    pe.matmul(pB[:, 0:TE], before[:], sel[:].rearrange("p t e -> p (t e)"), start=True, stop=True)
                    pe.matmul(pA[:, 0:TE], ones[:], sel[:].rearrange("p t e -> p (t e)"), start=True, stop=True)\
                      .then_inc(counted, 1)

                @block.vector
                def _(dve):
                    step = Chain(dve, chain)
                    if h == 0:
                        dve.wait_ge(consts, 5)
                        step(dve.tensor_copy(e8[:], self.e8i[:]))
                        step(dve.tensor_copy(trash[:], self.tri[:]))
                        step(dve.tensor_scalar(choice[:], trash[:], float(ex.ROWS), None, ALU.subtract))
                        step(dve.tensor_scalar(ebase[:], e8[:], float(CAP), None, ALU.mult))
                        step(dve.tensor_scalar(e8[:], e8[:], float(NE), None, ALU.subtract))
                        step(dve.memset(count[:], 0.0))
                    step(dve.memset(one[:], 1.0))
                    step(dve.tensor_reduce(m1[:], logits[:, tiles], AX.X, ALU.max))
                    dve.tensor_tensor(p[:], logits[:, tiles], col(m1), ALU.subtract).then_inc(shifted, 1)
                    dve.wait_ge(raised, 1)
                    for best, hot in ((m1, hot1), (m2, hot2)):
                        step(dve.tensor_reduce(best[:], p[:], AX.X, ALU.max))
                        step(dve.tensor_tensor(tmp[:], p[:], col(best), ALU.is_equal))
                        step(dve.tensor_tensor(tmp[:], tmp[:], erow(e8), ALU.mult))
                        step(dve.tensor_reduce(idx[:], tmp[:], AX.X, ALU.min))
                        step(dve.tensor_tensor(hot[:], erow(e8), col(idx), ALU.is_equal))
                        if hot is hot1:
                            step(dve.scalar_tensor_tensor(out=p[:].rearrange("p t e -> p (t e)"),
                                                          in0=hot[:].rearrange("p t e -> p (t e)"), scalar=-2.0,
                                                          in1=p[:].rearrange("p t e -> p (t e)"), op0=ALU.mult, op1=ALU.add))
                    dve.tensor_tensor(sel[:], hot1[:], hot2[:], ALU.add).then_inc(chosen, 1)
                    step(dve.tensor_tensor(total[:], m1[:], m2[:], ALU.add))
                    step(dve.reciprocal(total[:], total[:]))
                    dve.tensor_tensor(gate[:, 0, tiles], m1[:], total[:], ALU.mult)
                    step(dve.tensor_tensor(gate[:, 1, tiles], m2[:], total[:], ALU.mult))
                    dve.wait_ge(counted, 1)
                    step(dve.tensor_copy(tot[:].rearrange("p e t -> p t e"),
                                         pA[:, 0:TE].rearrange("p (t e) -> p t e", e=NE)))
                    step(dve.tensor_reduce(chose[:], tot[:], AX.X, ALU.add))
                    step(dve.tensor_tensor_scan(cum[:].rearrange("p e t -> p (e t)"), one[:],
                                                tot[:].rearrange("p e t -> p (e t)"), 0.0, ALU.mult, ALU.add))
                    step(dve.tensor_tensor(cum[:], cum[:], tot[:], ALU.subtract))
                    step(dve.tensor_tensor(tot[:], cum[:], cum[:, :, 0:1].to_broadcast([P, NE, TH]), ALU.subtract))
                    step(dve.tensor_tensor(within[:], tot[:].rearrange("p e t -> p t e"),
                                           pB[:, 0:TE].rearrange("p (t e) -> p t e", e=NE), ALU.add))
                    step(dve.tensor_tensor(within[:], within[:], erow(count), ALU.add))
                    step(dve.tensor_tensor(count[:], count[:], chose[:], ALU.add))
                    step(dve.tensor_scalar(sel[:], within[:], float(CAP), None, ALU.is_lt))
                    step(dve.tensor_tensor(within[:], within[:], erow(ebase), ALU.add))
                    for c, hot in ((0, hot1), (1, hot2)):
                        step(dve.tensor_tensor(tmp[:], hot[:], sel[:], ALU.mult))
                        step(dve.tensor_reduce(keep[:], tmp[:], AX.X, ALU.add))
                        step(dve.tensor_tensor(tmp[:], tmp[:], within[:], ALU.mult))
                        step(dve.tensor_reduce(slot[:], tmp[:], AX.X, ALU.add))
                        step(dve.tensor_tensor(gate[:, c, tiles], gate[:, c, tiles], keep[:], ALU.mult))
                        step(dve.tensor_scalar(keep[:], keep[:], -1.0, 1.0, ALU.mult, ALU.add))
                        step(dve.tensor_tensor(keep[:], keep[:], trash[:, c, tiles], ALU.mult))
                        step(dve.tensor_tensor(slot[:], slot[:], keep[:], ALU.add))
                        step(dve.tensor_copy(slot_in[:, c, tiles], slot[:]))


def expert_products(core, name, ex, count):
    nc, NE, CAP, FFN = core.nc, ex.NE, ex.CAP, ex.FFN
    CT, FC = CAP // P, FFN // P
    CH = ((0, 4), (4, 4), (8, 2))
    with ExitStack() as ctx:
        sb = lambda n, s, dt=F32: core.sb(f"{name}_{n}", s, dt, ctx)
        W1, W2 = sb("W1", [P, 2, FFN]), sb("W2", [P, 2, FC, D])
        rows, xT = sb("rows", [P, 2, CT, D + 1]), sb("xT", [P, CAP])
        number, empty, filled, target = (sb(n, [P, CT]) for n in ("number", "empty", "filled", "target"))
        number_i, place = sb("number_i", [P, CT], I32), sb("place", [P, 2, CT], U32)
        hT, y = sb("hT", [P, FC, CAP]), sb("y", [P, 2, CT, D])
        pT = core.ps(f"{name}_epT", [P, 2, 512], F32, ctx)
        pH = core.ps(f"{name}_epH", [P, 4, 512], F32, ctx)
        pO = core.ps(f"{name}_epO", [P, 2, 512], F32, ctx)
        s = {n: core.sem(f"{name}_e_{n}") for n in
             "rows_loaded0 rows_loaded1 weights_loaded0 weights_loaded1 turned x_copied "
             "h_made raised o_made o_copied stored0 stored1 y_free "
             "numbers chain sending".split()}
        with nc.Block() as block:
            @block.sync
            def _(sp):
                with sp.Fori(0, NE // 2) as i:
                    for u in range(2):
                        e = 2 * i + u
                        sp.wait_ge(s["o_made"], e * 3 + 3)
                        sp.dma_start(rows[:, u], ex.rows_in[bass.ds(e * CAP, CAP), :].rearrange("(t p) d -> p t d", p=P))\
                          .then_inc(s[f"rows_loaded{u}"], 16)
                        sp.dma_start(W1[:, u], ex.moe_w1[bass.ds(e, 1)].rearrange("e p f -> (e p) f"))\
                          .then_inc(s[f"weights_loaded{u}"], 16)
                        sp.dma_start(W2[:, u], ex.moe_w2[bass.ds(e, 1)].rearrange("e (c p) n -> (e p) c n", p=P))\
                          .then_inc(s[f"weights_loaded{u}"], 16)

            @block.gpsimd
            def _(pool):
                pool.iota(number_i[:], [[P, CT]], base=0, channel_multiplier=1).then_inc(s["numbers"], 1)
                pool.sem_inc(s["y_free"], 2)
                with pool.Fori(0, NE // 2) as i:
                    for u in range(2):
                        e = 2 * i + u
                        for c, (t0, n) in enumerate(CH):
                            pool.wait_ge(s["o_copied"], e * 3 + c + 1 + 2)
                            pool.sem_inc(s["sending"], 1)
                            for t in range(t0, t0 + n):
                                pool.indirect_dma_start(
                                    out=ex.rows_out, out_offset=bass.IndirectOffsetOnAxis(ap=place[:, u, t:t + 1], axis=0),
                                    in_=y[:, u, t, :], in_offset=None).then_inc(s[f"stored{u}"], 16)
                        pool.wait_ge(s[f"stored{u}"], i * 16 * CT + 16 * CT)
                        pool.sem_inc(s["y_free"], 1)

            @block.tensor
            def _(pe):
                pe.sem_inc(s["o_made"], 6)
                pe.sem_inc(s["h_made"], 12)
                with pe.Fori(0, NE // 2) as i:
                    for u in range(2):
                        e = 2 * i + u
                        pe.wait_ge(s[f"rows_loaded{u}"], i * 16 + 16)
                        for c, (t0, n) in enumerate(CH):
                            slot = (c + u) % 2
                            pe.wait_ge(s["x_copied"], e * 3 + c + 1)
                            for j in range(n):
                                ins = pe.transpose(pT[:, slot, bass.ts(j, P)], rows[:, u, t0 + j, 0:D], core.ident[:])
                            ins.then_inc(s["turned"], 1)
                        pe.wait_ge(s[f"weights_loaded{u}"], i * 32 + 32)
                        for c, (t0, n) in enumerate(CH):
                            pe.wait_ge(s["x_copied"], e * 3 + c + 3)
                            for f in range(FC):
                                pe.wait_ge(s["raised"], e * 12 + 4 * c + f + 1)
                                pe.matmul(pH[:, f, 0:n * P], W1[:, u, bass.ts(f, P)], xT[:, t0 * P:(t0 + n) * P],
                                          start=True, stop=True).then_inc(s["h_made"], 1)
                        for c, (t0, n) in enumerate(CH):
                            slot = (c + u) % 2
                            pe.wait_ge(s["raised"], e * 12 + 4 * c + 4 + 4)
                            pe.wait_ge(s["o_copied"], e * 3 + c + 1)
                            for j in range(n):
                                for f in range(FC):
                                    ins = pe.matmul(pO[:, slot, bass.ts(j, D)], hT[:, f, bass.ts(t0 + j, P)], W2[:, u, f, :],
                                                    start=(f == 0), stop=(f == FC - 1))
                            ins.then_inc(s["o_made"], 1)

            @block.scalar
            def _(act):
                act.sem_inc(s["raised"], 4)
                with act.Fori(0, NE // 2) as i:
                    for u in range(2):
                        e = 2 * i + u
                        for c, (t0, n) in enumerate(CH):
                            act.wait_ge(s["o_made"], e * 3 + c + 1 + 3)
                            for f in range(FC):
                                act.wait_ge(s["h_made"], e * 12 + 4 * c + f + 1 + 12)
                                act.activation(hT[:, f, t0 * P:(t0 + n) * P], pH[:, f, 0:n * P], ACT.Gelu)\
                                   .then_inc(s["raised"], 1)

            @block.vector
            def _(dve):
                dve.sem_inc(s["x_copied"], 2)
                dve.sem_inc(s["o_copied"], 2)
                dve.wait_ge(s["numbers"], 1)
                step = Chain(dve, s["chain"])
                step(dve.tensor_copy(number[:], number_i[:]))
                step(dve.tensor_scalar(empty[:], number[:], float(ex.TOP * TOKENS), None, ALU.add))
                with dve.Fori(0, NE // 2) as i:
                    for u in range(2):
                        e = 2 * i + u
                        for c, (t0, n) in enumerate(CH):
                            dve.wait_ge(s["turned"], e * 3 + c + 1)
                            dve.wait_ge(s["h_made"], e * 12 + 4 * c + 4)
                            dve.tensor_copy(xT[:, t0 * P:(t0 + n) * P], pT[:, (c + u) % 2, 0:n * P])\
                               .then_inc(s["x_copied"], 1)
                        dve.wait_ge(s["y_free"], e + 1)
                        step = Chain(dve, s["chain"], e * 5 + 2)
                        step(dve.tensor_scalar(filled[:], number[:], count[:, bass.ds(e, 1)], None, ALU.is_lt))
                        step(dve.tensor_tensor(target[:], rows[:, u, :, D:D + 1].rearrange("p t o -> p (t o)"), empty[:],
                                               ALU.subtract))
                        step(dve.tensor_tensor(target[:], target[:], filled[:], ALU.mult))
                        step(dve.tensor_tensor(target[:], target[:], empty[:], ALU.add))
                        step(dve.tensor_copy(place[:, u, :], target[:]))
                        for c, (t0, n) in enumerate(CH):
                            dve.wait_ge(s["o_made"], e * 3 + c + 1 + 6)
                            dve.tensor_copy(y[:, u, t0:t0 + n, :].rearrange("p t d -> p (t d)"),
                                            pO[:, (c + u) % 2, 0:n * P]).then_inc(s["o_copied"], 1)


def full_attention(core, name, wqkv_t, bqkv, wo_t, bo, wq, wk):
    nc = core.nc
    NH, DH, SL, NP_ = 16, 8, 64, 8
    NQ = BTILES
    C3 = 3 * D
    AHEAD = 4
    QSLOT = {"h": ((0, 2, 8), (3, 1, 8)), "m": ((2, 1, 8), (5, 1, 8)), "l": 4}
    KSLOT = {"h": ((0, 3, 16),), "m": ((1, 1, 8), (5, 1, 8)), "l": 3}
    with ExitStack() as ctx:
        sb = lambda n, s, dt=F32: core.sb(f"{name}_{n}", s, dt, ctx)
        ps = lambda n, s: core.ps(f"{name}_{n}", s, F32, ctx)
        W, Wo = sb("W", [D, C3]), sb("Wo", [D, D])
        bias, brow = sb("bias", [P, C3]), sb("brow", [P, D])
        wqr, wkr, wqk = sb("wqr", [P, DH]), sb("wkr", [P, DH]), sb("wqk", [P, NH, DH])
        nrm, uT = sb("nrm", [P, BTILES, D]), sb("uT", [P, SEQ])
        qkv = sb("qkv", [P, BTILES, C3])
        sq = sb("sq", [P, BTILES, 2 * D])
        ss, rs, rt = (sb(n, [P, BTILES * 2 * NH]) for n in ("ss", "rs", "rt"))
        Q6, K6 = sb("Q6", [P, BTILES, NH, SL], BF16), sb("K6", [P, BTILES, NH, SL], BF16)
        QT, KZ = sb("QT", [P, NP_, SEQ], BF16), sb("KZ", [P, 2, NP_, SEQ], BF16)
        QM = sb("QM", [P, 2, SEQ], BF16)
        PT = sb("PT", [P, 4, SEQ])
        V1 = sb("V1", [P, BTILES, NH, DH + 1])
        mxh, mx, mr = sb("mxh", [P, 2, NQ, 2, 2]), sb("mx", [P, NQ, 2]), sb("mr", [P, NQ, 2])
        OT, osum = sb("OT", [P, 512]), sb("osum", [P, 16])
        Z, ZT = sb("Z", [P, BTILES, NH, DH]), sb("ZT", [P, BTILES, P])
        p2, p1 = ps("p2", [P, 4, 512]), ps("p1", [P, 2, 512])
        pT, pO = ps("pT", [P, 512]), ps("pO", [P, 512])
        names = ("loaded wqk_made ones_made slots_made normed normed_qk h_cast r_made m_cast l_made kq_turned "
                 "k_used q_used s1_made s1_used m_made t_made t_used v_made s2_made exped pv_done o_used bias_added "
                 "chain").split()
        CASTS = []
        for part in "hm":
            for w, slots in enumerate((QSLOT, KSLOT)):
                group = [[part, w, s0, c, st] for s0, count, st in slots[part] for c in range(count)]
                CASTS += [tuple(x) + (x is group[0], x is group[-1]) for x in group]
        s = {n: core.sem(f"{name}_{n}") for n in names}
        rows_in = [("U", 0), ("U", 1)] + [("V", k) for k in range(BTILES)]
        first_uses = rows_in + [("QM", 0)]
        ends = [("Z", 0), ("Z", 1), ("Y", 0), ("Y", 1)]

        def row_uses(last):
            out = []
            for pr in range(NP_):
                out += [("O", pr - 1)] if pr > 0 else []
                out += rows_in if pr == NP_ - 2 and not last else []
                out += [("QM", pr + 1)] if pr < NP_ - 1 else []
            return out + [("O", NP_ - 1)] + ends + ([] if last else [("QM", 0)])

        uses = {last: row_uses(last) for last in (False, True)}
        FIRST, NT = len(first_uses), len(uses[False])

        def use_of(key, b, last):
            return first_uses.index(key) if b is None else FIRST + b * NT + uses[last].index(key)

        LEAD = 2 * NQ + AHEAD
        ENDS_AT = {1: ("Z", 0), 2: ("Z", 1), 4: ("Y", 0), 7: ("Y", 1)}
        ROWS_AT = {4 + k: key for k, key in enumerate(rows_in)}
        CASTS_AT = 4

        q6v = Q6[:].rearrange("p t h c -> p (t h) c")
        k6v = K6[:].rearrange("p t h c -> p (t h) c")
        pTb = pT[:].bitcast(BF16)

        def loads(sp):
            row = lambda a, n: a.rearrange("(o c) -> o c", o=1).to_broadcast([P, n])
            for t, a in ((W[:], wqkv_t), (Wo[:], wo_t), (bias[:], row(bqkv, C3)), (brow[:], row(bo, D)),
                         (wqr[:], row(wq, DH)), (wkr[:], row(wk, DH))):
                sp.dma_start(t, a).then_inc(s["loaded"], 16)

        stream_stats(core, f"{name}_in", loads=loads)
        with nc.Block() as block:
            @block.gpsimd
            def _(pool):
                pool.memset(KZ[:], 0.0).then_inc(s["ones_made"], 1)
                pool.memset(V1[:], 1.0).then_inc(s["ones_made"], 1)

            @block.scalar
            def _(act):
                act.sem_inc(s["exped"], 2)
                act.sem_inc(s["o_used"], 1)
                act.wait_ge(s["slots_made"], 3)
                act.wait_ge(s["ones_made"], 2)

                def take_rows(c, b, last):
                    act.wait_ge(s["t_made"], use_of(("U", c), b, last) + 1)
                    act.activation(uT[:, bass.ts(c, 512)], pT[:], ACT.Copy).then_inc(s["t_used"], 1)

                def cast(k, row):
                    part, w, s0, c, st, first, last = CASTS[k]
                    v = (q6v, k6v)[w]
                    if first:
                        act.wait_ge(s["normed_qk" if part == "h" else "r_made"], row * 2 + w + 1)
                    src = (qkv if part == "h" else sq)[:, :, w * D:(w + 1) * D].rearrange("p t (h d) -> p t h d", d=DH)
                    c0 = s0 * DH + c * st
                    ins = act.activation(v[:, :, c0:c0 + DH].rearrange("p (t h) d -> p t h d", t=BTILES), src, ACT.Copy)
                    if last:
                        ins.then_inc(s["h_cast" if part == "h" else "m_cast"], 1)

                def take_queries(pr, b, last):
                    act.wait_ge(s["t_made"], use_of(("QM", pr), b, last) + 1)
                    act.activation(QM[:, pr % 2, :], pTb, ACT.Copy).then_inc(s["t_used"], 1)

                def lead(row, b):
                    for pr in range(NP_):
                        act.wait_ge(s["kq_turned"], row * 16 + 2 * pr + 1)
                        bank = p2[:, (2 * pr) % 4, :].bitcast(BF16)
                        for par in range(2):
                            half = slice(64 * par, 64 * par + 64)
                            ins = act.activation(KZ[half, par, pr, :], bank[half, :], ACT.Copy)
                        ins.then_inc(s["k_used"], 1)
                        act.wait_ge(s["kq_turned"], row * 16 + 2 * pr + 2)
                        act.activation(QT[:, pr, :], p2[:, (2 * pr + 1) % 4, :].bitcast(BF16), ACT.Copy)\
                           .then_inc(s["q_used"], 1)
                    take_queries(0, b, False)

                for c in range(2):
                    take_rows(c, None, False)
                for k in range(len(CASTS)):
                    cast(k, 0)
                lead(0, None)

                def row(b, last):
                    for pr in range(NP_):
                        for j in range(2 * NQ):
                            k2 = b * 16 * NP_ + 16 * pr + j
                            act.wait_ge(s["s2_made"], k2 + 1)
                            act.wait_ge(s["pv_done"], k2 + 1)
                            act.activation(PT[:, j % 4, :], p2[:, 2 * (j % 2):2 * (j % 2) + 2, :].rearrange("p a c -> p (a c)"),
                                           ACT.Exp).then_inc(s["exped"], 1)
                            if pr == NP_ - 2 and not last and ROWS_AT.get(j, "-")[0] == "U":
                                take_rows(ROWS_AT[j][1], b, last)
                            if pr == NP_ - 1 and not last and 0 <= j - CASTS_AT < len(CASTS):
                                cast(j - CASTS_AT, b + 1)
                        if pr < NP_ - 1:
                            take_queries(pr + 1, b, last)
                        act.wait_ge(s["pv_done"], b * 16 * NP_ + 16 * (pr + 1) + 4)
                        if pr > 0:
                            act.wait_ge(s["t_made"], use_of(("O", pr - 1), b, last) + 1)
                        act.activation(OT[:], pO[:], ACT.Copy).then_inc(s["o_used"], 1)
                    if not last:
                        lead(b + 1, b)
                batch_rows(act, row)

            @block.vector
            def _(dve):
                dve.sem_inc(s["s1_used"], 2)
                dve.sem_inc(s["t_used"], 1)
                dve.memset(Q6[:], 0.0).then_inc(s["slots_made"], 1)
                dve.memset(K6[:], 0.0).then_inc(s["slots_made"], 1)
                dve.wait_ge(s["slots_made"], 2)
                dve.memset(k6v[:, :, 48:51], 1.0).then_inc(s["slots_made"], 1)
                dve.memset(pO[:], 0.0).then_inc(s["wqk_made"], 1)
                dve.wait_ge(s["loaded"], 16 * 6)
                dve.wait_ge(s["ones_made"], 2)
                dve.wait_ge(s["wqk_made"], 1)
                dve.tensor_tensor(wqr[:], wqr[:], wkr[:], ALU.mult).then_inc(s["wqk_made"], 1)
                dve.wait_ge(s["wqk_made"], 2)
                dve.tensor_copy(wqk[:], wqr[:].rearrange("p (o d) -> p o d", o=1).to_broadcast([P, NH, DH]))\
                   .then_inc(s["wqk_made"], 1)
                dve.wait_ge(s["wqk_made"], 3)

                def norm_rows(row):
                    for k in range(BTILES):
                        t = bass.ds(row * BTILES + k, 1)
                        ins = dve.tensor_scalar(nrm[:, k, :], core.X[:, t, :].rearrange("p t d -> p (t d)"),
                                                core.rstd[:, t], core.shift[:, t], ALU.mult, ALU.add)
                    ins.then_inc(s["normed"], 1)

                def take_product(k, b, last):
                    dve.wait_ge(s["t_made"], use_of(("V", k), b, last) + 1)
                    dve.tensor_tensor(qkv[:, k, :], pT[:, 0:C3], bias[:], ALU.add).then_inc(s["t_used"], 1)

                def unit_rows(row, b, last, step):
                    dve.wait_ge(s["t_used"], use_of(("V", BTILES - 1), b, last) + 2)
                    step(dve.tensor_tensor(sq[:], qkv[:, :, 0:2 * D], qkv[:, :, 0:2 * D], ALU.mult))
                    step(dve.tensor_reduce(ss[:].rearrange("p (t h) -> p t h", t=BTILES),
                                           sq[:].rearrange("p t (h d) -> p t h d", d=DH), AX.X, ALU.add))
                    step(dve.tensor_scalar(ss[:], ss[:], 1.0 / DH, 1e-6, ALU.mult, ALU.add))
                    newton_rsqrt(dve, step, rs[:], ss[:], rt[:])
                    for w in range(2):
                        src = qkv[:, :, w * D:(w + 1) * D].rearrange("p t (h d) -> p t h d", d=DH)
                        r = rs[:].rearrange("p (t w h o) -> p t w h o", t=BTILES, w=2, o=1)[:, :, w]\
                            .to_broadcast([P, BTILES, NH, DH])
                        ins = dve.tensor_tensor(src, src, r, ALU.mult)
                        if w == 0:
                            ins.then_inc(s["normed_qk"], 1)
                    step(ins)
                    flat = qkv[:, :, D:2 * D]
                    dve.tensor_tensor(flat, flat, wqk[:].rearrange("p (o h) d -> p o (h d)", o=1).to_broadcast([P, BTILES, D]),
                                      ALU.mult).then_inc(s["normed_qk"], 1)

                def split_rows(row):
                    dve.wait_ge(s["normed_qk"], row * 2 + 2)
                    for w, v in enumerate((q6v, k6v)):
                        dve.wait_ge(s["h_cast"], row * 2 + w + 1)
                        src = qkv[:, :, w * D:(w + 1) * D].rearrange("p t (h d) -> p t h d", d=DH)
                        r1 = sq[:, :, w * D:(w + 1) * D].rearrange("p t (h d) -> p t h d", d=DH)
                        dve.tensor_tensor(r1, src, v[:, :, 0:DH].rearrange("p (t h) d -> p t h d", t=BTILES),
                                          ALU.subtract).then_inc(s["r_made"], 1)
                    for w, (v, slots) in enumerate(((q6v, QSLOT), (k6v, KSLOT))):
                        dve.wait_ge(s["m_cast"], row * 2 + w + 1)
                        r1 = sq[:, :, w * D:(w + 1) * D].rearrange("p t (h d) -> p t h d", d=DH)
                        c, m = slots["l"] * DH, slots["m"][0][0] * DH
                        dve.tensor_tensor(v[:, :, c:c + DH].rearrange("p (t h) d -> p t h d", t=BTILES), r1,
                                          v[:, :, m:m + DH].rearrange("p (t h) d -> p t h d", t=BTILES),
                                          ALU.subtract).then_inc(s["l_made"], 1)

                def maxima(row, g, step):
                    pr, j = g // 16, g % 16
                    for half in range(2):
                        k1 = row * 32 * NP_ + 2 * g + half
                        dve.wait_ge(s["s1_made"], k1 + 1)
                        dve.tensor_reduce(mxh[:, pr % 2, j // 2, j % 2, half:half + 1], p1[:, half, :], AX.X, ALU.max)\
                           .then_inc(s["s1_used"], 1)
                    if j == 15:
                        dve.wait_ge(s["s1_used"], row * 32 * NP_ + 2 * g + 2 + 2)
                        mh = mxh[:, pr % 2]
                        slot = lambda c: Q6[:, :, 2 * pr:2 * pr + 2, 48 + c:49 + c].rearrange("p t h o -> p t (h o)")
                        step(dve.tensor_reduce(mx[:], mh, AX.X, ALU.max, negate=True))
                        step(dve.tensor_copy(slot(0), mx[:]))
                        step(dve.tensor_tensor(mr[:], mx[:], slot(0), ALU.subtract))
                        step(dve.tensor_copy(slot(1), mr[:]))
                        step(dve.tensor_tensor(slot(2), mr[:], slot(1), ALU.subtract))
                        dve.sem_inc(s["m_made"], 1)

                def outputs(pr, b, last, step):
                    dve.wait_ge(s["t_made"], use_of(("O", pr), b, last) + 1)
                    view = pT[:].rearrange("p (q c d) -> p q c d", q=4, c=4)
                    step(dve.reciprocal(osum[:].rearrange("p (q c o) -> p q c o", q=4, o=1), view[:, :, :, DH:DH + 1]))
                    r = osum[:].rearrange("p (q a h o) -> p h q a o", q=4, a=2, o=1)
                    v = pT[:].rearrange("p (q a h d) -> p h q a d", q=4, a=2, h=2)
                    for half in range(2):
                        ins = dve.tensor_tensor(Z[:, 4 * half:4 * half + 4, 2 * pr:2 * pr + 2, :], v[:, half, :, :, 0:DH],
                                                r[:, half].to_broadcast([P, 4, 2, DH]), ALU.mult)
                    ins.then_inc(s["t_used"], 1)

                def end(key, b, last):
                    kind, half = key
                    if key == ("Y", 0):
                        xs = core.X[:, bass.ds(b * BTILES, BTILES), :]
                        dve.tensor_tensor(xs, xs, brow[:].rearrange("p (o d) -> p o d", o=1).to_broadcast([P, BTILES, D]),
                                          ALU.add).then_inc(s["bias_added"], 1)
                        dve.wait_ge(s["bias_added"], b + 1)
                    dve.wait_ge(s["t_made"], use_of(key, b, last) + 1)
                    if kind == "Z":
                        dve.tensor_copy(ZT[:, 4 * half:4 * half + 4, :].rearrange("p t q -> p (t q)"), pT[:])\
                           .then_inc(s["t_used"], 1)
                    else:
                        x4 = core.X[:, bass.ds(b * BTILES + 4 * half, 4), :]
                        dve.tensor_tensor(x4, x4, pT[:].rearrange("p (t d) -> p t d", d=D), ALU.add).then_inc(s["t_used"], 1)
                    if key == ("Y", 1):
                        dve.wait_ge(s["t_used"], use_of(key, b, last) + 2)
                        row_moments(dve, core, core.X, b * BTILES, BTILES)

                def lead(row, b, step):
                    for g in range(LEAD):
                        maxima(row, g, step)
                        if b is not None and g in ENDS_AT:
                            end(ENDS_AT[g], b, False)
                        if g == LEAD - 3:
                            dve.tensor_copy(V1[:, :, :, 0:DH], qkv[:, :, 2 * D:C3].rearrange("p t (h d) -> p t h d", d=DH))\
                               .then_inc(s["v_made"], 1)

                step = Chain(dve, s["chain"])
                norm_rows(0)
                for k in range(BTILES):
                    take_product(k, None, False)
                unit_rows(0, None, False, step)
                split_rows(0)
                lead(0, None, step)
                BEFORE = step.n
                CH = (3 + 10 + 1) + 5 * NP_ + NP_

                def row(b, last):
                    step = Chain(dve, s["chain"], BEFORE + b * CH)
                    for pr in range(NP_):
                        for j in range(2 * NQ):
                            if pr == NP_ - 2 and j == 0 and not last:
                                norm_rows(b + 1)
                            g = 16 * (pr + 1) + j + AHEAD
                            if g < 16 * NP_:
                                maxima(b, g, step)
                            if j == 3 and pr > 0 and (pr < NP_ - 1 or last):
                                outputs(pr - 1, b, last, step)
                            if pr == NP_ - 2 and not last and ROWS_AT.get(j, "-")[0] == "V":
                                take_product(ROWS_AT[j][1], b, last)
                    if not last:
                        unit_rows(b + 1, b, last, step)
                        outputs(NP_ - 2, b, last, step)
                        split_rows(b + 1)
                    outputs(NP_ - 1, b, last, step)
                    if last:
                        for key in ends:
                            end(key, b, last)
                    else:
                        lead(b + 1, b, step)
                        assert step.n == CH, (step.n, CH)
                batch_rows(dve, row)

            @block.tensor
            def _(pe):
                pe.sem_inc(s["pv_done"], 4)
                pe.wait_ge(s["loaded"], 16 * 6)
                pe.wait_ge(s["ones_made"], 2)
                q6f, k6f = Q6[:].rearrange("p t h c -> p t (h c)"), K6[:].rearrange("p t h c -> p t (h c)")
                pe.wait_ge(s["wqk_made"], 1)

                def turn(key, b, last):
                    kind, n = key
                    pe.wait_ge(s["t_used"], use_of(key, b, last) + 1)
                    if kind == "U":
                        pe.wait_ge(s["normed"], 1 if b is None else b + 2)
                        for k in range(4):
                            ins = pe.transpose(pT[:, bass.ts(k, P)], nrm[:, 4 * n + k, :], core.ident[:])
                    elif kind == "V":
                        ins = pe.matmul(pT[:, 0:C3], uT[:, bass.ts(n, P)], W[:], start=True, stop=True)
                    elif kind == "QM":
                        row = (0 if b is None else b) + (1 if n == 0 and b is not None else 0)
                        pe.wait_ge(s["m_made"], row * NP_ + n + 1)
                        for k in range(BTILES):
                            ins = pe.transpose(pTb[:, bass.ts(k, P)], q6f[:, k, bass.ts(n, P)], core.identb[:])
                    elif kind == "O":
                        pe.wait_ge(s["o_used"], b * NP_ + n + 2)
                        for k in range(4):
                            ins = pe.transpose(pT[:, bass.ts(k, P)], OT[:, bass.ts(k, P)], core.ident[:])
                    elif kind == "Z":
                        for k in range(4):
                            ins = pe.transpose(pT[:, bass.ts(k, P)], Z[:, 4 * n + k].rearrange("p h d -> p (h d)"),
                                               core.ident[:])
                    else:
                        for k in range(4):
                            ins = pe.matmul(pT[:, bass.ts(k, P)], ZT[:, 4 * n + k, :], Wo[:], start=True, stop=True)
                    ins.then_inc(s["t_made"], 1)

                def turn_pair(row, pr):
                    for w, src in ((0, k6f), (1, q6f)):
                        if pr >= 2:
                            pe.wait_ge(s["q_used" if w else "k_used"], row * NP_ + pr - 1)
                        bank = p2[:, (2 * pr + w) % 4, :].bitcast(BF16)
                        for k in range(BTILES):
                            ins = pe.transpose(bank[:, bass.ts(k, P)], src[:, k, bass.ts(pr, P)], core.identb[:])
                        ins.then_inc(s["kq_turned"], 1)

                def max_scores(row, g, half):
                    pr, j = g // 16, g % 16
                    qt, par = j // 2, j % 2
                    k1 = row * 32 * NP_ + 2 * g + half
                    if j == 0 and half == 0:
                        pe.wait_ge(s["q_used"], row * NP_ + pr + 1)
                    pe.wait_ge(s["s1_used"], k1 + 1)
                    pe.matmul(p1[:, half, :], QT[:, pr, bass.ts(qt, P)], KZ[:, par, pr, bass.ts(half, 512)],
                              start=True, stop=True).then_inc(s["s1_made"], 1)

                def lead(row, b):
                    pe.wait_ge(s["l_made"], row * 2 + 2)
                    pe.wait_ge(s["exped"], row * 16 * NP_ + 2)
                    turn_pair(row, 0)
                    turn_pair(row, 1)
                    for g in range(LEAD):
                        max_scores(row, g, 0)
                        max_scores(row, g, 1)
                        if b is not None and g in ENDS_AT:
                            turn(ENDS_AT[g], b, False)
                        if g % 2 == 0 and g // 2 + 2 < NP_:
                            turn_pair(row, g // 2 + 2)
                        if g == 2 * NQ:
                            turn(("QM", 0), b, False)

                for key in rows_in:
                    turn(key, None, False)
                lead(0, None)

                def row(b, last):
                    def scores(pr, j):
                        kt, par = j // 2, j % 2
                        k2 = b * 16 * NP_ + 16 * pr + j
                        pe.wait_ge(s["exped"], k2 + 1)
                        for half in range(2):
                            ins = pe.matmul(p2[:, 2 * par + half, :], KZ[:, par, pr, bass.ts(kt, P)],
                                            QM[:, pr % 2, bass.ts(half, 512)], start=True, stop=True)
                        ins.then_inc(s["s2_made"], 1)

                    def values(pr, kt):
                        k2 = b * 16 * NP_ + 16 * pr + 2 * kt
                        if kt == 0:
                            pe.wait_ge(s["o_used"], b * NP_ + pr + 1)
                        pe.wait_ge(s["exped"], k2 + 4)
                        for par in range(2):
                            for half in range(2):
                                c = 2 * par + half
                                ins = pe.matmul(pO[32 * c:32 * c + DH + 1, :], V1[:, kt, 2 * pr + par, :],
                                                PT[:, (2 * kt + par) % 4, bass.ts(half, 512)], start=(kt == 0),
                                                stop=(kt == NQ - 1), skip_group_check=True)
                        ins.then_inc(s["pv_done"], 2)

                    pe.wait_ge(s["k_used"], b * NP_ + NP_)
                    pe.wait_ge(s["q_used"], b * NP_ + NP_)
                    pe.wait_ge(s["v_made"], b + 1)
                    pe.wait_ge(s["t_used"], FIRST + b * NT + 1)
                    for pr in range(NP_):
                        for j in range(2 * NQ):
                            scores(pr, j)
                            g = 16 * (pr + 1) + j + AHEAD
                            if g < 16 * NP_:
                                max_scores(b, g, 0)
                            if j % 2 == 1 and j > 1:
                                values(pr, (j - 3) // 2)
                            if g < 16 * NP_:
                                max_scores(b, g, 1)
                            if j == 2 and pr > 0:
                                turn(("O", pr - 1), b, last)
                            if pr == NP_ - 2 and not last and j in ROWS_AT:
                                turn(ROWS_AT[j], b, last)
                            if j == 14 and pr < NP_ - 1:
                                turn(("QM", pr + 1), b, last)
                        values(pr, NQ - 1)
                        if pr < NP_ - 1:
                            pe.wait_ge(s["t_used"], use_of(("QM", pr + 1), b, last) + 2)
                    turn(("O", NP_ - 1), b, last)
                    if last:
                        for key in ends:
                            turn(key, b, last)
                    else:
                        lead(b + 1, b)
                batch_rows(pe, row)


def _as_is(a):
    return a


def _turned(a):
    return a.T


LAYOUT = {
    "x": ("L0_attn_a_u", _as_is),
    "scan_bc": ("L0_attn_a_x_proj_w", lambda a: np.tile(a[64:].T, (1, 3))),
    "scan_dt": ("L0_attn_a_x_proj_w", lambda a: a[:64].T),
    "scan_delta": ("L0_attn_a_dt_proj_w", _turned),
    "scan_delta_bias": ("L0_attn_a_dt_proj_b", _as_is),
    "scan_a_log": ("L0_attn_a_A_log", _as_is),
    "scan_skip": ("L0_attn_a_D", _as_is),
    "ffn_kernel": ("L0_ffn_kernel", _as_is),
    "ffn_bias": ("L0_ffn_bias", _as_is),
    "ffn_a_t": ("L0_ffn_a", _turned),
    "ffn_b": ("L0_ffn_b", _as_is),
    "mqa_g1": ("L0_attn_b_g1", _as_is),
    "mqa_wq_t": ("L0_attn_b_Wq", _turned),
    "mqa_wkv_t": ("L0_attn_b_Wkv", _turned),
    "mqa_wout_t": ("L0_attn_b_Wout", _turned),
    "mqa_g2": ("L0_attn_b_g2", _as_is),
    "single_qw": ("L1_attn_a_Qw", _as_is),
    "single_kw": ("L1_attn_a_Kw", _as_is),
    "single_vw": ("L1_attn_a_Vw", _as_is),
    "full_wqkv_t": ("L1_attn_b_Wqkv", _turned),
    "full_bqkv": ("L1_attn_b_bqkv", _as_is),
    "full_wo_t": ("L1_attn_b_Wo", _turned),
    "full_bo": ("L1_attn_b_bo", _as_is),
    "full_wq": ("L1_attn_b_wq", _as_is),
    "full_wk": ("L1_attn_b_wk", _as_is),
    "moe_ln1_weight": ("L1_ffn_ln1_weight", _as_is),
    "moe_ln1_bias": ("L1_ffn_ln1_bias", _as_is),
    "moe_ln2_weight": ("L1_ffn_ln2_weight", _as_is),
    "moe_ln2_bias": ("L1_ffn_ln2_bias", _as_is),
    "moe_router_weight": ("L1_ffn_router_weight", _as_is),
    "moe_w1": ("L1_ffn_moe_w1", _as_is),
    "moe_w2": ("L1_ffn_moe_w2", _as_is),
    "moe_qkv_t": ("L1_ffn_qkv_weight", _turned),
    "moe_proj_t": ("L1_ffn_proj_weight", _turned),
}


def program(nc, w, out):
    x, out = w["x"].rearrange("b s d -> (b s) d"), out.rearrange("b s d -> (b s) d")
    with ExitStack() as ctx:
        core = Core(nc, ctx)
        ex = Experts(core, w)
        scan_block(core, "scan", x, w["scan_bc"], w["scan_dt"], w["scan_delta"], w["scan_delta_bias"],
                   w["scan_a_log"], w["scan_skip"])
        core.end_stage()
        ffn(core, "ffn1", w["ffn_kernel"], w["ffn_bias"], w["ffn_a_t"], w["ffn_b"])
        core.end_stage()
        causal_mqa(core, "mqa", w["mqa_g1"], w["mqa_wq_t"], w["mqa_wkv_t"], w["mqa_wout_t"], w["mqa_g2"])
        core.end_stage()
        ffn(core, "ffn3", w["ffn_kernel"], w["ffn_bias"], w["ffn_a_t"], w["ffn_b"])
        core.end_stage()
        causal_single(core, "single", w["single_qw"], w["single_kw"], w["single_vw"])
        core.end_stage()
        experts(core, "moe5", ex)
        core.end_stage()
        full_attention(core, "full", w["full_wqkv_t"], w["full_bqkv"], w["full_wo_t"], w["full_bo"], w["full_wq"],
                       w["full_wk"])
        core.end_stage()
        experts(core, "moe7", ex, out)


def kernel(**inputs):
    import concourse.bacc as bacc
    from concourse.bass_utils import run_bass_kernel_spmd

    nc = bacc.Bacc("TRN2", target_bir_lowering=False, num_devices=1)
    arrays, given = {}, {}
    for name, (source, lay_out) in LAYOUT.items():
        a = np.ascontiguousarray(lay_out(np.asarray(inputs[source])))
        arrays["in_" + name] = a
        given[name] = nc.dram_tensor("in_" + name, a.shape, mybir.dt.from_np(a.dtype), kind="ExternalInput").ap()
    out = nc.dram_tensor("out", (BATCH, SEQ, D), F32, kind="ExternalOutput").ap()
    program(nc, given, out)
    return run_bass_kernel_spmd(nc, [arrays], core_ids=[0]).results[0]["out"]
```
